# Optimizing a Trainium2 kernel written in Bass

```python
import numpy as np
import jax
import jax.numpy as jnp

def _softmax(x, axis=-1):
    return jax.nn.softmax(x, axis=axis)

def _gelu(x):
    return jax.nn.gelu(x, approximate=True)

def _silu(x):
    return jax.nn.silu(x)

def _sigmoid(x):
    return jax.nn.sigmoid(x)

def _layernorm(x, axis=-1, eps=1e-05):
    m = jnp.mean(x, axis=axis, keepdims=True)
    v = jnp.var(x, axis=axis, keepdims=True)
    return (x - m) / jnp.sqrt(v + eps)

def _scatter_add(tgt, idx, src, axis=0):
    return tgt.at[idx].add(src)

def _segment_sum(src, seg, n):
    return jax.ops.segment_sum(src, seg, n)
kernel_name = 'mk_gnn_resnorm_d4_gnn_r64_1753a0'

def setup_inputs(seed: int=0):
    np.random.seed(seed)
    _w = jnp.asarray

    def _rec_inputs():
        import jax
        import jax.numpy as jnp
        _gk = jax.random.key(seed)
        x = -0.0004402 + 1 * jax.random.normal(jax.random.fold_in(_gk, 1), (100000, 16), jnp.float32)
        src = jax.random.randint(jax.random.fold_in(_gk, 2), (50000,), 0, 100000, jnp.int32)
        dst = jax.random.randint(jax.random.fold_in(_gk, 3), (50000,), 0, 100000, jnp.int32)
        _o = jnp.argsort(dst, stable=True)
        src = src[_o]
        dst = dst[_o]
        edge_attr_16 = -3.57403e-05 + 0.999761 * jax.random.normal(jax.random.fold_in(_gk, 12), (50000, 16), jnp.float32)
        edge_attr_8 = -5.3897e-05 + 0.999841 * jax.random.normal(jax.random.fold_in(_gk, 13), (50000, 8), jnp.float32)
        node_vec1 = -0.00472126 + 0.997171 * jax.random.normal(jax.random.fold_in(_gk, 15), (100000, 1), jnp.float32)
        return (x, src, dst, edge_attr_16, edge_attr_8, node_vec1)
    x, src, dst, edge_attr_16, edge_attr_8, node_vec1 = _rec_inputs()

    def _L0_gnn_setup():
        import jax, jax.numpy as jnp
        import numpy as np
        N_NODES = 30000
        N_EDGES = 300000
        IN_FEATS = 16
        OUT_FEATS = 16
        EDGE_DIM = 16
        key = jax.random.key(seed)
        ks = jax.random.split(key, 8)
        feat = jax.random.normal(ks[0], (N_NODES, IN_FEATS), dtype=jnp.float32)
        efeat = jax.random.normal(ks[1], (N_EDGES, EDGE_DIM), dtype=jnp.float32)
        W_msg = jax.random.normal(ks[2], (EDGE_DIM, IN_FEATS * OUT_FEATS), dtype=jnp.float32) * 0.1
        b_msg = jnp.zeros((IN_FEATS * OUT_FEATS,), dtype=jnp.float32)
        W_attn = jax.random.normal(ks[3], (EDGE_DIM, IN_FEATS * OUT_FEATS), dtype=jnp.float32) * 0.1
        b_attn = jnp.zeros((IN_FEATS * OUT_FEATS,), dtype=jnp.float32)
        src = jax.random.randint(ks[4], (N_EDGES,), 0, N_NODES, dtype=jnp.int32)
        dst = jax.random.randint(ks[5], (N_EDGES,), 0, N_NODES, dtype=jnp.int32)
        return {'feat': feat, 'efeat': efeat, 'W_msg': W_msg, 'b_msg': b_msg, 'W_attn': W_attn, 'b_attn': b_attn, 'src': src, 'dst': dst}
    _L0_gnn_all = _L0_gnn_setup()
    _L0_gnn_in = {k: v for k, v in _L0_gnn_all.items() if k in ('W_msg', 'b_msg', 'W_attn', 'b_attn')}
    del _L0_gnn_all

    def _L1_gnn_setup():
        import jax, jax.numpy as jnp
        import numpy as np
        N_NODES = 100000
        N_EDGES = 50000
        D_FEAT = 16
        key = jax.random.key(seed)
        k1, k2, k3 = jax.random.split(key, 3)
        x = jax.random.normal(k1, (N_NODES, D_FEAT), dtype=jnp.float32)
        edge_index = jax.random.randint(k2, (2, N_EDGES), 0, N_NODES, dtype=jnp.int64)
        edge_attr = jax.random.normal(k3, (N_EDGES, D_FEAT), dtype=jnp.float32)
        return {'x': x, 'edge_index': edge_index, 'edge_attr': edge_attr}
    _L1_gnn_all = _L1_gnn_setup()
    _L1_gnn_in = {k: v for k, v in _L1_gnn_all.items() if k in ()}
    del _L1_gnn_all

    def _L2_gnn_setup():
        import jax, jax.numpy as jnp
        import numpy as np
        N_NODES = 100000
        N_EDGES = 50000
        D_NODE = 16
        D_EDGE = 8
        D_HIDDEN = 16
        key = jax.random.key(seed)
        ks = jax.random.split(key, 8)
        node_features = jax.random.normal(ks[0], (N_NODES, D_NODE), dtype=jnp.float32)
        edge_attr_e3nn = jax.random.normal(ks[1], (N_EDGES, D_EDGE), dtype=jnp.float32)
        node_attr_scalar_raw = jax.random.normal(ks[2], (N_NODES, 1), dtype=jnp.float32)
        W_msg_tp = jax.random.normal(ks[3], (D_NODE, D_EDGE, D_HIDDEN), dtype=jnp.float32)
        W_msg_lin = jax.random.normal(ks[4], (D_HIDDEN, D_HIDDEN), dtype=jnp.float32)
        W_upd_tp = jax.random.normal(ks[5], (D_NODE, D_HIDDEN, D_HIDDEN), dtype=jnp.float32)
        W_upd_lin = jax.random.normal(ks[6], (D_HIDDEN, D_NODE), dtype=jnp.float32)
        edge_index = jax.random.randint(ks[7], (2, N_EDGES), 0, N_NODES, dtype=jnp.int64)
        return {'node_features': node_features, 'edge_attr_e3nn': edge_attr_e3nn, 'node_attr_scalar_raw': node_attr_scalar_raw, 'W_msg_tp': W_msg_tp, 'W_msg_lin': W_msg_lin, 'W_upd_tp': W_upd_tp, 'W_upd_lin': W_upd_lin, 'edge_index': edge_index}
    _L2_gnn_all = _L2_gnn_setup()
    _L2_gnn_in = {k: v for k, v in _L2_gnn_all.items() if k in ('W_msg_tp', 'W_msg_lin', 'W_upd_tp', 'W_upd_lin')}
    del _L2_gnn_all

    def _L3_gnn_setup():
        import jax, jax.numpy as jnp
        import numpy as np
        N_NODES = 3125
        N_EDGES = 50000
        F_IN = 16
        N_CLASSES = 16

        def _gin_conv(x, src, dst, eps, wa, ba, wb, bb, n_nodes):
            agg = jax.ops.segment_sum(x[src], dst, num_segments=n_nodes)
            h = (1.0 + eps) * x + agg
            h = jax.nn.relu(h @ wa + ba) @ wb + bb
            return h
        key = jax.random.key(seed)
        ks = jax.random.split(key, 8)
        s = 1.0 / np.sqrt(F_IN)
        return {'x': jax.random.normal(ks[0], (N_NODES, F_IN), dtype=jnp.float32), 'edge_index': jax.random.randint(ks[1], (2, N_EDGES), 0, N_NODES, dtype=jnp.int32), 'eps1': jnp.zeros((), dtype=jnp.float32), 'w1a': jax.random.normal(ks[2], (F_IN, 16), dtype=jnp.float32) * s, 'b1a': jnp.zeros((16,), dtype=jnp.float32), 'w1b': jax.random.normal(ks[3], (16, 16), dtype=jnp.float32) * 0.25, 'b1b': jnp.zeros((16,), dtype=jnp.float32), 'eps2': jnp.zeros((), dtype=jnp.float32), 'w2a': jax.random.normal(ks[4], (16, N_CLASSES), dtype=jnp.float32) * 0.25, 'b2a': jnp.zeros((N_CLASSES,), dtype=jnp.float32), 'w2b': jax.random.normal(ks[5], (N_CLASSES, N_CLASSES), dtype=jnp.float32) * 0.25, 'b2b': jnp.zeros((N_CLASSES,), dtype=jnp.float32)}
    _L3_gnn_all = _L3_gnn_setup()
    _L3_gnn_in = {k: v for k, v in _L3_gnn_all.items() if k in ('eps1', 'w1a', 'b1a', 'w1b', 'b1b', 'eps2', 'w2a', 'b2a', 'w2b', 'b2b')}
    del _L3_gnn_all
    return {'x': x, 'src': src, 'dst': dst, 'edge_attr_16': edge_attr_16, 'edge_attr_8': edge_attr_8, 'node_vec1': node_vec1, 'L0_gnn_W_msg': _L0_gnn_in['W_msg'], 'L0_gnn_b_msg': _L0_gnn_in['b_msg'], 'L0_gnn_W_attn': _L0_gnn_in['W_attn'], 'L0_gnn_b_attn': _L0_gnn_in['b_attn'], 'L2_gnn_W_msg_tp': _L2_gnn_in['W_msg_tp'], 'L2_gnn_W_msg_lin': _L2_gnn_in['W_msg_lin'], 'L2_gnn_W_upd_tp': _L2_gnn_in['W_upd_tp'], 'L2_gnn_W_upd_lin': _L2_gnn_in['W_upd_lin'], 'L3_gnn_eps1': _L3_gnn_in['eps1'], 'L3_gnn_w1a': _L3_gnn_in['w1a'], 'L3_gnn_b1a': _L3_gnn_in['b1a'], 'L3_gnn_w1b': _L3_gnn_in['w1b'], 'L3_gnn_b1b': _L3_gnn_in['b1b'], 'L3_gnn_eps2': _L3_gnn_in['eps2'], 'L3_gnn_w2a': _L3_gnn_in['w2a'], 'L3_gnn_b2a': _L3_gnn_in['b2a'], 'L3_gnn_w2b': _L3_gnn_in['w2b'], 'L3_gnn_b2b': _L3_gnn_in['b2b']}

def reference(x, src, dst, edge_attr_16, edge_attr_8, node_vec1, L0_gnn_W_msg, L0_gnn_b_msg, L0_gnn_W_attn, L0_gnn_b_attn, L2_gnn_W_msg_tp, L2_gnn_W_msg_lin, L2_gnn_W_upd_tp, L2_gnn_W_upd_lin, L3_gnn_eps1, L3_gnn_w1a, L3_gnn_b1a, L3_gnn_w1b, L3_gnn_b1b, L3_gnn_eps2, L3_gnn_w2a, L3_gnn_b2a, L3_gnn_w2b, L3_gnn_b2b):
    import jax
    import jax.numpy as jnp

    def _L0_gnn_ref(feat, efeat, W_msg, b_msg, W_attn, b_attn, src, dst):
        import jax, jax.numpy as jnp
        import numpy as np
        N_NODES = 30000
        N_EDGES = 300000
        IN_FEATS = 16
        OUT_FEATS = 16
        EDGE_DIM = 16
        N, in_f = feat.shape
        E = efeat.shape[0]
        w_m = (efeat @ W_msg + b_msg).reshape(E, in_f, -1)
        w_a = (efeat @ W_attn + b_attn).reshape(E, in_f, -1)
        h_src = feat[src][:, :, None]
        e1 = w_m * h_src
        e2 = w_a * h_src
        seg_max = jax.ops.segment_max(e2, dst, num_segments=N)
        ex = jnp.exp(e2 - seg_max[dst])
        denom = jax.ops.segment_sum(ex, dst, num_segments=N)
        attn = ex / denom[dst]
        ft = jax.ops.segment_sum(e1 * attn, dst, num_segments=N)
        return ft.sum(axis=1)

    def _L1_gnn_ref(x, edge_index, edge_attr):
        import jax, jax.numpy as jnp
        import numpy as np
        N_NODES = 100000
        N_EDGES = 50000
        D_FEAT = 16
        nb_node = x.shape[0]
        dst = edge_index[1]
        sums = jax.ops.segment_sum(edge_attr, dst, num_segments=nb_node)
        counts = jax.ops.segment_sum(jnp.ones((edge_attr.shape[0],), dtype=edge_attr.dtype), dst, num_segments=nb_node)
        denom = jnp.maximum(counts, 1.0)[:, None]
        return sums / denom

    def _L2_gnn_ref(node_features, edge_attr_e3nn, node_attr_scalar_raw, W_msg_tp, W_msg_lin, W_upd_tp, W_upd_lin, edge_index):
        import jax, jax.numpy as jnp
        import numpy as np
        N_NODES = 100000
        N_EDGES = 50000
        D_NODE = 16
        D_EDGE = 8
        D_HIDDEN = 16
        n_nodes = node_features.shape[0]
        row = edge_index[0]
        col = edge_index[1]
        norm_msg_tp = 1.0 / np.float32(np.sqrt(D_NODE * D_EDGE))
        norm_upd_tp = 1.0 / np.float32(np.sqrt(D_NODE * D_HIDDEN))
        norm_lin = 1.0 / np.float32(np.sqrt(D_HIDDEN))
        x_j = node_features[col]
        m = jnp.einsum('ei,ej,ijh->eh', x_j, edge_attr_e3nn, W_msg_tp) * norm_msg_tp
        m = jax.nn.silu(m)
        m = m @ W_msg_lin * norm_lin
        agg = jax.ops.segment_sum(m, row, num_segments=n_nodes)
        u = jnp.einsum('ni,nh,ihk->nk', node_features, agg, W_upd_tp) * norm_upd_tp
        u = jax.nn.silu(u)
        u = u @ W_upd_lin * norm_lin
        return node_features + u

    def _L3_gnn_ref(x, edge_index, eps1, w1a, b1a, w1b, b1b, eps2, w2a, b2a, w2b, b2b):
        import jax, jax.numpy as jnp
        import numpy as np
        N_NODES = 3125
        N_EDGES = 50000
        F_IN = 16
        N_CLASSES = 16

        def _gin_conv(x, src, dst, eps, wa, ba, wb, bb, n_nodes):
            agg = jax.ops.segment_sum(x[src], dst, num_segments=n_nodes)
            h = (1.0 + eps) * x + agg
            h = jax.nn.relu(h @ wa + ba) @ wb + bb
            return h
        src, dst = (edge_index[0], edge_index[1])
        n = x.shape[0]
        h = jax.nn.relu(_gin_conv(x, src, dst, eps1, w1a, b1a, w1b, b1b, n))
        h = _gin_conv(h, src, dst, eps2, w2a, b2a, w2b, b2b, n)
        return jax.nn.log_softmax(h, axis=1)
    edge_index = jnp.stack([src, dst])
    x = _layernorm(x + _L0_gnn_ref(x, edge_attr_16, L0_gnn_W_msg, L0_gnn_b_msg, L0_gnn_W_attn, L0_gnn_b_attn, src, dst), axis=-1)
    x = _layernorm(x + _L1_gnn_ref(x, edge_index, edge_attr_16), axis=-1)
    x = _layernorm(x + _L2_gnn_ref(x, edge_attr_8, node_vec1, L2_gnn_W_msg_tp, L2_gnn_W_msg_lin, L2_gnn_W_upd_tp, L2_gnn_W_upd_lin, edge_index), axis=-1)
    x = _layernorm(x + _L3_gnn_ref(x, edge_index, L3_gnn_eps1, L3_gnn_w1a, L3_gnn_b1a, L3_gnn_w1b, L3_gnn_b1b, L3_gnn_eps2, L3_gnn_w2a, L3_gnn_b2a, L3_gnn_w2b, L3_gnn_b2b), axis=-1)
    return x

_drawn_inputs = setup_inputs


def setup_inputs(seed=0):
    import zlib

    import numpy as np

    out = dict(_drawn_inputs(seed))
    spreads = {'L0_gnn_b_msg': (0.0, 0.1),
     'L0_gnn_b_attn': (0.0, 0.614),
     'L3_gnn_b1a': (0.0, 0.1),
     'L3_gnn_b1b': (0.0, 0.1),
     'L3_gnn_b2a': (0.0, 0.1),
     'L3_gnn_b2b': (0.0, 0.1)}
    factors = {}
    for name, (base, spread) in spreads.items():
        noise = np.random.default_rng([zlib.crc32(name.encode()), seed]).standard_normal(out[name].shape)
        drawn = base * np.exp(spread * noise) if base else spread * noise
        out[name] = jnp.asarray(drawn.astype(out[name].dtype))
    for name, factor in factors.items():
        out[name] = (out[name] * factor).astype(out[name].dtype)
    return out
```

```python
from contextlib import ExitStack

import concourse.bass as bass
from concourse import mybir

F32 = mybir.dt.float32
I32 = mybir.dt.int32
U32 = mybir.dt.uint32
ALU = mybir.AluOpType
ACT = mybir.ActivationFunctionType
AX = mybir.AxisListType

P = 128
D = 16
DE = 8
CH = D * D
TPC = 4
CE = TPC * P
RESET = -(2.0 ** 100)
UW = 48
EPS = 1e-5


def there(index, count):
    return not isinstance(index, int) or 0 <= index < count


def need(engine, semaphore, value):
    if not isinstance(value, int) or value > 0:
        engine.wait_ge(semaphore, value)


class Semaphores:

    def __init__(self, nc):
        self.nc, self.handles = nc, []

    def __enter__(self):
        return self

    def enter(self, name):
        self.handles.append(self.nc.alloc_semaphore(name=name))
        return self.handles[-1]

    def __exit__(self, kind, value, trace):
        if kind is None:
            self.nc.clear_and_free_semaphores(self.handles)
            self.nc.all_engine_barrier()


class Shapes:
    def __init__(self, n, e):
        self.N, self.E = n, e
        self.chunks = -(-e // CE)
        assert self.chunks % 2 == 0 and self.chunks >= 6
        self.tiles = self.chunks * TPC
        self.full = e // P
        self.rest = e - self.full * P
        self.NP = 125
        self.NJ = n // self.NP
        assert self.NP * self.NJ == n and self.NJ % 32 == 0
        self.G = self.tiles // TPC
        self.none = 1 << 21
        self.far = 200000
        assert self.far > n


def waits_apart(engine):
    engine.nop(nofuse=True)


def chunk_loop(engine, chunks, body):
    for c in range(4):
        body(c, c % 2, c // 2)
    with engine.Fori(2, chunks // 2 - 1) as pair:
        for u in (0, 1):
            body(pair * 2 + u, u, pair)
    for c in range(chunks - 2, chunks + 2):
        body(c, c % 2, c // 2)


def constants_and_indices(nc, sems, sh, b, io):
    def sem(name):
        return sems.enter(name)

    G, N = sh.G, sh.N
    zeroed, made, sel_done = sem("zeroed"), sem("made"), sem("sel_done")
    weights_in, edges_in, idx_in = sem("weights_in"), sem("edges_in"), sem("idx_in")
    tables_zero = sem("tables_zero")
    rows_done, turned, columns_done = sem("rows_done"), sem("turned"), sem("columns_done")
    with ExitStack() as scratch:
        dst_rows = scratch.enter_context(nc.sbuf_tensor("dst_rows", [G, TPC, P + 2], I32))
        src_rows = scratch.enter_context(nc.sbuf_tensor("src_rows", [G, TPC, P], I32))
        dst_f = scratch.enter_context(nc.sbuf_tensor("dst_f", [G, TPC, P + 2], F32))
        rows_f = scratch.enter_context(nc.sbuf_tensor("rows_f", [G, 5, TPC, P], F32))
        end_f = scratch.enter_context(nc.sbuf_tensor("end_f", [G, TPC, P], F32))
        turned_ps = [scratch.enter_context(nc.psum_tensor(f"turned_ps{i}", [P, 512], F32)) for i in range(5)]
        START, SCAT, GDST, GSRC, SRC = range(5)
        src, dst = io["src"], io["dst"]
        last = sh.full - 3 * G

        block = scratch.enter_context(nc.Block())

        @block.gpsimd
        def _(pool):
            pool.memset(b.ident[:, :], 0.0).then_inc(zeroed, 1)
            pool.memset(dst_rows[:, :, :], sh.far).then_inc(zeroed, 1)
            pool.memset(src_rows[:, :, :], sh.N).then_inc(zeroed, 1)
            pool.memset(b.zeros[:, :], 0.0).then_inc(zeroed, 1)
            pool.memset(b.ea16[:, :, :], 0.0).then_inc(zeroed, 1)
            pool.memset(b.ea8[:, :, :], 0.0).then_inc(zeroed, 1)
            for w in (b.bd_lin, b.bd_upd, b.bd1a, b.bd1b, b.bd2a, b.bd2b):
                pool.memset(w[:, :], 0.0).then_inc(zeroed, 1)
            pool.memset(b.w_att[:, :], 0.0).then_inc(zeroed, 1)
            pool.memset(b.w_msg[:, :], 0.0).then_inc(zeroed, 1)
            pool.memset(b.w_h[:, :], 1.0).then_inc(made, 1)
            pool.memset(b.w_start[:, :], 0.0).then_inc(made, 1)
            pool.memset(b.lower[:, :], 1.0).then_inc(made, 1)
            pool.memset(b.eps_col[:, :], EPS).then_inc(made, 1)
            for u in range(2):
                pool.memset(b.u[u][:, :, :], 0.0).then_inc(made, 1)
            for a in (b.gsrc, b.gdst, b.scat):
                pool.memset(a[:, :], 0).then_inc(made, 1)
            for a in (b.start, b.srcf):
                pool.memset(a[:, :], 0.0).then_inc(made, 1)
            pool.iota(b.dummy_i[:, :], pattern=[[0, 1]], base=N + 1, channel_multiplier=1).then_inc(made, 1)
            pool.wait_ge(made, 12)
            pool.wait_ge(zeroed, 1)
            pool.affine_select(out=b.ident[:, :], in_=b.ident[:, :], compare_op=ALU.not_equal, fill=1.0,
                               base=0, pattern=[[-1, P]], channel_multiplier=1).then_inc(sel_done, 1)
            pool.affine_select(out=b.w_h[:, :], in_=b.w_h[:, :], compare_op=ALU.is_ge, fill=0.0,
                               base=D * 32, pattern=[[1, CH]], channel_multiplier=-D).then_inc(sel_done, 1)
            pool.wait_ge(sel_done, 2)
            pool.affine_select(out=b.w_h[:, :], in_=b.w_h[:, :], compare_op=ALU.is_ge, fill=0.0,
                               base=-D * 32 + D - 1, pattern=[[-1, CH]], channel_multiplier=D).then_inc(sel_done, 1)
            pool.affine_select(out=b.w_start[:, :], in_=b.w_start[:, :], compare_op=ALU.not_equal, fill=1.0,
                               base=-(D + 1), pattern=[[0, P]], channel_multiplier=1).then_inc(sel_done, 1)
            pool.affine_select(out=b.lower[:, :], in_=b.lower[:, :], compare_op=ALU.is_gt, fill=0.0,
                               base=0, pattern=[[-1, P]], channel_multiplier=1).then_inc(sel_done, 1)

        @block.sync
        def _(sp):
            sp.wait_ge(zeroed, 3)
            for g in range(TPC):
                n = G if g < 3 else last
                r0 = 0 if g else 1
                at = g * G * P
                sp.dma_start(dst_rows[r0:n, g, :], bass.AP(dst.tensor, at + r0 * P - 1, [[P, n - r0], [1, P + 2]])).then_inc(idx_in, 16)
                sp.dma_start(src_rows[0:n, g, :], src[at:at + n * P].rearrange("(r e) -> r e", e=P)).then_inc(idx_in, 16)
            sp.dma_start(dst_rows[0:1, 0, 1:P + 2], dst[0:P + 1].rearrange("(a e) -> a e", a=1)).then_inc(idx_in, 16)
            sp.dma_start(dst_rows[last:last + 1, 3, 0:sh.rest + 1], dst[sh.full * P - 1:sh.E].rearrange("(a e) -> a e", a=1)).then_inc(idx_in, 16)
            sp.dma_start(src_rows[last:last + 1, 3, 0:sh.rest], src[sh.full * P:sh.E].rearrange("(a e) -> a e", a=1)).then_inc(idx_in, 16)
            sp.wait_ge(zeroed, 6)
            for t, name, width in ((b.ea16, "edge_attr_16", D), (b.ea8, "edge_attr_8", DE)):
                a = io[name]
                sp.dma_start(t[:, 0:sh.full, :], a[0:sh.full * P, :].rearrange("(t p) c -> p t c", p=P)).then_inc(edges_in, 16)
                sp.dma_start(t[0:sh.rest, sh.full, :], a[sh.full * P:sh.E, :]).then_inc(edges_in, 16)
            sp.dma_start(b.xn[0:sh.NP, :], io["x"].rearrange("(p j) c -> p (j c)", p=sh.NP)).then_inc(edges_in, 16)
            sp.wait_ge(edges_in, 16 * 5)
            sp.wait_ge(idx_in, 16 * 11)

        @block.scalar
        def _(act):
            act.wait_ge(zeroed, 14)
            act.dma_start(b.w_att[0:D, :], io["L0_gnn_W_attn"]).then_inc(weights_in, 16)
            act.dma_start(b.w_att[D:D + 1, :], io["L0_gnn_b_attn"].rearrange("(a c) -> a c", a=1)).then_inc(weights_in, 16)
            act.dma_start(b.w_msg[0:D, :], io["L0_gnn_W_msg"]).then_inc(weights_in, 16)
            act.dma_start(b.w_msg[D:D + 1, :], io["L0_gnn_b_msg"].rearrange("(a c) -> a c", a=1)).then_inc(weights_in, 16)
            act.dma_start(b.w_tp[:, :], io["L2_gnn_W_msg_tp"].rearrange("i j h -> (i j) h")).then_inc(weights_in, 16)
            act.dma_start(b.w_up[:, :, :], io["L2_gnn_W_upd_tp"].rearrange("(a i) h k -> (i h) a k", a=2)).then_inc(weights_in, 16)
            n = 6
            for w, name in ((b.bd_lin, "L2_gnn_W_msg_lin"), (b.bd_upd, "L2_gnn_W_upd_lin"), (b.bd1a, "L3_gnn_w1a"),
                            (b.bd1b, "L3_gnn_w1b"), (b.bd2a, "L3_gnn_w2a"), (b.bd2b, "L3_gnn_w2b")):
                for k in range(P // D):
                    act.dma_start(w[k * D:(k + 1) * D, k * D:(k + 1) * D], io[name]).then_inc(weights_in, 16)
                    n += 1
            for w, name in ((b.b1a, "L3_gnn_b1a"), (b.b2a, "L3_gnn_b2a")):
                for k in range(P // D):
                    act.dma_start(w[k * D:(k + 1) * D, :], io[name].rearrange("(c a) -> c a", a=1)).then_inc(weights_in, 16)
                    n += 1
            for w, name, width in ((b.b1b, "L3_gnn_b1b", D), (b.b2b, "L3_gnn_b2b", D), (b.eps1, "L3_gnn_eps1", 1), (b.eps2, "L3_gnn_eps2", 1)):
                act.dma_start(w[:, :], bass.AP(io[name].tensor, 0, [[0, P], [1, width]])).then_inc(weights_in, 16)
                n += 1
            per = sh.NJ * 2 * D
            flat = b.t_first.rearrange("(p j) c -> p (j c)", p=sh.NP)
            for k in range(per // b.zw):
                act.dma_start(flat[:, k * b.zw:(k + 1) * b.zw], b.zeros[0:sh.NP, :]).then_inc(tables_zero, 16)
            act.wait_ge(weights_in, 16 * n)
            act.wait_ge(tables_zero, 16 * (per // b.zw))

        @block.vector
        def _(dve):
            dve.wait_ge(idx_in, 16 * 11)
            dve.tensor_copy(dst_f[:, :, :], dst_rows[:, :, :]).then_inc(rows_done, 1)
            dve.tensor_copy(rows_f[:, SRC, :, :], src_rows[:, :, :]).then_inc(rows_done, 1)
            dve.wait_ge(rows_done, 2)
            here = dst_f[:, :, 1:P + 1]
            dve.tensor_tensor(rows_f[:, START, :, :], here, dst_f[:, :, 0:P], ALU.not_equal).then_inc(rows_done, 1)
            dve.tensor_tensor(end_f[:, :, :], here, dst_f[:, :, 2:P + 2], ALU.is_equal).then_inc(rows_done, 1)
            dve.tensor_scalar(rows_f[:, GDST, :, :], here, float(N - 1), None, ALU.min).then_inc(rows_done, 1)
            dve.tensor_scalar(rows_f[:, GSRC, :, :], rows_f[:, SRC, :, :], float(N - 1), None, ALU.min).then_inc(rows_done, 1)
            dve.wait_ge(rows_done, 4)
            dve.scalar_tensor_tensor(rows_f[:, SCAT, :, :], end_f[:, :, :], float(sh.none), here, ALU.mult, ALU.add).then_inc(rows_done, 1)
            dve.wait_ge(made, 12)
            dve.wait_ge(turned, 5)
            for k, out in ((START, b.start), (SCAT, b.scat), (GDST, b.gdst), (GSRC, b.gsrc), (SRC, b.srcf)):
                dve.tensor_copy(out[:, 0:sh.tiles], turned_ps[k][:, 0:sh.tiles]).then_inc(columns_done, 1)
            dve.tensor_copy(b.dummy[:, :], b.dummy_i[:, :]).then_inc(columns_done, 1)
            dve.wait_ge(sel_done, 5)
            dve.tensor_reduce(b.sel[:, :], b.ident[:, :].rearrange("p (i o) -> p o i", o=D), AX.X, ALU.add).then_inc(columns_done, 1)
            for u in range(2):
                dve.memset(b.u[u][:, :, D:D + 1], 1.0).then_inc(columns_done, 1)
                dve.memset(b.e2[u][:, :, 0:1], 0.0).then_inc(columns_done, 1)
            dve.wait_ge(weights_in, 16 * (6 + 48 + 16 + 4))
            dve.tensor_scalar(b.eps1[:, :], b.eps1[:, :], 1.0, None, ALU.add).then_inc(columns_done, 1)
            dve.tensor_scalar(b.eps2[:, :], b.eps2[:, :], 1.0, None, ALU.add).then_inc(columns_done, 1)

        @block.tensor
        def _(pe):
            pe.wait_ge(sel_done, 1)
            pe.wait_ge(rows_done, 7)
            for k in range(5):
                for g in range(TPC):
                    mm = pe.transpose(turned_ps[k][:, g * G:(g + 1) * G], rows_f[:, k, g, :], b.ident[0:G, 0:G])
                mm.then_inc(turned, 1)


def attention_layer(nc, sems, sh, b, io):
    def sem(name):
        return sems.enter(name)

    C, S = sh.chunks, 2 * sh.chunks
    with ExitStack() as scratch:
        def sb(name, shape, dt=F32):
            return scratch.enter_context(nc.sbuf_tensor(name, shape, dt))

        def ps(name):
            return scratch.enter_context(nc.psum_tensor(name, [P, 512], F32))

        gather_idx = [sb(f"a_gather_idx{i}", [P, TPC], U32) for i in range(2)]
        scatter_idx = [sb(f"a_scatter_idx{i}", [P, TPC], U32) for i in range(2)]
        x_src = [sb(f"a_x_src{i}", [P, TPC, D]) for i in range(2)]
        ut = [sb(f"a_ut{i}", [UW, CE]) for i in range(2)]
        inside = sb("a_inside", [D + 1, CE])
        h_rep = [sb(f"a_h_rep{i}", [P, CE]) for i in range(2)]
        mp = [sb(f"a_mp{i}", [P, 2, CE]) for i in range(2)]
        q = [sb(f"a_q{i}", [P, CE]) for i in range(2)]
        relus = sb("a_relus", [P, 2, CE])
        exps = [sb(f"a_exps{i}", [P, 2, CE]) for i in range(2)]
        msg = [sb(f"a_msg{i}", [P, CE]) for i in range(2)]
        den = [sb(f"a_den{i}", [P, 2, CE]) for i in range(2)]
        num = [sb(f"a_num{i}", [P, 2, CE]) for i in range(2)]
        log_den = sb("a_log_den", [P, CE])
        inv_den = [sb(f"a_inv_den{i}", [P, CE]) for i in range(2)]
        ratio = [sb(f"a_ratio{i}", [P, CE]) for i in range(2)]
        attr_sum = [sb(f"a_attr_sum{i}", [D + 1, CE]) for i in range(2)]
        back = [sb(f"a_back{i}", [P, TPC, D + 1]) for i in range(2)]
        inv_count = sb("a_inv_count", [P, TPC, 1])
        rows = [sb(f"a_rows{i}", [P, TPC, 2 * D]) for i in range(2)]

        t_ps, f_ps, h_ps, o_ps = ps("a_tps"), ps("a_fps"), ps("a_hps"), ps("a_ops")
        wa_ps = [ps(f"a_waps{i}") for i in range(2)]
        wm_ps = [ps(f"a_wmps{i}") for i in range(2)]

        ft_ps = o_ps[:, 0:TPC * D]
        back_ps = o_ps[:, 128:256].rearrange("p (t c) -> p t c", t=TPC)

        idx_staged, gathered = sem("a_idx_staged"), [sem(f"a_gathered{i}") for i in range(2)]
        u_ready, u_turned, ut_ready = sem("a_u_ready"), sem("a_u_turned"), sem("a_ut_ready")
        start_spread, h_spread, projected = sem("a_start_spread"), sem("a_h_spread"), sem("a_projected")
        inside_ready, h_ready = sem("a_inside_ready"), sem("a_h_ready")
        e2_done, carried, mp_done, q_done, msg_done = (
            sem("a_e2_done"), sem("a_carried"), sem("a_mp_done"), sem("a_q_done"), sem("a_msg_done"))
        relu_done, exp_done = sem("a_relu_done"), sem("a_exp_done")
        den_done, weighted, num_done = sem("a_den_done"), sem("a_weighted"), sem("a_num_done")
        log_done, inv_done, ratio_done = sem("a_log_done"), sem("a_inv_done"), sem("a_ratio_done")
        ft_done, attr_sum_done, turned_back = sem("a_ft_done"), sem("a_attr_sum_done"), sem("a_turned_back")
        inv_count_done, mean_done, ft_copied, back_copied = (
            sem("a_inv_count_done"), sem("a_mean_done"), sem("a_ft_copied"), sem("a_back_copied"))
        scattered = [sem(f"a_scattered{i}") for i in range(2)]
        tables_zero = sem("a_tables_zero")

        block = scratch.enter_context(nc.Block())

        @block.sync
        def _(sp):
            n = 0
            per = sh.NJ * D
            for t in [*b.t_adds, b.t_seg1, b.t_seg2]:
                flat = t[0:sh.N, :].rearrange("(p j) c -> p (j c)", p=sh.NP)
                for k in range(per // b.zw):
                    sp.dma_start(flat[:, k * b.zw:(k + 1) * b.zw], b.zeros[0:sh.NP, :]).then_inc(tables_zero, 16)
                    n += 1
            for t in b.t_adds:
                sp.dma_start(t[sh.N:sh.N + P, :], b.zeros[:, 0:D]).then_inc(tables_zero, 16)
                sp.dma_start(t[sh.N + P:sh.N + P + 1, :], b.zeros[0:1, 0:D]).then_inc(tables_zero, 16)
                n += 2
            sp.wait_ge(tables_zero, 16 * n)

        @block.gpsimd
        def _(pool):
            def gather(c, u):
                pool.wait_ge(idx_staged, c + 1)
                waits_apart(pool)
                for k in range(TPC):
                    pool.indirect_dma_start(out=x_src[u][:, k, :], out_offset=None, in_=io["x"],
                                            in_offset=bass.IndirectOffsetOnAxis(ap=gather_idx[u][:, k:k + 1], axis=0),
                                            ).then_inc(gathered[u], 16)

            def scatter(c, u):
                pool.wait_ge(ft_copied, 2 * (c + 1))
                pool.wait_ge(mean_done, c + 1)
                waits_apart(pool)
                for k in range(TPC):
                    pool.indirect_dma_start(out=b.t_first, out_offset=bass.IndirectOffsetOnAxis(ap=scatter_idx[u][:, k:k + 1], axis=0),
                                            in_=rows[u][:, k, :], in_offset=None,
                                            bounds_check=sh.N - 1, oob_is_err=False).then_inc(scattered[u], 16)

            for c in range(3):
                gather(c, c % 2)

            def body(c, u, pair):
                if there(c + 3, C):
                    gather(c + 3, 1 - u)
                if there(c - 2, C):
                    scatter(c - 2, u)

            chunk_loop(pool, C, body)
            for u in range(2):
                pool.wait_ge(scattered[u], 16 * TPC * (C // 2))

        @block.scalar
        def _(act):
            def stage_gather(c, u):
                act.activation(gather_idx[u][:, :], b.gsrc[:, bass.ds(c * TPC, TPC)], ACT.Copy).then_inc(idx_staged, 1)

            def build_u(c, u, pair):
                need(act, u_turned, c - 1)
                act.activation(b.u[u][:, :, 0:D], b.ea16[:, bass.ds(c * TPC, TPC), :], ACT.Copy).then_inc(u_ready, 1)
                act.activation(b.u[u][:, :, D + 1], b.start[:, bass.ds(c * TPC, TPC)], ACT.Copy,
                               scale=RESET).then_inc(u_ready, 1)
                act.wait_ge(gathered[u], (pair + 1) * (16 * TPC))
                act.activation(b.u[u][:, :, 32:48], x_src[u][:, :, :], ACT.Copy).then_inc(u_ready, 1)
                act.wait_ge(u_ready, 3 * (c + 1))
                stage_gather(c + 2, u)

            def evacuate_ut(c, u):
                act.wait_ge(u_turned, c + 1)
                need(act, projected, 2 * (c - 1))
                need(act, attr_sum_done, c - 1)
                act.activation(ut[u][:, :], t_ps[0:UW, :], ACT.Copy).then_inc(ut_ready, 1)

            def copy_h(s, h):
                act.wait_ge(h_spread, s + 1)
                need(act, msg_done, s - 1)
                act.activation(h_rep[h][:, :], h_ps[:, :], ACT.Copy).then_inc(h_ready, 1)

            def copy_inside(c):
                need(act, attr_sum_done, c)
                act.wait_ge(start_spread, c + 1)
                act.activation(inside[:, :], f_ps[0:D + 1, :], ACT.Copy, scale=-1.0 / RESET, bias=1.0).then_inc(inside_ready, 1)

            def softmax_factors(s, h):
                act.wait_ge(q_done, s + 1)
                need(act, exp_done, s)
                act.activation(relus[:, 0, :], q[h][:, :], ACT.Relu).then_inc(relu_done, 1)
                act.activation(relus[:, 1, :], q[h][:, :], ACT.Relu, scale=-1.0).then_inc(relu_done, 1)
                act.wait_ge(relu_done, 2 * (s + 1))
                need(act, num_done, s - 1)
                act.activation(exps[h][:, :, :], relus[:, :, :], ACT.Exp, scale=-1.0).then_inc(exp_done, 1)

            def invert_den(s, u, h):
                act.wait_ge(den_done, s + 1)
                need(act, inv_done, s)
                act.activation(log_den[:, :], den[u][:, h, :], ACT.Ln).then_inc(log_done, 1)
                act.wait_ge(log_done, s + 1)
                need(act, ratio_done, s - 1)
                act.activation(inv_den[h][:, :], log_den[:, :], ACT.Exp, scale=-1.0).then_inc(inv_done, 1)

            def copy_ft(c, u, pair):
                act.wait_ge(ft_done, 2 * (c + 1))
                need(act, scattered[u], pair * (16 * TPC))
                act.activation(rows[u][:, :, 0:D], ft_ps.rearrange("p (t c) -> p t c", t=TPC), ACT.Copy).then_inc(ft_copied, 1)
                act.activation(scatter_idx[u][:, :], b.scat[:, bass.ds(c * TPC, TPC)], ACT.Copy).then_inc(ft_copied, 1)

            def copy_back(c, u):
                act.wait_ge(turned_back, c + 1)
                need(act, ft_done, 2 * c - 1)
                need(act, mean_done, c - 1)
                act.activation(back[u][:, :, :], back_ps[:, :, 0:D + 1], ACT.Copy).then_inc(back_copied, 1)

            for c in range(2):
                stage_gather(c, c)
            for c in range(2):
                build_u(c, c, 0)
            evacuate_ut(0, 0)

            def body(c, u, pair):
                for h in (0, 1):
                    s = c * 2 + h
                    if h == 0 and there(c - 1, C):
                        copy_back(c - 1, 1 - u)
                    if h == 1 and there(c - 2, C):
                        copy_ft(c - 2, u, pair - 1)
                    if h == 1 and there(c + 1, C):
                        evacuate_ut(c + 1, 1 - u)
                    if there(s, S):
                        copy_h(s, h)
                        if h == 0:
                            copy_inside(c)
                        softmax_factors(s, h)
                    if there(s - 1, S):
                        invert_den(s - 1, u if h else 1 - u, 1 - h)
                if there(c + 2, C):
                    build_u(c + 2, u, pair + 1)

            chunk_loop(act, C, body)

        @block.tensor
        def _(pe):
            def turn_u(c, u):
                pe.wait_ge(u_ready, 3 * (c + 1))
                need(pe, ut_ready, c)
                waits_apart(pe)
                for k in range(TPC):
                    mm = pe.transpose(t_ps[0:UW, k * P:(k + 1) * P], b.u[u][:, k, :], b.ident[:, :])
                mm.then_inc(u_turned, 1)

            def project(c, u, s, h):
                cols = slice(h * P, (h + 1) * P)
                if h == 0:
                    pe.wait_ge(ut_ready, c + 1)
                    need(pe, mp_done, 2 * c)
                    need(pe, inside_ready, c)
                    pe.matmul(f_ps[:, :], b.w_start[:, :], ut[u][:, :], start=True, stop=True).then_inc(start_spread, 1)
                need(pe, h_ready, s)
                pe.matmul(h_ps[:, :], b.w_h[:, cols], ut[u][:, :], start=True, stop=True).then_inc(h_spread, 1)
                need(pe, msg_done, s - 1)
                need(pe, e2_done, s - 1)
                pe.matmul(wa_ps[h][:, :], b.w_att[:, cols], ut[u][:, :], start=True, stop=True)
                pe.matmul(wm_ps[h][:, :], b.w_msg[:, cols], ut[u][:, :], start=True, stop=True).then_inc(projected, 1)

            def sum_inputs(s, c, u, h):
                pe.wait_ge(ratio_done, s + 1)
                if h == 0:
                    need(pe, ft_copied, 2 * c)
                else:
                    need(pe, back_copied, c + 2 if not isinstance(c, int) or c + 2 <= C else C)
                for k in range(TPC):
                    mm = pe.matmul(ft_ps[:, k * D:(k + 1) * D], ratio[h][:, k * P:(k + 1) * P], b.sel[:, :],
                                   start=(h == 0 and k == 0), stop=(h == 1), skip_group_check=True)
                mm.then_inc(ft_done, 1)

            def turn_sums_back(c, u):
                pe.wait_ge(attr_sum_done, c + 1)
                need(pe, ft_copied, 2 * (c - 1))
                waits_apart(pe)
                for k in range(TPC):
                    mm = pe.transpose(back_ps[:, k, 0:D + 1], attr_sum[u][:, k * P:(k + 1) * P], b.ident[0:D + 1, 0:D + 1])
                mm.then_inc(turned_back, 1)

            turn_u(0, 0)

            def body(c, u, pair):
                for h in (0, 1):
                    s = c * 2 + h
                    if h == 0 and there(c + 1, C):
                        turn_u(c + 1, 1 - u)
                    if there(s, S):
                        project(c, u, s, h)
                    if h == 1 and there(c, C):
                        turn_sums_back(c, u)
                    if there(s - 3, S):
                        if h == 0:
                            sum_inputs(s - 3, c - 2, u, 1)
                        else:
                            sum_inputs(s - 3, c - 1, 1 - u, 0)

            chunk_loop(pe, C, body)

        @block.vector
        def _(dve):
            def logits_and_maximum(c, u, s, h):
                dve.wait_ge(h_ready, s + 1)
                dve.wait_ge(projected, s + 1)
                dve.tensor_tensor(b.e2[u][:, h, 1:CE + 1], wa_ps[h][:, :], h_rep[h][:, :], ALU.mult).then_inc(e2_done, 1)
                need(dve, num_done, s - 1)
                dve.tensor_tensor(msg[h][:, :], wm_ps[h][:, :], h_rep[h][:, :], ALU.mult).then_inc(msg_done, 1)
                dve.wait_ge(e2_done, s + 1)
                need(dve, mp_done, s - 1)
                dve.tensor_copy(b.e2[1 - u][:, h, 0:1], b.e2[u][:, h, CE:CE + 1]).then_inc(carried, 1)
                dve.wait_ge(inside_ready, c + 1)
                need(dve, carried, s - 1)
                dve.tensor_tensor_scan(mp[u][:, h, :], b.e2[u][:, h, 0:CE], f_ps[:, :],
                                       0.0 if isinstance(c, int) and c == 0 else mp[1 - u][:, h, CE - 1:CE],
                                       ALU.max, ALU.add).then_inc(mp_done, 1)
                dve.wait_ge(mp_done, s + 1)
                need(dve, relu_done, 2 * (s - 1))
                dve.tensor_tensor(q[h][:, :], mp[u][:, h, :], b.e2[u][:, h, 1:CE + 1], ALU.subtract).then_inc(q_done, 1)

            def sums(c, u, s, h):
                first = isinstance(c, int) and c == 0
                dve.wait_ge(exp_done, s + 1)
                dve.wait_ge(msg_done, s + 1)
                dve.tensor_tensor(msg[h][:, :], msg[h][:, :], exps[h][:, 0, :], ALU.mult).then_inc(weighted, 1)
                need(dve, den_done, s - 1)
                dve.tensor_tensor_scan(den[u][:, h, :], exps[h][:, 1, :], exps[h][:, 0, :],
                                       0.0 if first else den[1 - u][:, h, CE - 1:CE],
                                       ALU.mult, ALU.add).then_inc(den_done, 1)
                dve.wait_ge(weighted, s + 1)
                need(dve, num_done, s - 1)
                dve.tensor_tensor_scan(num[u][:, h, :], exps[h][:, 1, :], msg[h][:, :],
                                       0.0 if first else num[1 - u][:, h, CE - 1:CE],
                                       ALU.mult, ALU.add).then_inc(num_done, 1)

            def divide(s, u, h):
                dve.wait_ge(inv_done, s + 1)
                dve.wait_ge(num_done, s + 1)
                need(dve, ft_done, s - 1)
                dve.tensor_tensor(ratio[h][:, :], num[u][:, h, :], inv_den[h][:, :], ALU.mult).then_inc(ratio_done, 1)

            def attribute_sums(c, u):
                dve.wait_ge(inside_ready, c + 1)
                need(dve, turned_back, c - 1)
                need(dve, attr_sum_done, c)
                dve.tensor_tensor_scan(attr_sum[u][:, :], inside[:, :], ut[u][0:D + 1, :],
                                       0.0 if isinstance(c, int) and c == 0 else attr_sum[1 - u][:, CE - 1:CE],
                                       ALU.mult, ALU.add).then_inc(attr_sum_done, 1)

            def attribute_mean(c, u, pair):
                dve.wait_ge(back_copied, c + 1)
                need(dve, mean_done, c)
                dve.reciprocal(inv_count[:, :, :], back[u][:, :, D:D + 1]).then_inc(inv_count_done, 1)
                dve.wait_ge(inv_count_done, c + 1)
                need(dve, scattered[u], pair * (16 * TPC))
                dve.tensor_tensor(rows[u][:, :, D:2 * D], back[u][:, :, 0:D],
                                  inv_count[:, :, :].broadcast_to([P, TPC, D]), ALU.mult).then_inc(mean_done, 1)

            def body(c, u, pair):
                for h in (0, 1):
                    s = c * 2 + h
                    if there(s, S):
                        logits_and_maximum(c, u, s, h)
                    if h == 0 and there(c, C):
                        attribute_sums(c, u)
                    if h == 1 and there(c - 1, C):
                        attribute_mean(c - 1, 1 - u, pair if u else pair - 1)
                    if there(s - 1, S):
                        if h == 0:
                            sums(c - 1, 1 - u, s - 1, 1)
                        else:
                            sums(c, u, s - 1, 0)
                    if there(s - 2, S):
                        divide(s - 2, 1 - u, h)

            chunk_loop(dve, C, body)


def message_layer(nc, sems, sh, b, io):
    def sem(name):
        return sems.enter(name)

    C = sh.chunks
    W = TPC * D
    with ExitStack() as scratch:
        def sb(name, shape, dt=F32):
            return scratch.enter_context(nc.sbuf_tensor(name, shape, dt))

        def ps(name):
            return scratch.enter_context(nc.psum_tensor(name, [P, 512], F32))

        gather_idx = [sb(f"m_gather_idx{i}", [P, TPC], U32) for i in range(2)]
        add_idx = [sb(f"m_add_idx{i}", [P, TPC], U32) for i in range(2)]
        x_dst = [sb(f"m_x_dst{i}", [P, TPC, D]) for i in range(2)]
        z = [sb(f"m_z{i}", [P, TPC, D, DE]) for i in range(2)]
        zt = [sb(f"m_zt{i}", [P, CE]) for i in range(2)]
        act_m = [sb(f"m_act{i}", [P, W]) for i in range(2)]
        act_mt = [sb(f"m_act_t{i}", [W, P]) for i in range(2)]
        m = [sb(f"m_m{i}", [P, W]) for i in range(2)]
        sums = [sb(f"m_sums{i}", [P, TPC, D]) for i in range(2)]
        src = [sb(f"m_src{i}", [P, TPC]) for i in range(2)]
        equal = [sb(f"m_equal{i}", [P, TPC, P]) for i in range(2)]
        earlier = sb("m_earlier", [P, TPC, P])
        before = sb("m_before", [P, TPC])
        to_dummy = sb("m_to_dummy", [P, TPC])
        shift = sb("m_shift", [P, TPC])

        z_ps = [ps(f"m_zps{i}") for i in range(2)]
        src_ps, pre_ps, t_ps, m_ps, sum_ps = ps("m_srcps"), ps("m_preps"), ps("m_tps"), ps("m_mps"), ps("m_sumps")

        idx_staged, gathered = sem("m_idx_staged"), [sem(f"m_gathered{i}") for i in range(2)]
        z_done, z_turned, zt_ready, pre_done, act_done = (
            sem("m_z_done"), sem("m_z_turned"), sem("m_zt_ready"), sem("m_pre_done"), sem("m_act_done"))
        act_turned, act_t_ready, m_done, m_ready = sem("m_act_turned"), sem("m_act_t_ready"), sem("m_m_done"), sem("m_m_ready")
        src_staged, src_spread, equal_done = sem("m_src_staged"), sem("m_src_spread"), sem("m_equal_done")
        earlier_done, before_done, dummy_done, shift_done, add_idx_ready = (
            sem("m_earlier_done"), sem("m_before_done"), sem("m_dummy_done"), sem("m_shift_done"), sem("m_add_idx_ready"))
        summed, sums_ready = sem("m_summed"), sem("m_sums_ready")
        added = [sem(f"m_added{k}") for k in range(TPC)]

        block = scratch.enter_context(nc.Block())

        @block.gpsimd
        def _(pool):
            def gather(c, u):
                pool.wait_ge(idx_staged, c + 1)
                waits_apart(pool)
                for k in range(TPC):
                    pool.indirect_dma_start(out=x_dst[u][:, k, :], out_offset=None, in_=b.t_x,
                                            in_offset=bass.IndirectOffsetOnAxis(ap=gather_idx[u][:, k:k + 1], axis=0),
                                            ).then_inc(gathered[u], 16)

            def add(c, u):
                pool.wait_ge(sums_ready, c + 1)
                pool.wait_ge(add_idx_ready, c + 1)
                for k in range(TPC):
                    need(pool, added[k], c * 16)
                    waits_apart(pool)
                    pool.indirect_dma_start(out=b.t_adds[k], out_offset=bass.IndirectOffsetOnAxis(ap=add_idx[u][:, k:k + 1], axis=0),
                                            in_=sums[u][:, k, :], in_offset=None, compute_op=ALU.add,
                                            ).then_inc(added[k], 16)

            for c in range(2):
                gather(c, c)

            def body(c, u, pair):
                if there(c + 2, C):
                    gather(c + 2, u)
                if there(c - 2, C):
                    add(c - 2, u)

            chunk_loop(pool, C, body)
            for k in range(TPC):
                pool.wait_ge(added[k], 16 * C)

        @block.scalar
        def _(act):
            def stage_gather(c, u):
                need(act, z_done, c - 1)
                act.activation(gather_idx[u][:, :], b.gdst[:, bass.ds(c * TPC, TPC)], ACT.Copy).then_inc(idx_staged, 1)

            def stage_src(c, u):
                need(act, add_idx_ready, c - 1)
                need(act, src_spread, c - 1)
                act.activation(src[u][:, :], b.srcf[:, bass.ds(c * TPC, TPC)], ACT.Copy).then_inc(src_staged, 1)

            def early(c, u):
                act.wait_ge(z_turned, c + 1)
                need(act, pre_done, c - 1)
                act.activation(zt[u][:, :], z_ps[u][:, :], ACT.Copy).then_inc(zt_ready, 1)

            def turn(c, u):
                act.wait_ge(act_turned, c + 1)
                need(act, m_done, c - 1)
                act.activation(act_mt[u][:, :], t_ps[0:W, 0:P], ACT.Copy).then_inc(act_t_ready, 1)

            def silu(c, u):
                act.wait_ge(pre_done, c + 1)
                need(act, act_turned, c - 1)
                act.activation(act_m[u][:, :], pre_ps[:, 0:W], ACT.Silu, scale=float(D * DE) ** -0.5).then_inc(act_done, 1)

            def late(c, u):
                act.wait_ge(m_done, c + 1)
                need(act, summed, c - 1)
                act.activation(m[u][:, :], m_ps[:, 0:W], ACT.Copy, scale=float(D) ** -0.5).then_inc(m_ready, 1)
                act.wait_ge(summed, c + 1)
                for k in range(TPC):
                    need(act, added[k], (c - 1) * 16)
                act.activation(sums[u][:, :, :], sum_ps[:, 0:W].rearrange("p (t c) -> p t c", t=TPC), ACT.Copy).then_inc(sums_ready, 1)

            for c in range(2):
                stage_gather(c, c)
                stage_src(c, c)

            def body(c, u, pair):
                if there(c, C):
                    early(c, u)
                if there(c - 1, C):
                    turn(c - 1, 1 - u)
                if there(c, C):
                    silu(c, u)
                if there(c - 1, C):
                    late(c - 1, 1 - u)
                if there(c + 2, C):
                    stage_gather(c + 2, u)
                    stage_src(c + 2, u)

            chunk_loop(act, C, body)

        @block.tensor
        def _(pe):
            def spread_src(c, u):
                pe.wait_ge(src_staged, c + 1)
                need(pe, equal_done, TPC * c)
                for k in range(TPC):
                    mm = pe.matmul(src_ps[:, k * P:(k + 1) * P], src[u][:, k:k + 1].broadcast_to([P, P]), b.ident[:, :],
                                   start=True, stop=True)
                mm.then_inc(src_spread, 1)

            def turn_z(c, u):
                pe.wait_ge(z_done, c + 1)
                need(pe, zt_ready, c - 1)
                waits_apart(pe)
                for k in range(TPC):
                    mm = pe.transpose(z_ps[u][:, k * P:(k + 1) * P], z[u][:, k, :, :].rearrange("p i j -> p (i j)"), b.ident[:, :])
                mm.then_inc(z_turned, 1)

            def mix(c, u):
                pe.wait_ge(zt_ready, c + 1)
                need(pe, act_done, c)
                for k in range(TPC):
                    mm = pe.matmul(pre_ps[:, k * D:(k + 1) * D], zt[u][:, k * P:(k + 1) * P], b.w_tp[:, :], start=True, stop=True)
                mm.then_inc(pre_done, 1)

            def turn_act(c, u):
                pe.wait_ge(act_done, c + 1)
                need(pe, act_t_ready, c)
                waits_apart(pe)
                pe.transpose(t_ps[0:W, 0:P], act_m[u][:, :], b.ident[:, :]).then_inc(act_turned, 1)

            def linear(c, u):
                pe.wait_ge(act_t_ready, c + 1)
                need(pe, m_ready, c)
                pe.matmul(m_ps[:, 0:W], act_mt[u][:, :], b.bd_lin[0:W, 0:W], start=True, stop=True).then_inc(m_done, 1)

            def sum_equal(c, u):
                pe.wait_ge(m_ready, c + 1)
                pe.wait_ge(equal_done, TPC * (c + 1))
                need(pe, sums_ready, c)
                for k in range(TPC):
                    mm = pe.matmul(sum_ps[:, k * D:(k + 1) * D], equal[u][:, k, :], m[u][:, k * D:(k + 1) * D], start=True, stop=True)
                mm.then_inc(summed, 1)

            def body(c, u, pair):
                if there(c, C):
                    spread_src(c, u)
                    turn_z(c, u)
                if there(c - 1, C):
                    turn_act(c - 1, 1 - u)
                if there(c, C):
                    mix(c, u)
                if there(c - 1, C):
                    linear(c - 1, 1 - u)
                    sum_equal(c - 1, 1 - u)

            chunk_loop(pe, C, body)

        @block.vector
        def _(dve):
            def body(c, u, pair):
                if not there(c, C):
                    return
                dve.wait_ge(gathered[u], (pair + 1) * (16 * TPC))
                need(dve, z_turned, c - 1)
                dve.tensor_tensor(z[u][:, :, :, :], x_dst[u][:, :, :].unsqueeze(3).broadcast_to([P, TPC, D, DE]),
                                  b.ea8[:, bass.ds(c * TPC, TPC), :].unsqueeze(2).broadcast_to([P, TPC, D, DE]),
                                  ALU.mult).then_inc(z_done, 1)
                dve.wait_ge(src_spread, c + 1)
                need(dve, summed, c - 1)
                for k in range(TPC):
                    dve.tensor_scalar(equal[u][:, k, :], src_ps[:, k * P:(k + 1) * P], src[u][:, k:k + 1], None,
                                      ALU.is_equal).then_inc(equal_done, 1)
                dve.tensor_scalar(to_dummy[:, :], src[u][:, :], -1.0, b.dummy[:, 0:1], ALU.mult, ALU.add).then_inc(dummy_done, 1)
                dve.wait_ge(equal_done, TPC * (c + 1))
                dve.tensor_tensor(earlier[:, :, :], equal[u][:, :, :], b.lower[:, :].unsqueeze(1).broadcast_to([P, TPC, P]),
                                  ALU.mult).then_inc(earlier_done, 1)
                dve.wait_ge(earlier_done, c + 1)
                dve.tensor_reduce(before[:, :], earlier[:, :, :], AX.X, ALU.add).then_inc(before_done, 1)
                dve.wait_ge(before_done, c + 1)
                dve.wait_ge(dummy_done, c + 1)
                dve.scalar_tensor_tensor(shift[:, :], before[:, :], 1.0, to_dummy[:, :], ALU.min, ALU.mult).then_inc(shift_done, 1)
                dve.wait_ge(shift_done, c + 1)
                for k in range(TPC):
                    need(dve, added[k], (c - 1) * 16)
                dve.tensor_tensor(add_idx[u][:, :], shift[:, :], src[u][:, :], ALU.add).then_inc(add_idx_ready, 1)

            chunk_loop(dve, C, body)


def neighbour_sums(nc, sems, sh, b, name, table_in, table_out):
    def sem(what):
        return sems.enter(name + what)

    C = sh.chunks
    with ExitStack() as scratch:
        def sb(what, shape, dt=F32):
            return scratch.enter_context(nc.sbuf_tensor(name + what, shape, dt))

        def ps(what):
            return scratch.enter_context(nc.psum_tensor(name + what, [P, 512], F32))

        gather_idx = [sb(f"gather_idx{i}", [P, TPC], U32) for i in range(2)]
        scatter_idx = [sb(f"scatter_idx{i}", [P, TPC], U32) for i in range(2)]
        x_src = [sb(f"x_src{i}", [P, TPC, D]) for i in range(2)]
        mask = [sb(f"mask{i}", [P, TPC, D]) for i in range(2)]
        inside = [sb(f"inside{i}", [D, CE]) for i in range(2)]
        run = [sb(f"run{i}", [D, CE]) for i in range(2)]
        rows = [sb(f"rows{i}", [P, TPC, D]) for i in range(2)]
        x_ps = [ps(f"x_ps{i}") for i in range(2)]
        mask_ps = [ps(f"mask_ps{i}") for i in range(2)]
        back_ps = [ps(f"back_ps{i}") for i in range(2)]
        idx_staged, gathered = sem("idx_staged"), [sem(f"gathered{i}") for i in range(2)]
        mask_staged, mask_turned, inside_ready = sem("mask_staged"), sem("mask_turned"), sem("inside_ready")
        x_turned, run_done, turned_back, rows_ready = sem("x_turned"), sem("run_done"), sem("turned_back"), sem("rows_ready")
        scattered = [sem(f"scattered{i}") for i in range(2)]

        block = scratch.enter_context(nc.Block())

        @block.gpsimd
        def _(pool):
            def gather(c, u):
                pool.wait_ge(idx_staged, c + 1)
                waits_apart(pool)
                for k in range(TPC):
                    pool.indirect_dma_start(out=x_src[u][:, k, :], out_offset=None, in_=table_in,
                                            in_offset=bass.IndirectOffsetOnAxis(ap=gather_idx[u][:, k:k + 1], axis=0),
                                            ).then_inc(gathered[u], 16)

            for c in range(2):
                gather(c, c)

            def body(c, u, pair):
                if there(c + 2, C):
                    gather(c + 2, u)
                if there(c - 1, C):
                    pool.wait_ge(rows_ready, 2 * c)
                    waits_apart(pool)
                    for k in range(TPC):
                        pool.indirect_dma_start(out=table_out, out_offset=bass.IndirectOffsetOnAxis(ap=scatter_idx[1 - u][:, k:k + 1], axis=0),
                                                in_=rows[1 - u][:, k, :], in_offset=None,
                                                bounds_check=sh.N - 1, oob_is_err=False).then_inc(scattered[1 - u], 16)

            chunk_loop(pool, C, body)
            for u in range(2):
                pool.wait_ge(scattered[u], 16 * TPC * (C // 2))

        @block.scalar
        def _(act):
            def stage(c, u):
                need(act, x_turned, c - 1)
                act.activation(gather_idx[u][:, :], b.gsrc[:, bass.ds(c * TPC, TPC)], ACT.Copy).then_inc(idx_staged, 1)
                need(act, mask_turned, c - 1)
                act.activation(mask[u][:, :, :], b.start[:, bass.ds(c * TPC, TPC)].unsqueeze(2).broadcast_to([P, TPC, D]),
                               ACT.Copy, scale=-1.0, bias=1.0).then_inc(mask_staged, 1)

            def mask_out(c, u):
                act.wait_ge(mask_turned, c + 1)
                need(act, run_done, c - 1)
                act.activation(inside[u][:, :], mask_ps[u][0:D, :], ACT.Copy).then_inc(inside_ready, 1)

            def rows_out(c, u, pair):
                act.wait_ge(turned_back, c + 1)
                need(act, scattered[u], pair * (16 * TPC))
                act.activation(rows[u][:, :, :], back_ps[u][:, 0:TPC * D].rearrange("p (t c) -> p t c", t=TPC), ACT.Copy).then_inc(rows_ready, 1)
                act.activation(scatter_idx[u][:, :], b.scat[:, bass.ds(c * TPC, TPC)], ACT.Copy).then_inc(rows_ready, 1)

            for c in range(2):
                stage(c, c)

            def body(c, u, pair):
                if there(c, C):
                    mask_out(c, u)
                if there(c + 2, C):
                    stage(c + 2, u)
                if there(c, C):
                    rows_out(c, u, pair)

            chunk_loop(act, C, body)

        @block.tensor
        def _(pe):
            def body(c, u, pair):
                if not there(c, C):
                    return
                pe.wait_ge(mask_staged, c + 1)
                need(pe, inside_ready, c - 1)
                waits_apart(pe)
                for k in range(TPC):
                    mm = pe.transpose(mask_ps[u][0:D, k * P:(k + 1) * P], mask[u][:, k, :], b.ident[:, :])
                mm.then_inc(mask_turned, 1)
                pe.wait_ge(gathered[u], (pair + 1) * (16 * TPC))
                need(pe, run_done, c - 1)
                waits_apart(pe)
                for k in range(TPC):
                    mm = pe.transpose(x_ps[u][0:D, k * P:(k + 1) * P], x_src[u][:, k, :], b.ident[:, :])
                mm.then_inc(x_turned, 1)
                pe.wait_ge(run_done, c + 1)
                need(pe, rows_ready, 2 * (c - 1))
                waits_apart(pe)
                for k in range(TPC):
                    mm = pe.transpose(back_ps[u][:, k * D:(k + 1) * D], run[u][:, k * P:(k + 1) * P], b.ident[0:D, 0:D])
                mm.then_inc(turned_back, 1)

            chunk_loop(pe, C, body)

        @block.vector
        def _(dve):
            def body(c, u, pair):
                if not there(c, C):
                    return
                dve.wait_ge(x_turned, c + 1)
                dve.wait_ge(inside_ready, c + 1)
                need(dve, turned_back, c - 1)
                need(dve, run_done, c)
                dve.tensor_tensor_scan(run[u][:, :], inside[u][:, :], x_ps[u][0:D, :],
                                       0.0 if isinstance(c, int) and c == 0 else run[1 - u][:, CE - 1:CE],
                                       ALU.mult, ALU.add).then_inc(run_done, 1)

            chunk_loop(dve, C, body)


INPUTS = ["x", "src", "dst", "edge_attr_16", "edge_attr_8", "node_vec1", "L0_gnn_W_msg", "L0_gnn_b_msg",
          "L0_gnn_W_attn", "L0_gnn_b_attn", "L2_gnn_W_msg_tp", "L2_gnn_W_msg_lin", "L2_gnn_W_upd_tp",
          "L2_gnn_W_upd_lin", "L3_gnn_eps1", "L3_gnn_w1a", "L3_gnn_b1a", "L3_gnn_w1b", "L3_gnn_b1b",
          "L3_gnn_eps2", "L3_gnn_w2a", "L3_gnn_b2a", "L3_gnn_w2b", "L3_gnn_b2b"]
class Norm:

    def __init__(self, nc, sems, scratch, name, np_, nj):
        def sb(what, shape):
            return scratch.enter_context(nc.sbuf_tensor(name + what, shape, F32))

        def sem(what):
            return sems.enter(name + what)

        self.shape = [np_, nj, D]
        self.total, self.var, self.log_var, self.rstd = (sb(w, [np_, nj]) for w in ("total", "var", "log_var", "rstd"))
        self.centred, self.square = sb("centred", self.shape), sb("square", self.shape)
        self.total_done, self.centred_done, self.square_done, self.var_done = (
            sem("total_done"), sem("centred_done"), sem("square_done"), sem("var_done"))
        self.log_done, self.rstd_done, self.done = sem("log_done"), sem("rstd_done"), sem("done")

    def vector(self, dve, n, x, out):
        dve.tensor_reduce(self.total[:, :], x, AX.X, ALU.add).then_inc(self.total_done, 1)
        dve.wait_ge(self.total_done, n + 1)
        dve.scalar_tensor_tensor(self.centred[:, :, :], self.total[:, :].unsqueeze(2).broadcast_to(self.shape), -1.0 / D, x,
                                 ALU.mult, ALU.add).then_inc(self.centred_done, 1)
        dve.wait_ge(self.centred_done, n + 1)
        dve.tensor_tensor(self.square[:, :, :], self.centred[:, :, :], self.centred[:, :, :], ALU.mult).then_inc(self.square_done, 1)
        dve.wait_ge(self.square_done, n + 1)
        dve.tensor_reduce(self.var[:, :], self.square[:, :, :], AX.X, ALU.add).then_inc(self.var_done, 1)
        dve.wait_ge(self.rstd_done, n + 1)
        dve.tensor_tensor(out, self.centred[:, :, :], self.rstd[:, :].unsqueeze(2).broadcast_to(self.shape), ALU.mult).then_inc(self.done, 1)

    def scalar(self, act, n, eps_col):
        act.wait_ge(self.var_done, n + 1)
        act.activation(self.log_var[:, :], self.var[:, :], ACT.Ln, bias=eps_col, scale=1.0 / D).then_inc(self.log_done, 1)
        act.wait_ge(self.log_done, n + 1)
        act.activation(self.rstd[:, :], self.log_var[:, :], ACT.Exp, scale=-0.5).then_inc(self.rstd_done, 1)


def first_norms(nc, sems, sh, b, io):
    def sem(name):
        return sems.enter(name)

    J = 40
    I = sh.NJ // J
    NP = sh.NP
    with ExitStack() as scratch:
        agg = [scratch.enter_context(nc.sbuf_tensor(f"n1_agg{i}", [NP, J, 2 * D], F32)) for i in range(2)]
        y = scratch.enter_context(nc.sbuf_tensor("n1_y", [NP, J, D], F32))
        norm = Norm(nc, sems, scratch, "n1_", NP, J)
        agg_in = [sem(f"n1_agg_in{i}") for i in range(2)]
        summed, stored = sem("n1_summed"), sem("n1_stored")
        table = b.t_first.rearrange("(p j) c -> p j c", p=NP)
        out = b.t_x.rearrange("(p j) c -> p j c", p=NP)
        xn = b.xn[0:NP, :].rearrange("p (j c) -> p j c", c=D)
        block = scratch.enter_context(nc.Block())

        @block.sync
        def _(sp):
            def load(i, u):
                need(sp, norm.done, 2 * (i - 1))
                sp.dma_start(agg[u][:, :, :], table[:, bass.ds(i * J, J), :]).then_inc(agg_in[u], 16)

            for i in range(2):
                load(i, i)

            def body(i, u, pair):
                if there(i + 2, I):
                    load(i + 2, u)
                if there(i, I):
                    sp.wait_ge(norm.done, 2 * (i + 1))
                    sp.dma_start(out[:, bass.ds(i * J, J), :], xn[:, bass.ds(i * J, J), :]).then_inc(stored, 16)

            chunk_loop(sp, I, body)
            sp.wait_ge(stored, 16 * I)

        @block.vector
        def _(dve):
            def body(i, u, pair):
                if not there(i, I):
                    return
                x = xn[:, bass.ds(i * J, J), :]
                dve.wait_ge(agg_in[u], (pair + 1) * 16)
                dve.tensor_tensor(y[:, :, :], x, agg[u][:, :, 0:D], ALU.add).then_inc(summed, 1)
                dve.wait_ge(summed, 2 * i + 1)
                norm.vector(dve, 2 * i, y[:, :, :], y[:, :, :])
                dve.wait_ge(norm.done, 2 * i + 1)
                dve.tensor_tensor(y[:, :, :], y[:, :, :], agg[u][:, :, D:2 * D], ALU.add).then_inc(summed, 1)
                dve.wait_ge(summed, 2 * i + 2)
                norm.vector(dve, 2 * i + 1, y[:, :, :], x)

            chunk_loop(dve, I, body)

        @block.scalar
        def _(act):
            def body(i, u, pair):
                if there(i, I):
                    norm.scalar(act, 2 * i, b.eps_col[0:NP, :])
                    norm.scalar(act, 2 * i + 1, b.eps_col[0:NP, :])

            chunk_loop(act, I, body)


def update_nodes(nc, sems, sh, b, io):
    def sem(name):
        return sems.enter(name)

    J = 16
    I = sh.NJ // J
    NP = sh.NP
    GROUPS = J // 2
    with ExitStack() as scratch:
        def sb(name, shape):
            return scratch.enter_context(nc.sbuf_tensor(name, shape, F32))

        def ps(name):
            return scratch.enter_context(nc.psum_tensor(name, [P, 512], F32))

        parts = [sb(f"n2_parts{i}", [NP, TPC, J * D]) for i in range(2)]
        pairs, agg = sb("n2_pairs", [NP, 2, J * D]), sb("n2_agg", [NP, J, D])
        z = [sb(f"n2_z{i}", [NP, J, D, D]) for i in range(2)]
        zt = [sb(f"n2_zt{i}", [P, 4, NP]) for i in range(2)]
        act_u = [sb(f"n2_act{i}", [NP, J * D]) for i in range(2)]
        act_ut = [sb(f"n2_act_t{i}", [P, 2, NP]) for i in range(2)]
        y = sb("n2_y", [NP, J, D])
        norm = Norm(nc, sems, scratch, "n2_", NP, J)
        z_ps = [ps(f"n2_zps{i}") for i in range(2)]
        u_ps = [ps(f"n2_ups{i}") for i in range(2)]
        t_ps, v_ps = ps("n2_tps"), ps("n2_vps")
        parts_in = [sem(f"n2_parts_in{i}") for i in range(2)]
        pairs_done, agg_done, z_done = sem("n2_pairs_done"), sem("n2_agg_done"), sem("n2_z_done")
        z_turned, zt_ready, group_done = sem("n2_z_turned"), sem("n2_zt_ready"), sem("n2_group_done")
        act_done, act_turned, act_t_ready, v_done = sem("n2_act_done"), sem("n2_act_turned"), sem("n2_act_t_ready"), sem("n2_v_done")
        once, twice, stored = sem("n2_once"), sem("n2_twice"), sem("n2_stored")
        tables = [t[0:sh.N, :].rearrange("(p j) c -> p (j c)", p=NP) for t in b.t_adds]
        out = b.t_x.rearrange("(p j) c -> p j c", p=NP)
        xn = b.xn[0:NP, :].rearrange("p (j c) -> p j c", c=D)
        block = scratch.enter_context(nc.Block())

        @block.sync
        def _(sp):
            def load(i, u):
                need(sp, pairs_done, i - 1)
                for k in range(TPC):
                    sp.dma_start(parts[u][:, k, :], tables[k][:, bass.ds(i * (J * D), J * D)]).then_inc(parts_in[u], 16)

            for i in range(2):
                load(i, i)

            def body(i, u, pair):
                if there(i + 2, I):
                    load(i + 2, u)
                if there(i - 1, I):
                    sp.wait_ge(norm.done, i)
                    sp.dma_start(out[:, bass.ds((i - 1) * J, J), :], xn[:, bass.ds((i - 1) * J, J), :]).then_inc(stored, 16)

            chunk_loop(sp, I, body)
            sp.wait_ge(stored, 16 * I)

        @block.vector
        def _(dve):
            def product(i, u, pair):
                dve.wait_ge(parts_in[u], (pair + 1) * (16 * TPC))
                dve.tensor_tensor(pairs[:, :, :], parts[u][:, 0:2, :], parts[u][:, 2:4, :], ALU.add).then_inc(pairs_done, 1)
                dve.wait_ge(pairs_done, i + 1)
                dve.tensor_tensor(agg[:, :, :].rearrange("p j c -> p (j c)"), pairs[:, 0, :], pairs[:, 1, :], ALU.add).then_inc(agg_done, 1)
                dve.wait_ge(agg_done, i + 1)
                need(dve, z_turned, GROUPS * (i - 1))
                dve.tensor_tensor(z[u][:, :, :, :], xn[:, bass.ds(i * J, J), :].unsqueeze(3).broadcast_to([NP, J, D, D]),
                                  agg[:, :, :].unsqueeze(2).broadcast_to([NP, J, D, D]), ALU.mult).then_inc(z_done, 1)

            def update(i, u):
                x = xn[:, bass.ds(i * J, J), :]
                dve.wait_ge(v_done, i + 1)
                dve.scalar_tensor_tensor(y[:, :, :], v_ps[0:NP, 0:J * D].rearrange("p (j c) -> p j c", c=D), float(D) ** -0.5, x,
                                         ALU.mult, ALU.add).then_inc(once, 1)
                dve.wait_ge(once, i + 1)
                dve.tensor_tensor(y[:, :, :], y[:, :, :], x, ALU.add).then_inc(twice, 1)
                dve.wait_ge(twice, i + 1)
                norm.vector(dve, i, y[:, :, :], x)

            def body(i, u, pair):
                if there(i, I):
                    product(i, u, pair)
                if there(i - 1, I):
                    update(i - 1, 1 - u)

            chunk_loop(dve, I, body)

        @block.tensor
        def _(pe):
            def body(i, u, pair):
                if there(i, I):
                    pe.wait_ge(z_done, i + 1)
                    for g in range(GROUPS + 1):
                        if g < GROUPS:
                            need(pe, zt_ready, GROUPS * i + g - 1)
                            for k in range(4):
                                half = z[u][:, 2 * g + k // 2, (k % 2) * 8:(k % 2) * 8 + 8, :].rearrange("p i h -> p (i h)")
                                mm = pe.transpose(z_ps[g % 2][:, k * NP:(k + 1) * NP], half, b.ident[0:NP, 0:NP])
                            mm.then_inc(z_turned, 1)
                        if g > 0:
                            o = g - 1
                            pe.wait_ge(zt_ready, GROUPS * i + g)
                            if o == 0:
                                need(pe, act_done, i - 1)
                            for k in range(4):
                                node = 2 * o + k // 2
                                mm = pe.matmul(u_ps[u][0:NP, node * D:(node + 1) * D], zt[o % 2][:, k, :], b.w_up[:, k % 2, :],
                                               start=(k % 2 == 0), stop=(k % 2 == 1))
                            mm.then_inc(group_done, 1)
                if there(i - 1, I):
                    w = 1 - u
                    pe.wait_ge(act_done, i)
                    need(pe, act_t_ready, i - 1)
                    for k in range(2):
                        mm = pe.transpose(t_ps[:, k * NP:(k + 1) * NP], act_u[w][:, k * P:(k + 1) * P], b.ident[0:NP, 0:NP])
                    mm.then_inc(act_turned, 1)
                    pe.wait_ge(act_t_ready, i)
                    need(pe, once, i - 1)
                    for k in range(2):
                        mm = pe.matmul(v_ps[0:NP, k * P:(k + 1) * P], act_ut[w][:, k, :], b.bd_upd[:, :], start=True, stop=True)
                    mm.then_inc(v_done, 1)

            chunk_loop(pe, I, body)

        @block.scalar
        def _(act):
            def body(i, u, pair):
                if there(i - 1, I):
                    w = 1 - u
                    act.wait_ge(group_done, GROUPS * i)
                    need(act, act_turned, i - 2)
                    act.activation(act_u[w][:, :], u_ps[w][0:NP, 0:J * D], ACT.Silu, scale=1.0 / D).then_inc(act_done, 1)
                if there(i, I):
                    for g in range(GROUPS):
                        act.wait_ge(z_turned, GROUPS * i + g + 1)
                        need(act, group_done, GROUPS * i + g - 1)
                        act.activation(zt[g % 2][:, :, :], z_ps[g % 2][:, 0:4 * NP].rearrange("p (k n) -> p k n", k=4), ACT.Copy).then_inc(zt_ready, 1)
                if there(i - 1, I):
                    w = 1 - u
                    act.wait_ge(act_turned, i)
                    need(act, v_done, i - 2)
                    act.activation(act_ut[w][:, :, :], t_ps[:, 0:2 * NP].rearrange("p (k n) -> p k n", k=2), ACT.Copy).then_inc(act_t_ready, 1)
                    norm.scalar(act, i - 1, b.eps_col[0:NP, :])

            chunk_loop(act, I, body)


def graph_mlp(nc, sems, sh, b, name, seg_table, x_in, eps1, wa, ba, wb, bb, final):
    def sem(what):
        return sems.enter(name + what)

    J = 40
    I = sh.NJ // J
    NP = sh.NP
    B = J * D // P
    W0 = 4 * NP
    with ExitStack() as scratch:
        def sb(what, shape):
            return scratch.enter_context(nc.sbuf_tensor(name + what, shape, F32))

        def ps(what):
            return scratch.enter_context(nc.psum_tensor(name + what, [P, 1024], F32))

        seg = [sb(f"seg{i}", [NP, J, D]) for i in range(2)]
        h_in = sb("h_in", [NP, J, D])
        ht, hidden_t = sb("ht", [P, B * NP]), sb("hidden_t", [P, B * NP])
        y = sb("y", [NP, J, D])
        t_ps, hid_ps, o_ps = ps("t_ps"), ps("hid_ps"), ps("o_ps")
        seg_in = [sem(f"seg_in{i}") for i in range(2)]
        h_done, h_turned, ht_ready, hid_done, hidden_ready, o_done = (
            sem("h_done"), sem("h_turned"), sem("ht_ready"), sem("hid_done"), sem("hidden_ready"), sem("o_done"))
        biased, done, stored = sem("biased"), sem("done"), [sem(f"stored{i}") for i in range(2)]
        if final:
            norm = Norm(nc, sems, scratch, name + "norm_", NP, J)
            top, prob, den, log_den = sb("top", [NP, J]), sb("prob", [NP, J, D]), sb("den", [NP, J]), sb("log_den", [NP, J])
            result = [sb(f"result{i}", [NP, J, D]) for i in range(2)]
            top_done, less_done, prob_done, den_done, log_den_done, lsm_done, res_done = (
                sem("top_done"), sem("less_done"), sem("prob_done"), sem("den_done"), sem("log_den_done"), sem("lsm_done"), sem("res_done"))
            finished = norm.done
        else:
            finished = done
        table = seg_table.rearrange("(p j) c -> p j c", p=NP)
        out = (b.out if final else b.t_h).rearrange("(p j) c -> p j c", p=NP)
        nodes = x_in[0:NP, :].rearrange("p (j c) -> p j c", c=D)
        xn = b.xn[0:NP, :].rearrange("p (j c) -> p j c", c=D)
        hn = b.hn[0:NP, :].rearrange("p (j c) -> p j c", c=D)
        block = scratch.enter_context(nc.Block())

        def halves(t, rows=P):
            return ((t[0:rows, 0:W0], slice(0, W0)), (t[0:rows, 512:512 + NP], slice(W0, B * NP)))

        def at(k):
            return k * NP if k < 4 else 512

        @block.sync
        def _(sp):
            def load(i, u):
                need(sp, h_done, i - 1)
                sp.dma_start(seg[u][:, :, :], table[:, bass.ds(i * J, J), :]).then_inc(seg_in[u], 16)

            for i in range(2):
                load(i, i)

            def body(i, u, pair):
                if there(i + 2, I):
                    load(i + 2, u)
                if there(i, I):
                    sp.wait_ge(finished, i + 1)
                    sp.dma_start(out[:, bass.ds(i * J, J), :],
                                 result[u][:, :, :] if final else hn[:, bass.ds(i * J, J), :]).then_inc(stored[u], 16)

            chunk_loop(sp, I, body)
            for u in range(2):
                sp.wait_ge(stored[u], 16 * (I // 2))

        @block.vector
        def _(dve):
            def start(i, u, pair):
                dve.wait_ge(seg_in[u], (pair + 1) * 16)
                need(dve, h_turned, i)
                dve.scalar_tensor_tensor(h_in[:, :, :], nodes[:, bass.ds(i * J, J), :], eps1[0:NP, 0:1], seg[u][:, :, :],
                                         ALU.mult, ALU.add).then_inc(h_done, 1)

            def end(i, u, pair):
                dve.wait_ge(o_done, i + 1)
                need(dve, finished, i)
                dve.tensor_tensor(y[:, :, :], o_ps[0:NP, 0:J * D].rearrange("p (j c) -> p j c", c=D),
                                  bb[0:NP, :].unsqueeze(1).broadcast_to([NP, J, D]), ALU.add).then_inc(biased, 1)
                dve.wait_ge(biased, i + 1)
                if not final:
                    dve.tensor_scalar(hn[:, bass.ds(i * J, J), :], y[:, :, :], 0.0, None, ALU.max).then_inc(done, 1)
                    return
                dve.tensor_reduce(top[:, :], y[:, :, :], AX.X, ALU.max).then_inc(top_done, 1)
                dve.wait_ge(top_done, i + 1)
                dve.tensor_tensor(y[:, :, :], y[:, :, :], top[:, :].unsqueeze(2).broadcast_to([NP, J, D]), ALU.subtract).then_inc(less_done, 1)
                dve.wait_ge(prob_done, i + 1)
                dve.tensor_reduce(den[:, :], prob[:, :, :], AX.X, ALU.add).then_inc(den_done, 1)
                dve.wait_ge(log_den_done, i + 1)
                dve.tensor_tensor(y[:, :, :], y[:, :, :], log_den[:, :].unsqueeze(2).broadcast_to([NP, J, D]), ALU.subtract).then_inc(lsm_done, 1)
                dve.wait_ge(lsm_done, i + 1)
                dve.tensor_tensor(y[:, :, :], y[:, :, :], xn[:, bass.ds(i * J, J), :], ALU.add).then_inc(res_done, 1)
                dve.wait_ge(res_done, i + 1)
                need(dve, stored[u], pair * 16)
                norm.vector(dve, i, y[:, :, :], result[u][:, :, :])

            def body(i, u, pair):
                if there(i, I):
                    start(i, u, pair)
                if there(i - 1, I):
                    end(i - 1, 1 - u, pair if u else pair - 1)

            chunk_loop(dve, I, body)

        @block.tensor
        def _(pe):
            def body(i, u, pair):
                if not there(i, I):
                    return
                pe.wait_ge(h_done, i + 1)
                need(pe, ht_ready, 2 * i)
                for k in range(B):
                    mm = pe.transpose(t_ps[:, at(k):at(k) + NP], h_in[:, 8 * k:8 * k + 8, :].rearrange("p j c -> p (j c)"), b.ident[0:NP, 0:NP])
                mm.then_inc(h_turned, 1)
                need(pe, hidden_ready, 2 * i)
                for k, (part, cols) in enumerate(halves(hid_ps)):
                    pe.wait_ge(ht_ready, 2 * i + k + 1)
                    mm = pe.matmul(part, wa[:, :], ht[:, cols], start=True, stop=True)
                    mm.then_inc(hid_done, 1)
                pe.wait_ge(hidden_ready, 2 * (i + 1))
                need(pe, biased, i)
                for k in range(B):
                    mm = pe.matmul(o_ps[0:NP, k * P:(k + 1) * P], hidden_t[:, k * NP:(k + 1) * NP], wb[:, :], start=True, stop=True)
                mm.then_inc(o_done, 1)

            chunk_loop(pe, I, body)

        @block.scalar
        def _(act):
            def body(i, u, pair):
                if there(i, I):
                    act.wait_ge(h_turned, i + 1)
                    need(act, hid_done, 2 * i)
                    for part, cols in halves(t_ps):
                        act.activation(ht[:, cols], part, ACT.Copy).then_inc(ht_ready, 1)
                    need(act, o_done, i)
                    for k, (part, cols) in enumerate(halves(hid_ps)):
                        act.wait_ge(hid_done, 2 * i + k + 1)
                        act.activation(hidden_t[:, cols], part, ACT.Relu, bias=ba[:, 0:1]).then_inc(hidden_ready, 1)
                if final and there(i - 1, I):
                    act.wait_ge(less_done, i)
                    act.activation(prob[:, :, :], y[:, :, :], ACT.Exp).then_inc(prob_done, 1)
                    act.wait_ge(den_done, i)
                    act.activation(log_den[:, :], den[:, :], ACT.Ln).then_inc(log_den_done, 1)
                    norm.scalar(act, i - 1, b.eps_col[0:NP, :])

            chunk_loop(act, I, body)


class Buffers:
    pass


def build(nc, io, out):
    N, E = io["x"].shape[0], io["src"].shape[0]
    sh = Shapes(N, E)
    b = Buffers()
    with ExitStack() as ctx:
        def sb(name, shape, dt=F32):
            return ctx.enter_context(nc.sbuf_tensor(name, shape, dt))

        b.out = out
        b.t_first = nc.dram_tensor("t_first", [N, 2 * D], F32, kind="Internal").ap()
        b.t_x = nc.dram_tensor("t_x", [N, D], F32, kind="Internal").ap()
        b.t_x3 = b.t_x
        b.t_h = nc.dram_tensor("t_h", [N, D], F32, kind="Internal").ap()
        b.t_adds = [nc.dram_tensor(f"t_add{k}", [N + 1 + P, D], F32, kind="Internal").ap() for k in range(TPC)]
        b.t_seg1 = nc.dram_tensor("t_seg1", [N, D], F32, kind="Internal").ap()
        b.t_seg2 = nc.dram_tensor("t_seg2", [N, D], F32, kind="Internal").ap()

        b.ident, b.lower, b.sel = sb("ident", [P, P]), sb("lower", [P, P]), sb("sel", [P, D])
        b.eps_col, b.dummy, b.dummy_i = sb("eps_col", [P, 1]), sb("dummy_row", [P, 1]), sb("dummy_row_i", [P, 1], I32)
        b.w_att, b.w_msg, b.w_h, b.w_start = sb("w_att", [UW, CH]), sb("w_msg", [UW, CH]), sb("w_h", [UW, CH]), sb("w_start", [UW, P])
        b.w_tp, b.w_up = sb("w_tp", [P, D]), sb("w_up", [P, 2, D])
        b.bd_lin, b.bd_upd, b.bd1a, b.bd1b, b.bd2a, b.bd2b = (sb(w, [P, P]) for w in ("bd_lin", "bd_upd", "bd1a", "bd1b", "bd2a", "bd2b"))
        b.b1a, b.b2a, b.b1b, b.b2b = sb("b1a", [P, 1]), sb("b2a", [P, 1]), sb("b1b", [P, D]), sb("b2b", [P, D])
        b.eps1, b.eps2 = sb("eps1", [P, 1]), sb("eps2", [P, 1])
        cols = sh.tiles + 2 * TPC
        b.gsrc, b.gdst, b.scat = (sb(w, [P, cols], I32) for w in ("gsrc", "gdst", "scat"))
        b.start, b.srcf = sb("start", [P, cols]), sb("srcf", [P, cols])
        b.xn = sb("xn", [P, sh.NJ * D])
        with ExitStack() as edges:
            b.ea8 = edges.enter_context(nc.sbuf_tensor("ea8", [P, sh.tiles, DE], F32))
            with ExitStack() as first:
                b.zw = 1600
                b.zeros = first.enter_context(nc.sbuf_tensor("zeros", [P, b.zw], F32))
                b.ea16 = first.enter_context(nc.sbuf_tensor("ea16", [P, sh.tiles, D], F32))
                b.u = [first.enter_context(nc.sbuf_tensor(f"u{i}", [P, TPC, UW], F32)) for i in range(2)]
                b.e2 = [first.enter_context(nc.sbuf_tensor(f"e2_{i}", [P, 2, CE + 1], F32)) for i in range(2)]
                with Semaphores(nc) as sems:
                    constants_and_indices(nc, sems, sh, b, io)
                with Semaphores(nc) as sems:
                    attention_layer(nc, sems, sh, b, io)
            with Semaphores(nc) as sems:
                first_norms(nc, sems, sh, b, io)
            with Semaphores(nc) as sems:
                message_layer(nc, sems, sh, b, io)
        with Semaphores(nc) as sems:
            update_nodes(nc, sems, sh, b, io)
        b.hn = sb("hn", [P, sh.NJ * D])
        with Semaphores(nc) as sems:
            neighbour_sums(nc, sems, sh, b, "s1_", b.t_x, b.t_seg1)
        with Semaphores(nc) as sems:
            graph_mlp(nc, sems, sh, b, "g1_", b.t_seg1, b.xn, b.eps1, b.bd1a, b.b1a, b.bd1b, b.b1b, False)
        with Semaphores(nc) as sems:
            neighbour_sums(nc, sems, sh, b, "s2_", b.t_h, b.t_seg2)
        with Semaphores(nc) as sems:
            graph_mlp(nc, sems, sh, b, "g2_", b.t_seg2, b.hn, b.eps2, b.bd2a, b.b2a, b.bd2b, b.b2b, True)


def kernel(**inputs):
    import numpy as np
    import concourse.bacc as bacc
    from concourse.bass_utils import run_bass_kernel_spmd

    nc = bacc.Bacc("TRN2", target_bir_lowering=False, num_devices=1)
    arrays, io = {}, {}
    for name in INPUTS:
        a = np.ascontiguousarray(inputs[name])
        if a.ndim == 0:
            a = a.reshape(1)
        arrays[f"in_{name}"] = a
        io[name] = nc.dram_tensor(f"in_{name}", a.shape, mybir.dt.from_np(a.dtype), kind="ExternalInput").ap()
    out = nc.dram_tensor("out", list(inputs["x"].shape), F32, kind="ExternalOutput").ap()
    build(nc, io, out)
    r = run_bass_kernel_spmd(nc, [arrays], core_ids=[0])
    return r.results[0]["out"]
```

```python
from contextlib import ExitStack

import concourse.bass as bass
from concourse import mybir

F32 = mybir.dt.float32
BF16 = mybir.dt.bfloat16
I32 = mybir.dt.int32
U32 = mybir.dt.uint32
ALU = mybir.AluOpType
ACT = mybir.ActivationFunctionType
AX = mybir.AxisListType

P = 128
D = 16
DE = 8
CH = D * D
TPC = 4
CE = TPC * P
RESET = -(2.0 ** 100)
PARTS = ((0, 0), (0, 1), (0, 2), (1, 0), (1, 1), (2, 0))
ROWS = len(PARTS) * D
BIAS = ROWS
START_ROW = ROWS + 3
EPS = 1e-5


def there(index, count):
    return not isinstance(index, int) or 0 <= index < count


def need(engine, semaphore, value):
    if not isinstance(value, int) or value > 0:
        engine.wait_ge(semaphore, value)


class Semaphores:

    def __init__(self, nc):
        self.nc, self.handles = nc, []

    def __enter__(self):
        return self

    def enter(self, name):
        self.handles.append(self.nc.alloc_semaphore(name=name))
        return self.handles[-1]

    def __exit__(self, kind, value, trace):
        if kind is None:
            self.nc.clear_and_free_semaphores(self.handles)
            self.nc.all_engine_barrier()


class Shapes:
    def __init__(self, n, e):
        self.N, self.E = n, e
        self.chunks = -(-e // CE)
        assert self.chunks % 2 == 0 and self.chunks >= 6
        self.tiles = self.chunks * TPC
        self.full = e // P
        self.rest = e - self.full * P
        self.NP = 125
        self.NJ = n // self.NP
        assert self.NP * self.NJ == n and self.NJ % 32 == 0
        self.G = self.tiles // TPC
        self.none = 1 << 21
        self.far = 200000
        assert self.far > n


def waits_apart(engine):
    engine.nop(nofuse=True)


def chunk_loop(engine, chunks, body):
    for c in range(4):
        body(c, c % 2, c // 2)
    with engine.Fori(2, chunks // 2 - 1) as pair:
        for u in (0, 1):
            body(pair * 2 + u, u, pair)
    for c in range(chunks - 2, chunks + 2):
        body(c, c % 2, c // 2)


def split(engine, parts, rest, x, done, at):
    engine.tensor_copy(parts[0], x).then_inc(done, 1)
    engine.wait_ge(done, at + 1)
    engine.tensor_tensor(rest, x, parts[0], ALU.subtract).then_inc(done, 1)
    engine.wait_ge(done, at + 2)
    engine.tensor_copy(parts[1], rest).then_inc(done, 1)
    engine.wait_ge(done, at + 3)
    engine.tensor_tensor(parts[2], rest, parts[1], ALU.subtract).then_inc(done, 1)


def constants_and_indices(nc, sems, sh, b, io):
    def sem(name):
        return sems.enter(name)

    G, N = sh.G, sh.N
    zeroed, made, sel_done = sem("zeroed"), sem("made"), sem("sel_done")
    weights_in, edges_in, idx_in = sem("weights_in"), sem("edges_in"), sem("idx_in")
    rows_done, turned, columns_done = sem("rows_done"), sem("turned"), sem("columns_done")
    weights_split, weights_picked, masks_done, edges_split, edges_doubled = (
        sem("weights_split"), sem("weights_picked"), sem("masks_done"), sem("edges_split"), sem("edges_doubled"))
    thrice_done, spread_done = sem("thrice_done"), sem("spread_done")
    with ExitStack() as scratch:
        def sb(name, shape, dt=F32):
            return scratch.enter_context(nc.sbuf_tensor(name, shape, dt))

        dst_rows, src_rows = sb("dst_rows", [G, TPC, P + 2], I32), sb("src_rows", [G, TPC, P], I32)
        dst_f, end_f = sb("dst_f", [G, TPC, P + 2]), sb("end_f", [G, TPC, P])
        rows_f = sb("rows_f", [G, 5, TPC, P])
        ea16, weights = sb("ea16", [P, sh.tiles, D]), sb("weights", [P, 3, CH])
        parts = [sb(f"weights_part{i}", [P, 3, CH], BF16) for i in range(3)]
        picked = [sb(f"weights_picked{i}", [P, 3, CH]) for i in range(2)]
        blocks, mask = sb("blocks", [P, 8]), sb("mask", [P, 3])
        h_rows, thrice = sb("h_rows", [D, CH]), sb("thrice", [D, 3, D])
        turned_ps = [scratch.enter_context(nc.psum_tensor(f"turned_ps{i}", [P, 512], F32)) for i in range(5)]
        spread_ps = scratch.enter_context(nc.psum_tensor("spread_ps", [P, 512], F32))
        START, SCAT, GDST, GSRC, SRC = range(5)
        src, dst = io["src"], io["dst"]
        last = sh.full - 3 * G

        block = scratch.enter_context(nc.Block())

        @block.gpsimd
        def _(pool):
            pool.memset(b.ident[:, :], 0.0).then_inc(zeroed, 1)
            pool.memset(dst_rows[:, :, :], sh.far).then_inc(zeroed, 1)
            pool.memset(src_rows[:, :, :], sh.N).then_inc(zeroed, 1)
            pool.memset(weights[:, :, :], 0.0).then_inc(zeroed, 1)
            pool.memset(ea16[:, sh.full:sh.tiles, :], 0.0).then_inc(zeroed, 1)
            pool.memset(h_rows[:, :], 1.0).then_inc(made, 1)
            pool.memset(b.w_start[:, :], 0.0).then_inc(made, 1)
            pool.memset(b.lower[:, :], 1.0).then_inc(made, 1)
            pool.memset(b.eps_col[:, :], EPS).then_inc(made, 1)
            pool.memset(b.zeros[:, :], 0.0).then_inc(made, 1)
            for a in (b.gsrc, b.gdst, b.scat):
                pool.memset(a[:, :], 0).then_inc(made, 1)
            for a in (b.start, b.srcf):
                pool.memset(a[:, :], 0.0).then_inc(made, 1)
            pool.iota(b.dummy_i[:, :], pattern=[[0, 1]], base=N + 1, channel_multiplier=1).then_inc(made, 1)
            pool.wait_ge(made, 11)
            pool.wait_ge(zeroed, 1)
            pool.affine_select(out=b.ident[:, :], in_=b.ident[:, :], compare_op=ALU.not_equal, fill=1.0,
                               base=0, pattern=[[-1, P]], channel_multiplier=1).then_inc(sel_done, 1)
            pool.affine_select(out=h_rows[:, :], in_=h_rows[:, :], compare_op=ALU.is_ge, fill=0.0,
                               base=0, pattern=[[1, CH]], channel_multiplier=-D).then_inc(sel_done, 1)
            pool.wait_ge(sel_done, 2)
            pool.affine_select(out=h_rows[:, :], in_=h_rows[:, :], compare_op=ALU.is_ge, fill=0.0,
                               base=D - 1, pattern=[[-1, CH]], channel_multiplier=D).then_inc(sel_done, 1)
            pool.affine_select(out=b.w_start[:, :], in_=b.w_start[:, :], compare_op=ALU.not_equal, fill=RESET,
                               base=-START_ROW, pattern=[[0, P]], channel_multiplier=1).then_inc(sel_done, 1)
            pool.affine_select(out=b.lower[:, :], in_=b.lower[:, :], compare_op=ALU.is_gt, fill=0.0,
                               base=0, pattern=[[-1, P]], channel_multiplier=1).then_inc(sel_done, 1)
            pool.memset(b.edges[:, :, BIAS:BIAS + 3], 1.0).then_inc(edges_doubled, 1)
            pool.memset(b.edges[:, :, START_ROW + 1:P], 0.0).then_inc(edges_doubled, 1)

        @block.sync
        def _(sp):
            sp.wait_ge(zeroed, 3)
            for g in range(TPC):
                n = G if g < 3 else last
                r0 = 0 if g else 1
                at = g * G * P
                sp.dma_start(dst_rows[r0:n, g, :], bass.AP(dst.tensor, at + r0 * P - 1, [[P, n - r0], [1, P + 2]])).then_inc(idx_in, 16)
                sp.dma_start(src_rows[0:n, g, :], src[at:at + n * P].rearrange("(r e) -> r e", e=P)).then_inc(idx_in, 16)
            sp.dma_start(dst_rows[0:1, 0, 1:P + 2], dst[0:P + 1].rearrange("(a e) -> a e", a=1)).then_inc(idx_in, 16)
            sp.dma_start(dst_rows[last:last + 1, 3, 0:sh.rest + 1], dst[sh.full * P - 1:sh.E].rearrange("(a e) -> a e", a=1)).then_inc(idx_in, 16)
            sp.dma_start(src_rows[last:last + 1, 3, 0:sh.rest], src[sh.full * P:sh.E].rearrange("(a e) -> a e", a=1)).then_inc(idx_in, 16)

        @block.scalar
        def _(act):
            act.preload_act_table_set("natural_log_exp_and_others")
            act.wait_ge(zeroed, 5)
            a = io["edge_attr_16"]
            act.dma_start(ea16[:, 0:sh.full, :], a[0:sh.full * P, :].rearrange("(t p) c -> p t c", p=P)).then_inc(edges_in, 16)
            act.dma_start(ea16[0:sh.rest, sh.full, :], a[sh.full * P:sh.E, :]).then_inc(edges_in, 16)
            names = ("L0_gnn_W_attn", "L0_gnn_W_msg", "L2_gnn_W_upd_tp")
            for k, name in enumerate(names):
                w = io[name] if k < 2 else io[name].rearrange("i h k -> i (h k)")
                for n in range(len(PARTS)):
                    act.dma_start(weights[n * D:(n + 1) * D, k, :], w).then_inc(weights_in, 16)
            for k, name in enumerate(("L0_gnn_b_attn", "L0_gnn_b_msg")):
                act.dma_start(weights[BIAS:BIAS + 3, k, :], bass.AP(io[name].tensor, 0, [[0, 3], [1, CH]])).then_inc(weights_in, 16)
            for at, (x_part, step) in enumerate(((0, 1), (0, 1), (1, 3))):
                act.wait_ge(edges_split, step)
                to, of = ((1, 0), (2, 0), (4, 3))[at]
                act.activation(b.edges[:, :, to * D:(to + 1) * D], b.edges[:, :, of * D:(of + 1) * D], ACT.Copy).then_inc(edges_doubled, 1)

        @block.vector
        def _(dve):
            dve.wait_ge(idx_in, 16 * 11)
            dve.tensor_copy(dst_f[:, :, :], dst_rows[:, :, :]).then_inc(rows_done, 1)
            dve.tensor_copy(rows_f[:, SRC, :, :], src_rows[:, :, :]).then_inc(rows_done, 1)
            dve.wait_ge(rows_done, 2)
            here = dst_f[:, :, 1:P + 1]
            dve.tensor_tensor(rows_f[:, START, :, :], here, dst_f[:, :, 0:P], ALU.not_equal).then_inc(rows_done, 1)
            dve.tensor_tensor(end_f[:, :, :], here, dst_f[:, :, 2:P + 2], ALU.is_equal).then_inc(rows_done, 1)
            dve.tensor_scalar(rows_f[:, GDST, :, :], here, float(N - 1), None, ALU.min).then_inc(rows_done, 1)
            dve.tensor_scalar(rows_f[:, GSRC, :, :], rows_f[:, SRC, :, :], float(N - 1), None, ALU.min).then_inc(rows_done, 1)
            dve.wait_ge(rows_done, 4)
            dve.scalar_tensor_tensor(rows_f[:, SCAT, :, :], end_f[:, :, :], float(sh.none), here, ALU.mult, ALU.add).then_inc(rows_done, 1)
            dve.wait_ge(made, 11)
            dve.wait_ge(turned, 5)
            for k, out in ((START, b.start), (SCAT, b.scat), (GDST, b.gdst), (GSRC, b.gsrc), (SRC, b.srcf)):
                dve.tensor_copy(out[:, 0:sh.tiles], turned_ps[k][:, 0:sh.tiles]).then_inc(columns_done, 1)
            dve.tensor_copy(b.dummy[:, :], b.dummy_i[:, :]).then_inc(columns_done, 1)
            dve.wait_ge(edges_in, 32)
            split(dve, [b.edges[:, :, n * D:(n + 1) * D] for n in (0, 3, 5)], ea16[:, :, :], ea16[:, :, :], edges_split, 0)
            dve.wait_ge(columns_done, 1)
            dve.tensor_copy(b.edges[:, :, START_ROW], b.start[:, 0:sh.tiles]).then_inc(columns_done, 1)
            dve.wait_ge(sel_done, 5)
            dve.tensor_copy(thrice[:, :, :], b.ident[0:D, 0:D].unsqueeze(1).broadcast_to([D, 3, D])).then_inc(thrice_done, 1)
            dve.tensor_copy(b.ident_b[:, :], b.ident[:, :]).then_inc(columns_done, 1)
            dve.tensor_reduce(b.sel[:, :], b.ident[:, :].rearrange("p (i o) -> p o i", o=D), AX.X, ALU.add).then_inc(columns_done, 1)
            dve.tensor_reduce(blocks[:, 0:6], b.ident[:, 0:ROWS].rearrange("p (n i) -> p n i", i=D), AX.X, ALU.add).then_inc(masks_done, 1)
            dve.wait_ge(masks_done, 1)
            dve.tensor_tensor(mask[:, 0:2], blocks[:, 0:2], blocks[:, 3:5], ALU.add).then_inc(masks_done, 1)
            dve.tensor_tensor(mask[:, 2:3], blocks[:, 2:3], b.ident[:, BIAS + 2:BIAS + 3], ALU.add).then_inc(masks_done, 1)
            dve.wait_ge(masks_done, 2)
            dve.tensor_tensor(mask[:, 0:2], mask[:, 0:2], b.ident[:, BIAS:BIAS + 2], ALU.add).then_inc(masks_done, 1)
            dve.wait_ge(masks_done, 4)
            dve.tensor_tensor(mask[:, 0:1], mask[:, 0:1], blocks[:, 5:6], ALU.add).then_inc(masks_done, 1)
            dve.wait_ge(weights_in, 16 * 20)
            split(dve, [p[:, :, :] for p in parts], weights[:, :, :], weights[:, :, :], weights_split, 0)
            dve.wait_ge(weights_split, 4)
            dve.wait_ge(masks_done, 5)
            dve.tensor_scalar(picked[0][:, :, :], parts[0][:, :, :], mask[:, 0:1], None, ALU.mult).then_inc(weights_picked, 1)
            for k in (1, 2):
                dve.wait_ge(weights_picked, k)
                dve.scalar_tensor_tensor(picked[k][:, :, :] if k == 1 else b.w_split[:, :, :], parts[k][:, :, :], mask[:, k:k + 1],
                                         picked[k - 1][:, :, :], ALU.mult, ALU.add).then_inc(weights_picked, 1)
            dve.tensor_tensor(b.w_attr[:, 0:D], b.ident[:, 0:D], b.ident[:, 3 * D:4 * D], ALU.add).then_inc(masks_done, 1)
            dve.tensor_copy(b.w_attr[:, D:D + 1], b.ident[:, BIAS:BIAS + 1]).then_inc(masks_done, 1)
            dve.wait_ge(masks_done, 6)
            dve.tensor_tensor(b.w_attr[:, 0:D], b.w_attr[:, 0:D], b.ident[:, 5 * D:6 * D], ALU.add).then_inc(masks_done, 1)
            for u in range(2):
                dve.memset(b.e2[u][:, :, 0:1], 0.0).then_inc(columns_done, 1)
            dve.wait_ge(spread_done, 1)
            dve.tensor_copy(b.w_h[:, :], spread_ps[0:3 * D, 0:CH]).then_inc(columns_done, 1)

        @block.tensor
        def _(pe):
            pe.wait_ge(sel_done, 1)
            pe.wait_ge(rows_done, 7)
            for k in range(5):
                for g in range(TPC):
                    mm = pe.transpose(turned_ps[k][:, g * G:(g + 1) * G], rows_f[:, k, g, :], b.ident[0:G, 0:G])
                mm.then_inc(turned, 1)
            pe.wait_ge(sel_done, 3)
            pe.wait_ge(thrice_done, 1)
            pe.matmul(spread_ps[0:3 * D, 0:CH], thrice[:, :, :].rearrange("i n o -> i (n o)"), h_rows[:, :],
                      start=True, stop=True).then_inc(spread_done, 1)


def attention_layer(nc, sems, sh, b, io):
    def sem(name):
        return sems.enter(name)

    C, S = sh.chunks, 2 * sh.chunks
    with ExitStack() as scratch:
        def sb(name, shape, dt=F32):
            return scratch.enter_context(nc.sbuf_tensor(name, shape, dt))

        def ps(name):
            return scratch.enter_context(nc.psum_tensor(name, [P, 512], F32))

        gather_idx = [sb(f"a_gather_idx{i}", [P, TPC], U32) for i in range(2)]
        scatter_idx = [sb(f"a_scatter_idx{i}", [P, TPC], U32) for i in range(2)]
        x_src = [sb(f"a_x_src{i}", [P, TPC, D]) for i in range(2)]
        x_parts = [sb(f"a_x_parts{i}", [P, TPC, 3, D], BF16) for i in range(2)]
        x_rest = sb("a_x_rest", [P, TPC, D])
        ut = [sb(f"a_ut{i}", [P, CE], BF16) for i in range(2)]
        vt = [sb(f"a_vt{i}", [3 * D, CE], BF16) for i in range(2)]
        inside = sb("a_inside", [D + 1, CE])
        h_rep = [sb(f"a_h_rep{i}", [P, CE]) for i in range(2)]
        mp = [sb(f"a_mp{i}", [P, 2, CE]) for i in range(2)]
        q = [sb(f"a_q{i}", [P, CE]) for i in range(2)]
        relus = sb("a_relus", [P, 2, CE])
        exps = [sb(f"a_exps{i}", [P, 2, CE]) for i in range(2)]
        msg = [sb(f"a_msg{i}", [P, CE]) for i in range(2)]
        den = [sb(f"a_den{i}", [P, 2, CE]) for i in range(2)]
        num = [sb(f"a_num{i}", [P, 2, CE]) for i in range(2)]
        log_den = sb("a_log_den", [P, CE])
        inv_den = [sb(f"a_inv_den{i}", [P, CE]) for i in range(2)]
        ratio = [sb(f"a_ratio{i}", [P, CE]) for i in range(2)]
        attr_sum = [sb(f"a_attr_sum{i}", [D + 1, CE]) for i in range(2)]
        back = [sb(f"a_back{i}", [P, TPC, D + 1]) for i in range(2)]
        inv_count = sb("a_inv_count", [P, TPC, 1])
        rows = [sb(f"a_rows{i}", [P, TPC, 2 * D]) for i in range(2)]

        f_ps, h_ps, o_ps, attr_ps, wm_ps = ps("a_fps"), ps("a_hps"), ps("a_ops"), ps("a_attrps"), ps("a_wmps")
        t_ps = scratch.enter_context(nc.psum_tensor("a_tps", [P, 2, CE], BF16))
        wa_ps = [ps(f"a_waps{i}") for i in range(2)]

        ft_ps = o_ps[:, 0:TPC * D]
        back_ps = o_ps[:, 128:256].rearrange("p (t c) -> p t c", t=TPC)

        idx_staged, gathered = sem("a_idx_staged"), [sem(f"a_gathered{i}") for i in range(2)]
        split_steps, turned, ut_ready = sem("a_split_steps"), sem("a_turned"), sem("a_ut_ready")
        attr_picked = sem("a_attr_picked")
        start_spread, h_spread, projected = sem("a_start_spread"), sem("a_h_spread"), sem("a_projected")
        inside_ready, h_ready = sem("a_inside_ready"), sem("a_h_ready")
        e2_done, carried, mp_done, q_done, msg_done = (
            sem("a_e2_done"), sem("a_carried"), sem("a_mp_done"), sem("a_q_done"), sem("a_msg_done"))
        relu_done, exp_done = sem("a_relu_done"), sem("a_exp_done")
        den_done, weighted, num_done = sem("a_den_done"), sem("a_weighted"), sem("a_num_done")
        log_done, inv_done, ratio_done = sem("a_log_done"), sem("a_inv_done"), sem("a_ratio_done")
        ft_done, attr_sum_done, turned_back = sem("a_ft_done"), sem("a_attr_sum_done"), sem("a_turned_back")
        inv_count_done, mean_done, ft_copied, back_copied = (
            sem("a_inv_count_done"), sem("a_mean_done"), sem("a_ft_copied"), sem("a_back_copied"))
        scattered = [sem(f"a_scattered{i}") for i in range(2)]
        first_zero, tables_zero, cleared = sem("a_first_zero"), sem("a_tables_zero"), sem("a_cleared")
        weights_in, edges_in = sem("a_weights_in"), sem("a_edges_in")

        block = scratch.enter_context(nc.Block())

        @block.sync
        def _(sp):
            flat = b.t_first.rearrange("(p j) c -> p (j c)", p=sh.NP)
            for k in range(flat.shape[1] // b.zw):
                sp.dma_start(flat[:, k * b.zw:(k + 1) * b.zw], b.zeros[0:sh.NP, :]).then_inc(first_zero, 16)
            n = 0
            per = sh.NJ * D
            for t in [*b.t_adds, b.t_seg1, b.t_seg2]:
                flat = t[0:sh.N, :].rearrange("(p j) c -> p (j c)", p=sh.NP)
                for k in range(per // b.zw):
                    sp.dma_start(flat[:, k * b.zw:(k + 1) * b.zw], b.zeros[0:sh.NP, :]).then_inc(tables_zero, 16)
                    n += 1
            for t in b.t_adds:
                sp.dma_start(t[sh.N:sh.N + P, :], b.zeros[:, 0:D]).then_inc(tables_zero, 16)
                sp.dma_start(t[sh.N + P:sh.N + P + 1, :], b.zeros[0:1, 0:D]).then_inc(tables_zero, 16)
                n += 2
            sp.wait_ge(cleared, 7)
            k8 = P // D
            sp.dma_start(b.w_tp[:, :], io["L2_gnn_W_msg_tp"].rearrange("i j h -> (i j) h")).then_inc(weights_in, 16)
            for w, name in ((b.bd_lin, "L2_gnn_W_msg_lin"), (b.bd_upd, "L2_gnn_W_upd_lin"), (b.bd1a, "L3_gnn_w1a"),
                            (b.bd1b, "L3_gnn_w1b"), (b.bd2a, "L3_gnn_w2a"), (b.bd2b, "L3_gnn_w2b")):
                for k in range(k8):
                    sp.dma_start(w[k * D:(k + 1) * D, k * D:(k + 1) * D], io[name]).then_inc(weights_in, 16)
            for w, name in ((b.b1a, "L3_gnn_b1a"), (b.b2a, "L3_gnn_b2a")):
                for k in range(k8):
                    sp.dma_start(w[k * D:(k + 1) * D, :], io[name].rearrange("(c a) -> c a", a=1)).then_inc(weights_in, 16)
            for w, name, width in ((b.b1b, "L3_gnn_b1b", D), (b.b2b, "L3_gnn_b2b", D), (b.eps1, "L3_gnn_eps1", 1), (b.eps2, "L3_gnn_eps2", 1)):
                sp.dma_start(w[:, :], bass.AP(io[name].tensor, 0, [[0, P], [1, width]])).then_inc(weights_in, 16)
            a = io["edge_attr_8"]
            sp.dma_start(b.ea8[:, 0:sh.full, :], a[0:sh.full * P, :].rearrange("(t p) c -> p t c", p=P)).then_inc(edges_in, 16)
            sp.dma_start(b.ea8[0:sh.rest, sh.full, :], a[sh.full * P:sh.E, :]).then_inc(edges_in, 16)
            sp.wait_ge(first_zero, 16 * (2 * per // b.zw))
            sp.wait_ge(tables_zero, 16 * n)
            sp.wait_ge(weights_in, 16 * (1 + 8 * k8 + 4))
            sp.wait_ge(edges_in, 16 * 2)

        @block.gpsimd
        def _(pool):
            def gather(c, u):
                pool.wait_ge(idx_staged, c + 1)
                waits_apart(pool)
                for k in range(TPC):
                    pool.indirect_dma_start(out=x_src[u][:, k, :], out_offset=None, in_=io["x"],
                                            in_offset=bass.IndirectOffsetOnAxis(ap=gather_idx[u][:, k:k + 1], axis=0),
                                            ).then_inc(gathered[u], 16)

            def scatter(c, u):
                pool.wait_ge(ft_copied, 2 * (c + 1))
                pool.wait_ge(mean_done, c + 1)
                waits_apart(pool)
                for k in range(TPC):
                    pool.indirect_dma_start(out=b.t_first, out_offset=bass.IndirectOffsetOnAxis(ap=scatter_idx[u][:, k:k + 1], axis=0),
                                            in_=rows[u][:, k, :], in_offset=None,
                                            bounds_check=sh.N - 1, oob_is_err=False).then_inc(scattered[u], 16)

            for w in (b.bd_lin, b.bd_upd, b.bd1a, b.bd1b, b.bd2a, b.bd2b):
                pool.memset(w[:, :], 0.0).then_inc(cleared, 1)
            pool.memset(b.ea8[:, sh.full:sh.tiles, :], 0.0).then_inc(cleared, 1)
            for c in range(3):
                gather(c, c % 2)
            pool.wait_ge(first_zero, 16 * (2 * sh.NJ * D // b.zw))

            def body(c, u, pair):
                if there(c + 3, C):
                    gather(c + 3, 1 - u)
                if there(c - 2, C):
                    scatter(c - 2, u)

            chunk_loop(pool, C, body)
            for u in range(2):
                pool.wait_ge(scattered[u], 16 * TPC * (C // 2))

        @block.scalar
        def _(act):
            def stage_gather(c, u):
                need(act, split_steps, 4 * (c - 1))
                act.activation(gather_idx[u][:, :], b.gsrc[:, bass.ds(c * TPC, TPC)], ACT.Copy).then_inc(idx_staged, 1)

            def evacuate_turned(c, u):
                act.wait_ge(turned, c + 1)
                need(act, projected, 2 * (c - 1))
                act.activation(ut[u][:, :], t_ps[:, 0, :], ACT.Copy)
                act.activation(vt[u][:, :], t_ps[0:3 * D, 1, :], ACT.Copy).then_inc(ut_ready, 1)

            def copy_h(s, h):
                act.wait_ge(h_spread, s + 1)
                need(act, msg_done, s - 1)
                act.activation(h_rep[h][:, :], h_ps[:, :], ACT.Copy).then_inc(h_ready, 1)

            def copy_inside(c):
                need(act, attr_sum_done, c)
                act.wait_ge(start_spread, c + 1)
                act.activation(inside[:, :], f_ps[0:D + 1, :], ACT.Copy, scale=-1.0 / RESET, bias=1.0).then_inc(inside_ready, 1)

            def softmax_factors(s, h):
                act.wait_ge(q_done, s + 1)
                need(act, exp_done, s)
                act.activation(relus[:, 0, :], q[h][:, :], ACT.Relu).then_inc(relu_done, 1)
                act.activation(relus[:, 1, :], q[h][:, :], ACT.Relu, scale=-1.0).then_inc(relu_done, 1)
                act.wait_ge(relu_done, 2 * (s + 1))
                need(act, num_done, s - 1)
                act.activation(exps[h][:, :, :], relus[:, :, :], ACT.Exp, scale=-1.0).then_inc(exp_done, 1)

            def invert_den(s, u, h):
                act.wait_ge(den_done, s + 1)
                need(act, inv_done, s)
                act.activation(log_den[:, :], den[u][:, h, :], ACT.Ln).then_inc(log_done, 1)
                act.wait_ge(log_done, s + 1)
                need(act, ratio_done, s - 1)
                act.activation(inv_den[h][:, :], log_den[:, :], ACT.Exp, scale=-1.0).then_inc(inv_done, 1)

            def copy_ft(c, u, pair):
                act.wait_ge(ft_done, 2 * (c + 1))
                need(act, scattered[u], pair * (16 * TPC))
                act.activation(rows[u][:, :, 0:D], ft_ps.rearrange("p (t c) -> p t c", t=TPC), ACT.Copy).then_inc(ft_copied, 1)
                act.activation(scatter_idx[u][:, :], b.scat[:, bass.ds(c * TPC, TPC)], ACT.Copy).then_inc(ft_copied, 1)

            def copy_back(c, u):
                act.wait_ge(turned_back, c + 1)
                need(act, ft_done, 2 * c - 1)
                need(act, mean_done, c - 1)
                act.activation(back[u][:, :, :], back_ps[:, :, 0:D + 1], ACT.Copy).then_inc(back_copied, 1)

            act.preload_act_table_set("natural_log_exp_and_others")
            for c in range(3):
                stage_gather(c, c % 2)
            evacuate_turned(0, 0)
            copy_h(0, 0)

            def body(c, u, pair):
                for h in (0, 1):
                    s = c * 2 + h
                    if h == 0 and there(c - 1, C):
                        copy_back(c - 1, 1 - u)
                    if h == 1 and there(c - 2, C):
                        copy_ft(c - 2, u, pair - 1)
                    if h == 0 and there(c, C):
                        copy_inside(c)
                    if there(s, S):
                        softmax_factors(s, h)
                    if there(s + 1, S):
                        copy_h(s + 1, 1 - h)
                    if h == 0 and there(c + 1, C):
                        evacuate_turned(c + 1, 1 - u)
                    if there(s - 1, S):
                        invert_den(s - 1, u if h else 1 - u, 1 - h)
                if there(c + 3, C):
                    stage_gather(c + 3, 1 - u)

            chunk_loop(act, C, body)

        @block.tensor
        def _(pe):
            def turn(c, u):
                pe.wait_ge(split_steps, 4 * (c + 1))
                need(pe, ut_ready, c)
                waits_apart(pe)
                for k in range(TPC):
                    pe.transpose(t_ps[:, 0, k * P:(k + 1) * P], b.edges[:, bass.ds(c * TPC + k, 1), :].rearrange("p a c -> p (a c)"), b.ident_b[:, :])
                for k in range(TPC):
                    mm = pe.transpose(t_ps[0:3 * D, 1, k * P:(k + 1) * P], x_parts[u][:, k, :, :].rearrange("p a c -> p (a c)"), b.ident_b[:, :])
                mm.then_inc(turned, 1)

            def project(c, u, s, h):
                cols = slice(h * P, (h + 1) * P)
                if h == 0:
                    pe.wait_ge(ut_ready, c + 1)
                    need(pe, mp_done, 2 * c)
                    need(pe, inside_ready, c)
                    pe.matmul(f_ps[:, :], b.w_start[:, :], ut[u][:, :], start=True, stop=True).then_inc(start_spread, 1)
                    need(pe, attr_sum_done, c)
                    pe.matmul(attr_ps[0:D + 1, :], b.w_attr[:, :], ut[u][:, :], start=True, stop=True).then_inc(attr_picked, 1)
                need(pe, h_ready, s)
                pe.matmul(h_ps[:, :], b.w_h[:, cols], vt[u][:, :], start=True, stop=True).then_inc(h_spread, 1)
                need(pe, e2_done, s - 1)
                pe.matmul(wa_ps[h][:, :], b.w_split[:, 0, cols], ut[u][:, :], start=True, stop=True)
                need(pe, msg_done, s)
                pe.matmul(wm_ps[:, :], b.w_split[:, 1, cols], ut[u][:, :], start=True, stop=True).then_inc(projected, 1)

            def sum_inputs(s, c, u, h):
                pe.wait_ge(ratio_done, s + 1)
                if h == 0:
                    need(pe, ft_copied, 2 * c)
                else:
                    need(pe, back_copied, c + 2 if not isinstance(c, int) or c + 2 <= C else C)
                for k in range(TPC):
                    mm = pe.matmul(ft_ps[:, k * D:(k + 1) * D], ratio[h][:, k * P:(k + 1) * P], b.sel[:, :],
                                   start=(h == 0 and k == 0), stop=(h == 1), skip_group_check=True)
                mm.then_inc(ft_done, 1)

            def turn_sums_back(c, u):
                pe.wait_ge(attr_sum_done, c + 1)
                need(pe, ft_copied, 2 * (c - 1))
                waits_apart(pe)
                for k in range(TPC):
                    mm = pe.transpose(back_ps[:, k, 0:D + 1], attr_sum[u][:, k * P:(k + 1) * P], b.ident[0:D + 1, 0:D + 1])
                mm.then_inc(turned_back, 1)

            turn(0, 0)

            def body(c, u, pair):
                for h in (0, 1):
                    s = c * 2 + h
                    if there(s, S):
                        project(c, u, s, h)
                    if h == 0 and there(c + 1, C):
                        turn(c + 1, 1 - u)
                    if h == 1 and there(c, C):
                        turn_sums_back(c, u)
                    if there(s - 3, S):
                        if h == 0:
                            sum_inputs(s - 3, c - 2, u, 1)
                        else:
                            sum_inputs(s - 3, c - 1, 1 - u, 0)

            chunk_loop(pe, C, body)

        @block.vector
        def _(dve):
            def logits_and_maximum(c, u, s, h):
                dve.wait_ge(h_ready, s + 1)
                dve.wait_ge(projected, s + 1)
                dve.tensor_tensor(b.e2[u][:, h, 1:CE + 1], wa_ps[h][:, :], h_rep[h][:, :], ALU.mult).then_inc(e2_done, 1)
                need(dve, num_done, s - 1)
                dve.tensor_tensor(msg[h][:, :], wm_ps[:, :], h_rep[h][:, :], ALU.mult).then_inc(msg_done, 1)
                dve.wait_ge(e2_done, s + 1)
                need(dve, mp_done, s - 1)
                dve.tensor_copy(b.e2[1 - u][:, h, 0:1], b.e2[u][:, h, CE:CE + 1]).then_inc(carried, 1)
                dve.wait_ge(inside_ready, c + 1)
                need(dve, carried, s - 1)
                dve.tensor_tensor_scan(mp[u][:, h, :], b.e2[u][:, h, 0:CE], f_ps[:, :],
                                       0.0 if isinstance(c, int) and c == 0 else mp[1 - u][:, h, CE - 1:CE],
                                       ALU.max, ALU.add).then_inc(mp_done, 1)
                dve.wait_ge(mp_done, s + 1)
                need(dve, relu_done, 2 * (s - 1))
                dve.tensor_tensor(q[h][:, :], mp[u][:, h, :], b.e2[u][:, h, 1:CE + 1], ALU.subtract).then_inc(q_done, 1)

            def split_x(c, u, pair):
                dve.wait_ge(gathered[u], (pair + 1) * (16 * TPC))
                need(dve, turned, c - 1)
                need(dve, split_steps, 4 * c)
                split(dve, [x_parts[u][:, :, k, :] for k in range(3)], x_rest[:, :, :], x_src[u][:, :, :], split_steps, c * 4)

            def sums(c, u, s, h):
                first = isinstance(c, int) and c == 0
                dve.wait_ge(exp_done, s + 1)
                dve.wait_ge(msg_done, s + 1)
                dve.tensor_tensor(msg[h][:, :], msg[h][:, :], exps[h][:, 0, :], ALU.mult).then_inc(weighted, 1)
                need(dve, den_done, s - 1)
                dve.tensor_tensor_scan(den[u][:, h, :], exps[h][:, 1, :], exps[h][:, 0, :],
                                       0.0 if first else den[1 - u][:, h, CE - 1:CE],
                                       ALU.mult, ALU.add).then_inc(den_done, 1)
                dve.wait_ge(weighted, s + 1)
                need(dve, num_done, s - 1)
                dve.tensor_tensor_scan(num[u][:, h, :], exps[h][:, 1, :], msg[h][:, :],
                                       0.0 if first else num[1 - u][:, h, CE - 1:CE],
                                       ALU.mult, ALU.add).then_inc(num_done, 1)

            def divide(s, u, h):
                dve.wait_ge(inv_done, s + 1)
                dve.wait_ge(num_done, s + 1)
                need(dve, ft_done, s - 1)
                dve.tensor_tensor(ratio[h][:, :], num[u][:, h, :], inv_den[h][:, :], ALU.mult).then_inc(ratio_done, 1)

            def attribute_sums(c, u):
                dve.wait_ge(inside_ready, c + 1)
                dve.wait_ge(attr_picked, c + 1)
                need(dve, turned_back, c - 1)
                need(dve, attr_sum_done, c)
                dve.tensor_tensor_scan(attr_sum[u][:, :], inside[:, :], attr_ps[0:D + 1, :],
                                       0.0 if isinstance(c, int) and c == 0 else attr_sum[1 - u][:, CE - 1:CE],
                                       ALU.mult, ALU.add).then_inc(attr_sum_done, 1)

            def attribute_mean(c, u, pair):
                dve.wait_ge(back_copied, c + 1)
                need(dve, mean_done, c)
                dve.reciprocal(inv_count[:, :, :], back[u][:, :, D:D + 1]).then_inc(inv_count_done, 1)
                dve.wait_ge(inv_count_done, c + 1)
                need(dve, scattered[u], pair * (16 * TPC))
                dve.tensor_tensor(rows[u][:, :, D:2 * D], back[u][:, :, 0:D],
                                  inv_count[:, :, :].broadcast_to([P, TPC, D]), ALU.mult).then_inc(mean_done, 1)

            def body(c, u, pair):
                for h in (0, 1):
                    s = c * 2 + h
                    if there(s, S):
                        logits_and_maximum(c, u, s, h)
                    if h == 0 and there(c + 1, C):
                        split_x(c + 1, 1 - u, pair if u == 0 else pair + 1)
                    if h == 0 and there(c, C):
                        attribute_sums(c, u)
                    if h == 1 and there(c - 1, C):
                        attribute_mean(c - 1, 1 - u, pair if u else pair - 1)
                    if there(s - 1, S):
                        if h == 0:
                            sums(c - 1, 1 - u, s - 1, 1)
                        else:
                            sums(c, u, s - 1, 0)
                    if there(s - 2, S):
                        divide(s - 2, 1 - u, h)

            split_x(0, 0, 0)
            chunk_loop(dve, C, body)


def message_layer(nc, sems, sh, b, io):
    def sem(name):
        return sems.enter(name)

    C = sh.chunks
    W = TPC * D
    with ExitStack() as scratch:
        def sb(name, shape, dt=F32):
            return scratch.enter_context(nc.sbuf_tensor(name, shape, dt))

        def ps(name):
            return scratch.enter_context(nc.psum_tensor(name, [P, 512], F32))

        gather_idx = [sb(f"m_gather_idx{i}", [P, TPC], U32) for i in range(2)]
        add_idx = [sb(f"m_add_idx{i}", [P, TPC], U32) for i in range(2)]
        x_dst = [sb(f"m_x_dst{i}", [P, TPC, D]) for i in range(2)]
        z = [sb(f"m_z{i}", [P, TPC, D, DE]) for i in range(2)]
        zt = [sb(f"m_zt{i}", [P, CE]) for i in range(2)]
        act_m = [sb(f"m_act{i}", [P, W]) for i in range(2)]
        act_mt = [sb(f"m_act_t{i}", [W, P]) for i in range(2)]
        m = [sb(f"m_m{i}", [P, W]) for i in range(2)]
        sums = [sb(f"m_sums{i}", [P, TPC, D]) for i in range(2)]
        src = [sb(f"m_src{i}", [P, TPC]) for i in range(2)]
        equal = [sb(f"m_equal{i}", [P, TPC, P]) for i in range(2)]
        earlier = sb("m_earlier", [P, TPC, P])
        before = sb("m_before", [P, TPC])
        to_dummy = sb("m_to_dummy", [P, TPC])
        shift = sb("m_shift", [P, TPC])

        z_ps = [ps(f"m_zps{i}") for i in range(2)]
        src_ps, pre_ps, t_ps, m_ps, sum_ps = ps("m_srcps"), ps("m_preps"), ps("m_tps"), ps("m_mps"), ps("m_sumps")

        idx_staged, gathered = sem("m_idx_staged"), [sem(f"m_gathered{i}") for i in range(2)]
        z_done, z_turned, zt_ready, pre_done, act_done = (
            sem("m_z_done"), sem("m_z_turned"), sem("m_zt_ready"), sem("m_pre_done"), sem("m_act_done"))
        act_turned, act_t_ready, m_done, m_ready = sem("m_act_turned"), sem("m_act_t_ready"), sem("m_m_done"), sem("m_m_ready")
        src_staged, src_spread, equal_done = sem("m_src_staged"), sem("m_src_spread"), sem("m_equal_done")
        earlier_done, before_done, dummy_done, shift_done, add_idx_ready = (
            sem("m_earlier_done"), sem("m_before_done"), sem("m_dummy_done"), sem("m_shift_done"), sem("m_add_idx_ready"))
        summed, sums_ready = sem("m_summed"), sem("m_sums_ready")
        added = [sem(f"m_added{k}") for k in range(TPC)]

        block = scratch.enter_context(nc.Block())

        @block.gpsimd
        def _(pool):
            def gather(c, u):
                pool.wait_ge(idx_staged, c + 1)
                waits_apart(pool)
                for k in range(TPC):
                    pool.indirect_dma_start(out=x_dst[u][:, k, :], out_offset=None, in_=b.t_x,
                                            in_offset=bass.IndirectOffsetOnAxis(ap=gather_idx[u][:, k:k + 1], axis=0),
                                            ).then_inc(gathered[u], 16)

            def add(c, u):
                pool.wait_ge(sums_ready, c + 1)
                pool.wait_ge(add_idx_ready, c + 1)
                for k in range(TPC):
                    need(pool, added[k], c * 16)
                    waits_apart(pool)
                    pool.indirect_dma_start(out=b.t_adds[k], out_offset=bass.IndirectOffsetOnAxis(ap=add_idx[u][:, k:k + 1], axis=0),
                                            in_=sums[u][:, k, :], in_offset=None, compute_op=ALU.add,
                                            ).then_inc(added[k], 16)

            for c in range(2):
                gather(c, c)

            def body(c, u, pair):
                if there(c + 2, C):
                    gather(c + 2, u)
                if there(c - 2, C):
                    add(c - 2, u)

            chunk_loop(pool, C, body)
            for k in range(TPC):
                pool.wait_ge(added[k], 16 * C)

        @block.scalar
        def _(act):
            def stage_gather(c, u):
                need(act, z_done, c - 1)
                act.activation(gather_idx[u][:, :], b.gdst[:, bass.ds(c * TPC, TPC)], ACT.Copy).then_inc(idx_staged, 1)

            def stage_src(c, u):
                need(act, add_idx_ready, c - 1)
                need(act, src_spread, c - 1)
                act.activation(src[u][:, :], b.srcf[:, bass.ds(c * TPC, TPC)], ACT.Copy).then_inc(src_staged, 1)

            def early(c, u):
                act.wait_ge(z_turned, c + 1)
                need(act, pre_done, c - 1)
                act.activation(zt[u][:, :], z_ps[u][:, :], ACT.Copy).then_inc(zt_ready, 1)

            def turn(c, u):
                act.wait_ge(act_turned, c + 1)
                need(act, m_done, c - 1)
                act.activation(act_mt[u][:, :], t_ps[0:W, 0:P], ACT.Copy).then_inc(act_t_ready, 1)

            def silu(c, u):
                act.wait_ge(pre_done, c + 1)
                need(act, act_turned, c - 1)
                act.activation(act_m[u][:, :], pre_ps[:, 0:W], ACT.Silu, scale=float(D * DE) ** -0.5).then_inc(act_done, 1)

            def late(c, u):
                act.wait_ge(m_done, c + 1)
                need(act, summed, c - 1)
                act.activation(m[u][:, :], m_ps[:, 0:W], ACT.Copy, scale=float(D) ** -0.5).then_inc(m_ready, 1)
                act.wait_ge(summed, c + 1)
                for k in range(TPC):
                    need(act, added[k], (c - 1) * 16)
                act.activation(sums[u][:, :, :], sum_ps[:, 0:W].rearrange("p (t c) -> p t c", t=TPC), ACT.Copy).then_inc(sums_ready, 1)

            for c in range(2):
                stage_gather(c, c)
                stage_src(c, c)

            def body(c, u, pair):
                if there(c, C):
                    early(c, u)
                if there(c + 2, C):
                    stage_gather(c + 2, u)
                if there(c - 1, C):
                    turn(c - 1, 1 - u)
                if there(c + 2, C):
                    stage_src(c + 2, u)
                if there(c, C):
                    silu(c, u)
                if there(c - 1, C):
                    late(c - 1, 1 - u)

            chunk_loop(act, C, body)

        @block.tensor
        def _(pe):
            def spread_src(c, u):
                pe.wait_ge(src_staged, c + 1)
                need(pe, equal_done, TPC * c)
                for k in range(TPC):
                    mm = pe.matmul(src_ps[:, k * P:(k + 1) * P], src[u][:, k:k + 1].broadcast_to([P, P]), b.ident[:, :],
                                   start=True, stop=True)
                mm.then_inc(src_spread, 1)

            def turn_z(c, u):
                pe.wait_ge(z_done, c + 1)
                need(pe, zt_ready, c - 1)
                waits_apart(pe)
                for k in range(TPC):
                    mm = pe.transpose(z_ps[u][:, k * P:(k + 1) * P], z[u][:, k, :, :].rearrange("p i j -> p (i j)"), b.ident[:, :])
                mm.then_inc(z_turned, 1)

            def mix(c, u):
                pe.wait_ge(zt_ready, c + 1)
                need(pe, act_done, c)
                for k in range(TPC):
                    mm = pe.matmul(pre_ps[:, k * D:(k + 1) * D], zt[u][:, k * P:(k + 1) * P], b.w_tp[:, :], start=True, stop=True)
                mm.then_inc(pre_done, 1)

            def turn_act(c, u):
                pe.wait_ge(act_done, c + 1)
                need(pe, act_t_ready, c)
                waits_apart(pe)
                pe.transpose(t_ps[0:W, 0:P], act_m[u][:, :], b.ident[:, :]).then_inc(act_turned, 1)

            def linear(c, u):
                pe.wait_ge(act_t_ready, c + 1)
                need(pe, m_ready, c)
                pe.matmul(m_ps[:, 0:W], act_mt[u][:, :], b.bd_lin[0:W, 0:W], start=True, stop=True).then_inc(m_done, 1)

            def sum_equal(c, u):
                pe.wait_ge(m_ready, c + 1)
                pe.wait_ge(equal_done, TPC * (c + 1))
                need(pe, sums_ready, c)
                for k in range(TPC):
                    mm = pe.matmul(sum_ps[:, k * D:(k + 1) * D], equal[u][:, k, :], m[u][:, k * D:(k + 1) * D], start=True, stop=True)
                mm.then_inc(summed, 1)

            def body(c, u, pair):
                if there(c, C):
                    spread_src(c, u)
                    turn_z(c, u)
                if there(c - 1, C):
                    turn_act(c - 1, 1 - u)
                if there(c, C):
                    mix(c, u)
                if there(c - 1, C):
                    linear(c - 1, 1 - u)
                    sum_equal(c - 1, 1 - u)

            chunk_loop(pe, C, body)

        @block.vector
        def _(dve):
            def body(c, u, pair):
                if not there(c, C):
                    return
                dve.wait_ge(gathered[u], (pair + 1) * (16 * TPC))
                need(dve, z_turned, c - 1)
                dve.tensor_tensor(z[u][:, :, :, :], x_dst[u][:, :, :].unsqueeze(3).broadcast_to([P, TPC, D, DE]),
                                  b.ea8[:, bass.ds(c * TPC, TPC), :].unsqueeze(2).broadcast_to([P, TPC, D, DE]),
                                  ALU.mult).then_inc(z_done, 1)
                dve.wait_ge(src_spread, c + 1)
                need(dve, summed, c - 1)
                for k in range(TPC):
                    dve.tensor_scalar(equal[u][:, k, :], src_ps[:, k * P:(k + 1) * P], src[u][:, k:k + 1], None,
                                      ALU.is_equal).then_inc(equal_done, 1)
                dve.tensor_scalar(to_dummy[:, :], src[u][:, :], -1.0, b.dummy[:, 0:1], ALU.mult, ALU.add).then_inc(dummy_done, 1)
                dve.wait_ge(equal_done, TPC * (c + 1))
                dve.tensor_tensor(earlier[:, :, :], equal[u][:, :, :], b.lower[:, :].unsqueeze(1).broadcast_to([P, TPC, P]),
                                  ALU.mult).then_inc(earlier_done, 1)
                dve.wait_ge(earlier_done, c + 1)
                dve.tensor_reduce(before[:, :], earlier[:, :, :], AX.X, ALU.add).then_inc(before_done, 1)
                dve.wait_ge(before_done, c + 1)
                dve.wait_ge(dummy_done, c + 1)
                dve.scalar_tensor_tensor(shift[:, :], before[:, :], 1.0, to_dummy[:, :], ALU.min, ALU.mult).then_inc(shift_done, 1)
                dve.wait_ge(shift_done, c + 1)
                for k in range(TPC):
                    need(dve, added[k], (c - 1) * 16)
                dve.tensor_tensor(add_idx[u][:, :], shift[:, :], src[u][:, :], ALU.add).then_inc(add_idx_ready, 1)

            chunk_loop(dve, C, body)


def neighbour_sums(nc, sems, sh, b, name, table_in, table_out):
    def sem(what):
        return sems.enter(name + what)

    C = sh.chunks
    with ExitStack() as scratch:
        def sb(what, shape, dt=F32):
            return scratch.enter_context(nc.sbuf_tensor(name + what, shape, dt))

        def ps(what):
            return scratch.enter_context(nc.psum_tensor(name + what, [P, 512], F32))

        gather_idx = [sb(f"gather_idx{i}", [P, TPC], U32) for i in range(2)]
        scatter_idx = [sb(f"scatter_idx{i}", [P, TPC], U32) for i in range(2)]
        x_src = [sb(f"x_src{i}", [P, TPC, D]) for i in range(2)]
        mask = [sb(f"mask{i}", [P, TPC, D]) for i in range(2)]
        inside = [sb(f"inside{i}", [D, CE]) for i in range(2)]
        run = [sb(f"run{i}", [D, CE]) for i in range(2)]
        rows = [sb(f"rows{i}", [P, TPC, D]) for i in range(2)]
        x_ps = [ps(f"x_ps{i}") for i in range(2)]
        mask_ps = [ps(f"mask_ps{i}") for i in range(2)]
        back_ps = [ps(f"back_ps{i}") for i in range(2)]
        idx_staged, gathered = sem("idx_staged"), [sem(f"gathered{i}") for i in range(2)]
        mask_staged, mask_turned, inside_ready = sem("mask_staged"), sem("mask_turned"), sem("inside_ready")
        x_turned, run_done, turned_back, rows_ready = sem("x_turned"), sem("run_done"), sem("turned_back"), sem("rows_ready")
        scattered = [sem(f"scattered{i}") for i in range(2)]

        block = scratch.enter_context(nc.Block())

        @block.gpsimd
        def _(pool):
            def gather(c, u):
                pool.wait_ge(idx_staged, c + 1)
                waits_apart(pool)
                for k in range(TPC):
                    pool.indirect_dma_start(out=x_src[u][:, k, :], out_offset=None, in_=table_in,
                                            in_offset=bass.IndirectOffsetOnAxis(ap=gather_idx[u][:, k:k + 1], axis=0),
                                            ).then_inc(gathered[u], 16)

            for c in range(2):
                gather(c, c)

            def body(c, u, pair):
                if there(c + 2, C):
                    gather(c + 2, u)
                if there(c - 1, C):
                    pool.wait_ge(rows_ready, 2 * c)
                    waits_apart(pool)
                    for k in range(TPC):
                        pool.indirect_dma_start(out=table_out, out_offset=bass.IndirectOffsetOnAxis(ap=scatter_idx[1 - u][:, k:k + 1], axis=0),
                                                in_=rows[1 - u][:, k, :], in_offset=None,
                                                bounds_check=sh.N - 1, oob_is_err=False).then_inc(scattered[1 - u], 16)

            chunk_loop(pool, C, body)
            for u in range(2):
                pool.wait_ge(scattered[u], 16 * TPC * (C // 2))

        @block.scalar
        def _(act):
            def stage(c, u):
                need(act, x_turned, c - 1)
                act.activation(gather_idx[u][:, :], b.gsrc[:, bass.ds(c * TPC, TPC)], ACT.Copy).then_inc(idx_staged, 1)
                need(act, mask_turned, c - 1)
                act.activation(mask[u][:, :, :], b.start[:, bass.ds(c * TPC, TPC)].unsqueeze(2).broadcast_to([P, TPC, D]),
                               ACT.Copy, scale=-1.0, bias=1.0).then_inc(mask_staged, 1)

            def mask_out(c, u):
                act.wait_ge(mask_turned, c + 1)
                need(act, run_done, c - 1)
                act.activation(inside[u][:, :], mask_ps[u][0:D, :], ACT.Copy).then_inc(inside_ready, 1)

            def rows_out(c, u, pair):
                act.wait_ge(turned_back, c + 1)
                need(act, scattered[u], pair * (16 * TPC))
                act.activation(rows[u][:, :, :], back_ps[u][:, 0:TPC * D].rearrange("p (t c) -> p t c", t=TPC), ACT.Copy).then_inc(rows_ready, 1)
                act.activation(scatter_idx[u][:, :], b.scat[:, bass.ds(c * TPC, TPC)], ACT.Copy).then_inc(rows_ready, 1)

            for c in range(2):
                stage(c, c)

            def body(c, u, pair):
                if there(c, C):
                    mask_out(c, u)
                if there(c + 2, C):
                    stage(c + 2, u)
                if there(c, C):
                    rows_out(c, u, pair)

            chunk_loop(act, C, body)

        @block.tensor
        def _(pe):
            def body(c, u, pair):
                if not there(c, C):
                    return
                pe.wait_ge(mask_staged, c + 1)
                need(pe, inside_ready, c - 1)
                waits_apart(pe)
                for k in range(TPC):
                    mm = pe.transpose(mask_ps[u][0:D, k * P:(k + 1) * P], mask[u][:, k, :], b.ident[:, :])
                mm.then_inc(mask_turned, 1)
                pe.wait_ge(gathered[u], (pair + 1) * (16 * TPC))
                need(pe, run_done, c - 1)
                waits_apart(pe)
                for k in range(TPC):
                    mm = pe.transpose(x_ps[u][0:D, k * P:(k + 1) * P], x_src[u][:, k, :], b.ident[:, :])
                mm.then_inc(x_turned, 1)
                pe.wait_ge(run_done, c + 1)
                need(pe, rows_ready, 2 * (c - 1))
                waits_apart(pe)
                for k in range(TPC):
                    mm = pe.transpose(back_ps[u][:, k * D:(k + 1) * D], run[u][:, k * P:(k + 1) * P], b.ident[0:D, 0:D])
                mm.then_inc(turned_back, 1)

            chunk_loop(pe, C, body)

        @block.vector
        def _(dve):
            def body(c, u, pair):
                if not there(c, C):
                    return
                dve.wait_ge(x_turned, c + 1)
                dve.wait_ge(inside_ready, c + 1)
                need(dve, turned_back, c - 1)
                need(dve, run_done, c)
                dve.tensor_tensor_scan(run[u][:, :], inside[u][:, :], x_ps[u][0:D, :],
                                       0.0 if isinstance(c, int) and c == 0 else run[1 - u][:, CE - 1:CE],
                                       ALU.mult, ALU.add).then_inc(run_done, 1)

            chunk_loop(dve, C, body)


INPUTS = ["x", "src", "dst", "edge_attr_16", "edge_attr_8", "node_vec1", "L0_gnn_W_msg", "L0_gnn_b_msg",
          "L0_gnn_W_attn", "L0_gnn_b_attn", "L2_gnn_W_msg_tp", "L2_gnn_W_msg_lin", "L2_gnn_W_upd_tp",
          "L2_gnn_W_upd_lin", "L3_gnn_eps1", "L3_gnn_w1a", "L3_gnn_b1a", "L3_gnn_w1b", "L3_gnn_b1b",
          "L3_gnn_eps2", "L3_gnn_w2a", "L3_gnn_b2a", "L3_gnn_w2b", "L3_gnn_b2b"]
class Norm:

    def __init__(self, nc, sems, scratch, name, np_, nj):
        def sb(what, shape):
            return scratch.enter_context(nc.sbuf_tensor(name + what, shape, F32))

        def sem(what):
            return sems.enter(name + what)

        self.shape = [np_, nj, D]
        self.total, self.var, self.log_var, self.rstd = (sb(w, [np_, nj]) for w in ("total", "var", "log_var", "rstd"))
        self.centred, self.square = sb("centred", self.shape), sb("square", self.shape)
        self.total_done, self.centred_done, self.square_done, self.var_done = (
            sem("total_done"), sem("centred_done"), sem("square_done"), sem("var_done"))
        self.log_done, self.rstd_done, self.done = sem("log_done"), sem("rstd_done"), sem("done")

    def before(self, dve, n, x):
        dve.tensor_reduce(self.total[:, :], x, AX.X, ALU.add).then_inc(self.total_done, 1)
        dve.wait_ge(self.total_done, n + 1)
        need(dve, self.done, n)
        dve.scalar_tensor_tensor(self.centred[:, :, :], self.total[:, :].unsqueeze(2).broadcast_to(self.shape), -1.0 / D, x,
                                 ALU.mult, ALU.add).then_inc(self.centred_done, 1)
        dve.wait_ge(self.centred_done, n + 1)
        dve.tensor_tensor(self.square[:, :, :], self.centred[:, :, :], self.centred[:, :, :], ALU.mult).then_inc(self.square_done, 1)
        dve.wait_ge(self.square_done, n + 1)
        dve.tensor_reduce(self.var[:, :], self.square[:, :, :], AX.X, ALU.add).then_inc(self.var_done, 1)

    def after(self, dve, n, out):
        dve.wait_ge(self.rstd_done, n + 1)
        dve.tensor_tensor(out, self.centred[:, :, :], self.rstd[:, :].unsqueeze(2).broadcast_to(self.shape), ALU.mult).then_inc(self.done, 1)

    def vector(self, dve, n, x, out):
        self.before(dve, n, x)
        self.after(dve, n, out)

    def scalar(self, act, n, eps_col):
        act.wait_ge(self.var_done, n + 1)
        act.activation(self.log_var[:, :], self.var[:, :], ACT.Ln, bias=eps_col, scale=1.0 / D).then_inc(self.log_done, 1)
        act.wait_ge(self.log_done, n + 1)
        act.activation(self.rstd[:, :], self.log_var[:, :], ACT.Exp, scale=-0.5).then_inc(self.rstd_done, 1)


def first_norms(nc, sems, sh, b, io):
    def sem(name):
        return sems.enter(name)

    J = 40
    B = 2
    I = sh.NJ // (J * B)
    NP = sh.NP
    with ExitStack() as scratch:
        def sb(name, shape):
            return scratch.enter_context(nc.sbuf_tensor(name, shape, F32))

        agg = [sb(f"n1_agg{i}", [NP, B, J, 2 * D]) for i in range(2)]
        y = [[sb(f"n1_y{i}_{k}", [NP, J, D]) for k in range(B)] for i in range(2)]
        y2 = [sb(f"n1_y2_{k}", [NP, J, D]) for k in range(B)]
        norms = [Norm(nc, sems, scratch, f"n1_{k}_", NP, J) for k in range(B)]
        agg_in = [sem(f"n1_agg_in{i}") for i in range(2)]
        summed, summed_again, stored, eps_done = sem("n1_summed"), sem("n1_summed_again"), sem("n1_stored"), sem("n1_eps_done")
        table = b.t_first.rearrange("(p j) c -> p j c", p=NP)
        x_in = io["x"].rearrange("(p j) c -> p j c", p=NP)
        out = b.t_x.rearrange("(p j) c -> p j c", p=NP)
        xn = b.xn[0:NP, :].rearrange("p (j c) -> p j c", c=D)
        block = scratch.enter_context(nc.Block())

        @block.sync
        def _(sp):
            def load(i, u):
                for norm in norms:
                    need(sp, norm.done, 2 * (i - 1))
                sp.dma_start(agg[u][:, :, :, :], table[:, bass.ds(i * (B * J), B * J), :].rearrange("p (b j) c -> p b j c", b=B)).then_inc(agg_in[u], 16)
                sp.dma_start(xn[:, bass.ds(i * (B * J), B * J), :], x_in[:, bass.ds(i * (B * J), B * J), :]).then_inc(agg_in[u], 16)

            for i in range(2):
                load(i, i)

            def body(i, u, pair):
                if there(i + 2, I):
                    load(i + 2, u)
                if there(i, I):
                    for norm in norms:
                        sp.wait_ge(norm.done, 2 * (i + 1))
                    sp.dma_start(out[:, bass.ds(i * (B * J), B * J), :], xn[:, bass.ds(i * (B * J), B * J), :]).then_inc(stored, 16)

            chunk_loop(sp, I, body)
            sp.wait_ge(stored, 16 * I)

        @block.gpsimd
        def _(pool):
            def first(i, u, pair):
                pool.wait_ge(agg_in[u], (pair + 1) * 32)
                for k in range(B):
                    need(pool, norms[k].done, 2 * (i - 1))
                    pool.tensor_tensor(y[u][k][:, :, :], xn[:, bass.ds(i * (B * J) + k * J, J), :], agg[u][:, k, :, 0:D],
                                       ALU.add).then_inc(summed, 1)

            def second(i, u):
                for k in range(B):
                    pool.wait_ge(norms[k].done, 2 * i + 1)
                    pool.tensor_tensor(y2[k][:, :, :], y[u][k][:, :, :], agg[u][:, k, :, D:2 * D], ALU.add).then_inc(summed_again, 1)

            first(0, 0, 0)

            def body(i, u, pair):
                if there(i + 1, I):
                    first(i + 1, 1 - u, pair if u == 0 else pair + 1)
                if there(i, I):
                    second(i, u)

            chunk_loop(pool, I, body)

        @block.vector
        def _(dve):
            for eps in (b.eps1, b.eps2):
                dve.tensor_scalar(eps[:, :], eps[:, :], 1.0, None, ALU.add).then_inc(eps_done, 1)

            def body(i, u, pair):
                if not there(i, I):
                    return
                for k in range(B):
                    dve.wait_ge(summed, B * i + k + 1)
                    norms[k].before(dve, 2 * i, y[u][k][:, :, :])
                for k in range(B):
                    norms[k].after(dve, 2 * i, y[u][k][:, :, :])
                for k in range(B):
                    dve.wait_ge(summed_again, B * i + k + 1)
                    norms[k].before(dve, 2 * i + 1, y2[k][:, :, :])
                for k in range(B):
                    norms[k].after(dve, 2 * i + 1, xn[:, bass.ds(i * (B * J) + k * J, J), :])

            chunk_loop(dve, I, body)

        @block.scalar
        def _(act):
            act.preload_act_table_set("natural_log_exp_and_others")

            def body(i, u, pair):
                if there(i, I):
                    for n in (0, 1):
                        for k in range(B):
                            norms[k].scalar(act, 2 * i + n, b.eps_col[0:NP, :])

            chunk_loop(act, I, body)


def update_nodes(nc, sems, sh, b, io):
    def sem(name):
        return sems.enter(name)

    J = 16
    I = sh.NJ // J
    NP = sh.NP
    GROUPS = J // 2
    BANKS = 4
    with ExitStack() as scratch:
        def sb(name, shape, dt=F32):
            return scratch.enter_context(nc.sbuf_tensor(name, shape, dt))

        def ps(name, shape=(P, 512), dt=F32):
            return scratch.enter_context(nc.psum_tensor(name, list(shape), dt))

        parts = [sb(f"n2_parts{i}", [NP, TPC, J * D]) for i in range(2)]
        pairs, agg = sb("n2_pairs", [NP, 2, J * D]), [sb(f"n2_agg{i}", [NP, J, D]) for i in range(2)]
        x_parts = sb("n2_x_parts", [NP, J, len(PARTS), D], BF16)
        x_rest = sb("n2_x_rest", [NP, J, D])
        xt = [sb(f"n2_xt{i}", [ROWS, J * P], BF16) for i in range(2)]
        product = [sb(f"n2_product{i}", [NP, J, D, D]) for i in range(2)]
        half, quarter = sb("n2_half", [NP, J, D // 2, D]), sb("n2_quarter", [NP, J, D // 4, D])
        mixed, act_u = sb("n2_mixed", [NP, J * D]), sb("n2_act", [NP, J * D])
        act_ut = sb("n2_act_t", [P, 2, NP])
        y = sb("n2_y", [NP, J, D])
        norm = Norm(nc, sems, scratch, "n2_", NP, J)
        xt_ps = ps("n2_xtps", (ROWS, J * P), BF16)
        y_ps = [ps(f"n2_yps{i}") for i in range(BANKS)]
        t_ps, v_ps = ps("n2_tps"), ps("n2_vps")
        parts_in = [sem(f"n2_parts_in{i}") for i in range(2)]
        pairs_done, agg_done = sem("n2_pairs_done"), sem("n2_agg_done")
        first_done, rest_done, second_done, third_done = (
            sem("n2_first_done"), sem("n2_rest_done"), sem("n2_second_done"), sem("n2_third_done"))
        x_turned, xt_ready, group_done, product_done = sem("n2_x_turned"), sem("n2_xt_ready"), sem("n2_group_done"), sem("n2_product_done")
        half_done, quarter_done, mixed_done = sem("n2_half_done"), sem("n2_quarter_done"), sem("n2_mixed_done")
        act_done, act_turned, act_t_ready, v_done = sem("n2_act_done"), sem("n2_act_turned"), sem("n2_act_t_ready"), sem("n2_v_done")
        y_done, stored = sem("n2_y_done"), sem("n2_stored")
        tables = [t[0:sh.N, :].rearrange("(p j) c -> p (j c)", p=NP) for t in b.t_adds]
        out = b.t_x.rearrange("(p j) c -> p j c", p=NP)
        xn = b.xn[0:NP, :].rearrange("p (j c) -> p j c", c=D)
        block = scratch.enter_context(nc.Block())

        @block.sync
        def _(sp):
            def load(i, u):
                need(sp, pairs_done, i - 1)
                for k in range(TPC):
                    sp.dma_start(parts[u][:, k, :], tables[k][:, bass.ds(i * (J * D), J * D)]).then_inc(parts_in[u], 16)

            for i in range(2):
                load(i, i)

            def body(i, u, pair):
                if there(i + 2, I):
                    load(i + 2, u)
                if there(i - 2, I):
                    sp.wait_ge(norm.done, i - 1)
                    sp.dma_start(out[:, bass.ds((i - 2) * J, J), :], xn[:, bass.ds((i - 2) * J, J), :]).then_inc(stored, 16)

            chunk_loop(sp, I, body)
            sp.wait_ge(stored, 16 * I)

        @block.gpsimd
        def _(pool):
            def aggregate(i, u, pair):
                pool.wait_ge(parts_in[u], (pair + 1) * (16 * TPC))
                need(pool, agg_done, i)
                pool.tensor_tensor(pairs[:, :, :], parts[u][:, 0:2, :], parts[u][:, 2:4, :], ALU.add).then_inc(pairs_done, 1)
                pool.wait_ge(pairs_done, i + 1)
                need(pool, product_done, GROUPS * (i - 1))
                pool.tensor_tensor(agg[u][:, :, :].rearrange("p j c -> p (j c)"), pairs[:, 0, :], pairs[:, 1, :], ALU.add).then_inc(agg_done, 1)

            def rests(i):
                x = xn[:, bass.ds(i * J, J), :]
                pool.wait_ge(first_done, i + 1)
                need(pool, second_done, i)
                pool.tensor_tensor(x_rest[:, :, :], x, x_parts[:, :, 0, :], ALU.subtract).then_inc(rest_done, 1)
                pool.wait_ge(second_done, i + 1)
                pool.tensor_tensor(x_parts[:, :, 5, :], x_rest[:, :, :], x_parts[:, :, 3, :], ALU.subtract).then_inc(third_done, 1)

            def fold(i, u):
                pool.wait_ge(product_done, GROUPS * (i + 1))
                need(pool, quarter_done, i)
                pool.tensor_tensor(half[:, :, :, :], product[u][:, :, 0:8, :], product[u][:, :, 8:16, :], ALU.add).then_inc(half_done, 1)
                pool.wait_ge(half_done, i + 1)
                need(pool, mixed_done, i)
                pool.tensor_tensor(quarter[:, :, :, :], half[:, :, 0:4, :], half[:, :, 4:8, :], ALU.add).then_inc(quarter_done, 1)

            rests(0)
            aggregate(0, 0, 0)

            def body(i, u, pair):
                if there(i - 1, I):
                    fold(i - 1, 1 - u)
                if there(i + 1, I):
                    rests(i + 1)
                    aggregate(i + 1, 1 - u, pair if u == 0 else pair + 1)

            chunk_loop(pool, I, body)

        @block.scalar
        def _(act):
            def first_part(i):
                need(act, x_turned, i)
                need(act, third_done, i)
                act.activation(x_parts[:, :, 0:3, :], xn[:, bass.ds(i * J, J), :].unsqueeze(2).broadcast_to([NP, J, 3, D]), ACT.Copy).then_inc(first_done, 1)

            def second_part(i):
                act.wait_ge(rest_done, i + 1)
                act.activation(x_parts[:, :, 3:5, :], x_rest[:, :, :].unsqueeze(2).broadcast_to([NP, J, 2, D]), ACT.Copy).then_inc(second_done, 1)

            def copy_turned(i, u):
                act.wait_ge(x_turned, i + 1)
                need(act, group_done, GROUPS * (i - 1))
                act.activation(xt[u][:, :].rearrange("c (j p) -> c j p", j=J)[:, :, 0:NP],
                               xt_ps[:, :].rearrange("c (j p) -> c j p", j=J)[:, :, 0:NP], ACT.Copy).then_inc(xt_ready, 1)

            first_part(0)
            second_part(0)
            copy_turned(0, 0)

            def body(i, u, pair):
                if there(i + 1, I):
                    first_part(i + 1)
                if there(i - 2, I):
                    norm.scalar(act, i - 2, b.eps_col[0:NP, :])
                if there(i + 1, I):
                    second_part(i + 1)
                if there(i - 1, I):
                    act.wait_ge(mixed_done, i)
                    need(act, act_turned, i - 1)
                    act.activation(act_u[:, :], mixed[:, :], ACT.Silu, scale=1.0 / D).then_inc(act_done, 1)
                if there(i + 1, I):
                    copy_turned(i + 1, 1 - u)
                if there(i - 1, I):
                    act.wait_ge(act_turned, i)
                    need(act, v_done, i - 1)
                    act.activation(act_ut[:, :, :], t_ps[:, 0:2 * NP].rearrange("p (k n) -> p k n", k=2), ACT.Copy,
                                   scale=float(D) ** -0.5).then_inc(act_t_ready, 1)

            chunk_loop(act, I, body)

        @block.tensor
        def _(pe):
            def turn(i):
                pe.wait_ge(third_done, i + 1)
                pe.wait_ge(second_done, i + 1)
                need(pe, xt_ready, i)
                waits_apart(pe)
                for j in range(J):
                    mm = pe.transpose(xt_ps[:, j * P:j * P + NP], x_parts[:, j, :, :].rearrange("p n c -> p (n c)"), b.ident_b[0:NP, 0:NP])
                mm.then_inc(x_turned, 1)

            turn(0)

            def body(i, u, pair):
                if there(i, I):
                    pe.wait_ge(xt_ready, i + 1)
                    for g in range(GROUPS):
                        need(pe, product_done, GROUPS * i + g - BANKS + 1)
                        for j in (2 * g, 2 * g + 1):
                            mm = pe.matmul(y_ps[g % BANKS][0:NP, (j % 2) * CH:(j % 2 + 1) * CH], xt[u][:, j * P:j * P + NP], b.w_split[0:ROWS, 2, :],
                                           start=True, stop=True)
                        mm.then_inc(group_done, 1)
                if there(i + 1, I):
                    turn(i + 1)
                if there(i - 1, I):
                    pe.wait_ge(act_done, i)
                    need(pe, act_t_ready, i - 1)
                    waits_apart(pe)
                    for k in range(2):
                        mm = pe.transpose(t_ps[:, k * NP:(k + 1) * NP], act_u[:, k * P:(k + 1) * P], b.ident[0:NP, 0:NP])
                    mm.then_inc(act_turned, 1)
                    pe.wait_ge(act_t_ready, i)
                    need(pe, y_done, i - 1)
                    for k in range(2):
                        mm = pe.matmul(v_ps[0:NP, k * P:(k + 1) * P], act_ut[:, k, :], b.bd_upd[:, :], start=True, stop=True)
                    mm.then_inc(v_done, 1)

            chunk_loop(pe, I, body)

        @block.vector
        def _(dve):
            def products(i, u, groups):
                dve.wait_ge(agg_done, i + 1)
                need(dve, half_done, i - 1)
                for g in groups:
                    dve.wait_ge(group_done, GROUPS * i + g + 1)
                    dve.tensor_tensor(product[u][:, 2 * g:2 * g + 2, :, :], y_ps[g % BANKS][0:NP, :].rearrange("p (j h k) -> p j h k", j=2, h=D),
                                      agg[u][:, 2 * g:2 * g + 2, :].unsqueeze(3).broadcast_to([NP, 2, D, D]), ALU.mult).then_inc(product_done, 1)

            def mix(i):
                dve.wait_ge(quarter_done, i + 1)
                need(dve, act_done, i)
                dve.tensor_reduce(mixed[:, :].rearrange("p (j k) -> p j k", k=D), quarter[:, :, :, :].rearrange("p j h k -> p j k h"),
                                  AX.X, ALU.add).then_inc(mixed_done, 1)

            def update(i):
                dve.wait_ge(v_done, i + 1)
                need(dve, norm.centred_done, i)
                dve.scalar_tensor_tensor(y[:, :, :], xn[:, bass.ds(i * J, J), :], 2.0, v_ps[0:NP, 0:J * D].rearrange("p (j c) -> p j c", c=D),
                                         ALU.mult, ALU.add).then_inc(y_done, 1)
                dve.wait_ge(y_done, i + 1)
                norm.before(dve, i, y[:, :, :])

            def body(i, u, pair):
                if there(i - 2, I):
                    update(i - 2)
                if there(i, I):
                    products(i, u, range(0, GROUPS // 2))
                if there(i - 1, I):
                    mix(i - 1)
                if there(i, I):
                    products(i, u, range(GROUPS // 2, GROUPS))
                if there(i - 2, I):
                    norm.after(dve, i - 2, xn[:, bass.ds((i - 2) * J, J), :])

            chunk_loop(dve, I, body)


def graph_mlp(nc, sems, sh, b, name, seg_table, x_in, eps1, wa, ba, wb, bb, final):
    def sem(what):
        return sems.enter(name + what)

    J = 40
    I = sh.NJ // J
    NP = sh.NP
    B = J * D // P
    W0 = 4 * NP
    with ExitStack() as scratch:
        def sb(what, shape):
            return scratch.enter_context(nc.sbuf_tensor(name + what, shape, F32))

        def ps(what):
            return scratch.enter_context(nc.psum_tensor(name + what, [P, 1024], F32))

        seg = [sb(f"seg{i}", [NP, J, D]) for i in range(2)]
        h_in = sb("h_in", [NP, J, D])
        ht, hidden_t = sb("ht", [P, B * NP]), sb("hidden_t", [P, B * NP])
        y = sb("y", [NP, J, D])
        t_ps, hid_ps, o_ps = ps("t_ps"), ps("hid_ps"), ps("o_ps")
        seg_in = [sem(f"seg_in{i}") for i in range(2)]
        h_done, h_turned, ht_ready, hid_done, hidden_ready, o_done = (
            sem("h_done"), sem("h_turned"), sem("ht_ready"), sem("hid_done"), sem("hidden_ready"), sem("o_done"))
        biased, done, stored = sem("biased"), sem("done"), [sem(f"stored{i}") for i in range(2)]
        if final:
            norm = Norm(nc, sems, scratch, name + "norm_", NP, J)
            top, prob, den, log_den = sb("top", [NP, J]), sb("prob", [NP, J, D]), sb("den", [NP, J]), sb("log_den", [NP, J])
            result = [sb(f"result{i}", [NP, J, D]) for i in range(2)]
            top_done, less_done, prob_done, den_done, log_den_done, lsm_done, res_done = (
                sem("top_done"), sem("less_done"), sem("prob_done"), sem("den_done"), sem("log_den_done"), sem("lsm_done"), sem("res_done"))
            finished = norm.done
        else:
            finished = done
        table = seg_table.rearrange("(p j) c -> p j c", p=NP)
        out = (b.out if final else b.t_h).rearrange("(p j) c -> p j c", p=NP)
        nodes = x_in[0:NP, :].rearrange("p (j c) -> p j c", c=D)
        xn = b.xn[0:NP, :].rearrange("p (j c) -> p j c", c=D)
        hn = b.hn[0:NP, :].rearrange("p (j c) -> p j c", c=D)
        block = scratch.enter_context(nc.Block())

        def halves(t, rows=P):
            return ((t[0:rows, 0:W0], slice(0, W0)), (t[0:rows, 512:512 + NP], slice(W0, B * NP)))

        def at(k):
            return k * NP if k < 4 else 512

        @block.sync
        def _(sp):
            def load(i, u):
                need(sp, h_done, i - 1)
                sp.dma_start(seg[u][:, :, :], table[:, bass.ds(i * J, J), :]).then_inc(seg_in[u], 16)

            for i in range(2):
                load(i, i)

            def body(i, u, pair):
                if there(i + 2, I):
                    load(i + 2, u)
                if there(i, I):
                    sp.wait_ge(finished, i + 1)
                    sp.dma_start(out[:, bass.ds(i * J, J), :],
                                 result[u][:, :, :] if final else hn[:, bass.ds(i * J, J), :]).then_inc(stored[u], 16)

            chunk_loop(sp, I, body)
            for u in range(2):
                sp.wait_ge(stored[u], 16 * (I // 2))

        @block.vector
        def _(dve):
            def start(i, u, pair):
                dve.wait_ge(seg_in[u], (pair + 1) * 16)
                need(dve, h_turned, i)
                dve.scalar_tensor_tensor(h_in[:, :, :], nodes[:, bass.ds(i * J, J), :], eps1[0:NP, 0:1], seg[u][:, :, :],
                                         ALU.mult, ALU.add).then_inc(h_done, 1)

            def end(i, u, pair):
                dve.wait_ge(o_done, i + 1)
                need(dve, finished, i)
                dve.tensor_tensor(y[:, :, :], o_ps[0:NP, 0:J * D].rearrange("p (j c) -> p j c", c=D),
                                  bb[0:NP, :].unsqueeze(1).broadcast_to([NP, J, D]), ALU.add).then_inc(biased, 1)
                dve.wait_ge(biased, i + 1)
                if not final:
                    dve.tensor_scalar(hn[:, bass.ds(i * J, J), :], y[:, :, :], 0.0, None, ALU.max).then_inc(done, 1)
                    return
                dve.tensor_reduce(top[:, :], y[:, :, :], AX.X, ALU.max).then_inc(top_done, 1)
                dve.wait_ge(top_done, i + 1)
                dve.tensor_tensor(y[:, :, :], y[:, :, :], top[:, :].unsqueeze(2).broadcast_to([NP, J, D]), ALU.subtract).then_inc(less_done, 1)
                dve.wait_ge(prob_done, i + 1)
                dve.tensor_reduce(den[:, :], prob[:, :, :], AX.X, ALU.add).then_inc(den_done, 1)
                dve.wait_ge(log_den_done, i + 1)
                dve.tensor_tensor(y[:, :, :], y[:, :, :], log_den[:, :].unsqueeze(2).broadcast_to([NP, J, D]), ALU.subtract).then_inc(lsm_done, 1)
                dve.wait_ge(lsm_done, i + 1)
                dve.tensor_tensor(y[:, :, :], y[:, :, :], xn[:, bass.ds(i * J, J), :], ALU.add).then_inc(res_done, 1)
                dve.wait_ge(res_done, i + 1)
                need(dve, stored[u], pair * 16)
                norm.vector(dve, i, y[:, :, :], result[u][:, :, :])

            def body(i, u, pair):
                if there(i, I):
                    start(i, u, pair)
                if there(i - 1, I):
                    end(i - 1, 1 - u, pair if u else pair - 1)

            chunk_loop(dve, I, body)

        @block.tensor
        def _(pe):
            def body(i, u, pair):
                if not there(i, I):
                    return
                pe.wait_ge(h_done, i + 1)
                need(pe, ht_ready, 2 * i)
                for k in range(B):
                    mm = pe.transpose(t_ps[:, at(k):at(k) + NP], h_in[:, 8 * k:8 * k + 8, :].rearrange("p j c -> p (j c)"), b.ident[0:NP, 0:NP])
                mm.then_inc(h_turned, 1)
                need(pe, hidden_ready, 2 * i)
                for k, (part, cols) in enumerate(halves(hid_ps)):
                    pe.wait_ge(ht_ready, 2 * i + k + 1)
                    mm = pe.matmul(part, wa[:, :], ht[:, cols], start=True, stop=True)
                    mm.then_inc(hid_done, 1)
                pe.wait_ge(hidden_ready, 2 * (i + 1))
                need(pe, biased, i)
                for k in range(B):
                    mm = pe.matmul(o_ps[0:NP, k * P:(k + 1) * P], hidden_t[:, k * NP:(k + 1) * NP], wb[:, :], start=True, stop=True)
                mm.then_inc(o_done, 1)

            chunk_loop(pe, I, body)

        @block.scalar
        def _(act):
            act.preload_act_table_set("natural_log_exp_and_others")

            def body(i, u, pair):
                if there(i, I):
                    act.wait_ge(h_turned, i + 1)
                    need(act, hid_done, 2 * i)
                    for part, cols in halves(t_ps):
                        act.activation(ht[:, cols], part, ACT.Copy).then_inc(ht_ready, 1)
                    need(act, o_done, i)
                    for k, (part, cols) in enumerate(halves(hid_ps)):
                        act.wait_ge(hid_done, 2 * i + k + 1)
                        act.activation(hidden_t[:, cols], part, ACT.Relu, bias=ba[:, 0:1]).then_inc(hidden_ready, 1)
                if final and there(i - 1, I):
                    act.wait_ge(less_done, i)
                    act.activation(prob[:, :, :], y[:, :, :], ACT.Exp).then_inc(prob_done, 1)
                    act.wait_ge(den_done, i)
                    act.activation(log_den[:, :], den[:, :], ACT.Ln).then_inc(log_den_done, 1)
                    norm.scalar(act, i - 1, b.eps_col[0:NP, :])

            chunk_loop(act, I, body)


class Buffers:
    pass


def build(nc, io, out):
    N, E = io["x"].shape[0], io["src"].shape[0]
    sh = Shapes(N, E)
    b = Buffers()
    with ExitStack() as ctx:
        def sb(name, shape, dt=F32):
            return ctx.enter_context(nc.sbuf_tensor(name, shape, dt))

        b.out = out
        b.t_first = nc.dram_tensor("t_first", [N, 2 * D], F32, kind="Internal").ap()
        b.t_x = nc.dram_tensor("t_x", [N, D], F32, kind="Internal").ap()
        b.t_h = nc.dram_tensor("t_h", [N, D], F32, kind="Internal").ap()
        b.t_adds = [nc.dram_tensor(f"t_add{k}", [N + 1 + P, D], F32, kind="Internal").ap() for k in range(TPC)]
        b.t_seg1 = nc.dram_tensor("t_seg1", [N, D], F32, kind="Internal").ap()
        b.t_seg2 = nc.dram_tensor("t_seg2", [N, D], F32, kind="Internal").ap()

        b.ident, b.lower, b.sel = sb("ident", [P, P]), sb("lower", [P, P]), sb("sel", [P, D])
        b.ident_b = sb("ident_b", [P, P], BF16)
        b.eps_col, b.dummy, b.dummy_i = sb("eps_col", [P, 1]), sb("dummy_row", [P, 1]), sb("dummy_row_i", [P, 1], I32)
        b.w_split = sb("w_split", [P, 3, CH], BF16)
        b.w_tp = sb("w_tp", [P, D])
        b.bd_lin, b.bd_upd, b.bd1a, b.bd1b, b.bd2a, b.bd2b = (sb(w, [P, P]) for w in ("bd_lin", "bd_upd", "bd1a", "bd1b", "bd2a", "bd2b"))
        b.b1a, b.b2a, b.b1b, b.b2b = sb("b1a", [P, 1]), sb("b2a", [P, 1]), sb("b1b", [P, D]), sb("b2b", [P, D])
        b.eps1, b.eps2 = sb("eps1", [P, 1]), sb("eps2", [P, 1])
        cols = sh.tiles + 2 * TPC
        b.gsrc, b.gdst, b.scat = (sb(w, [P, cols], I32) for w in ("gsrc", "gdst", "scat"))
        b.start, b.srcf = sb("start", [P, cols]), sb("srcf", [P, cols])
        with ExitStack() as outer:
            b.ea8 = outer.enter_context(nc.sbuf_tensor("ea8", [P, sh.tiles, DE], F32))
            with ExitStack() as first:
                def early(name, shape, dt=F32):
                    return first.enter_context(nc.sbuf_tensor(name, shape, dt))

                b.zw = 800
                b.zeros = early("zeros", [P, b.zw])
                b.edges = early("edges", [P, sh.tiles, P], BF16)
                b.w_start, b.w_attr, b.w_h = early("w_start", [P, P], BF16), early("w_attr", [P, D + 1], BF16), early("w_h", [3 * D, CH], BF16)
                b.e2 = [early(f"e2_{i}", [P, 2, CE + 1]) for i in range(2)]
                with Semaphores(nc) as sems:
                    constants_and_indices(nc, sems, sh, b, io)
                with Semaphores(nc) as sems:
                    attention_layer(nc, sems, sh, b, io)
            b.xn = outer.enter_context(nc.sbuf_tensor("xn", [P, sh.NJ * D], F32))
            with Semaphores(nc) as sems:
                first_norms(nc, sems, sh, b, io)
            with Semaphores(nc) as sems:
                message_layer(nc, sems, sh, b, io)
            with Semaphores(nc) as sems:
                update_nodes(nc, sems, sh, b, io)
            b.hn = outer.enter_context(nc.sbuf_tensor("hn", [P, sh.NJ * D], F32))
            with Semaphores(nc) as sems:
                neighbour_sums(nc, sems, sh, b, "s1_", b.t_x, b.t_seg1)
            with Semaphores(nc) as sems:
                graph_mlp(nc, sems, sh, b, "g1_", b.t_seg1, b.xn, b.eps1, b.bd1a, b.b1a, b.bd1b, b.b1b, False)
            with Semaphores(nc) as sems:
                neighbour_sums(nc, sems, sh, b, "s2_", b.t_h, b.t_seg2)
            with Semaphores(nc) as sems:
                graph_mlp(nc, sems, sh, b, "g2_", b.t_seg2, b.hn, b.eps2, b.bd2a, b.b2a, b.bd2b, b.b2b, True)


def kernel(**inputs):
    import numpy as np
    import concourse.bacc as bacc
    from concourse.bass_utils import run_bass_kernel_spmd

    nc = bacc.Bacc("TRN2", target_bir_lowering=False, num_devices=1)
    arrays, io = {}, {}
    for name in INPUTS:
        a = np.ascontiguousarray(inputs[name])
        if a.ndim == 0:
            a = a.reshape(1)
        arrays[f"in_{name}"] = a
        io[name] = nc.dram_tensor(f"in_{name}", a.shape, mybir.dt.from_np(a.dtype), kind="ExternalInput").ap()
    out = nc.dram_tensor("out", list(inputs["x"].shape), F32, kind="ExternalOutput").ap()
    build(nc, io, out)
    r = run_bass_kernel_spmd(nc, [arrays], core_ids=[0])
    return r.results[0]["out"]
```

```python
from contextlib import ExitStack

import concourse.bass as bass
from concourse import mybir

F32 = mybir.dt.float32
BF16 = mybir.dt.bfloat16
I32 = mybir.dt.int32
U32 = mybir.dt.uint32
ALU = mybir.AluOpType
ACT = mybir.ActivationFunctionType
AX = mybir.AxisListType

P = 128
D = 16
DE = 8
CH = D * D
TPC = 4
CE = TPC * P
RESET = -(2.0 ** 100)
PARTS = ((0, 0), (0, 1), (0, 2), (1, 0), (1, 1), (2, 0))
ROWS = len(PARTS) * D
BIAS = ROWS
START_ROW = ROWS + 3
EPS = 1e-5


def there(index, count):
    return not isinstance(index, int) or 0 <= index < count


def need(engine, semaphore, value):
    if not isinstance(value, int) or value > 0:
        engine.wait_ge(semaphore, value)


class Semaphores:

    def __init__(self, nc):
        self.nc, self.handles = nc, []

    def __enter__(self):
        return self

    def enter(self, name):
        self.handles.append(self.nc.alloc_semaphore(name=name))
        return self.handles[-1]

    def __exit__(self, kind, value, trace):
        if kind is None:
            self.nc.clear_and_free_semaphores(self.handles)
            self.nc.all_engine_barrier()


class Shapes:
    def __init__(self, n, e):
        self.N, self.E = n, e
        self.chunks = -(-e // CE)
        assert self.chunks % 2 == 0 and self.chunks >= 6
        self.tiles = self.chunks * TPC
        self.full = e // P
        self.rest = e - self.full * P
        self.NP = 125
        self.NJ = n // self.NP
        assert self.NP * self.NJ == n and self.NJ % 32 == 0
        self.G = self.tiles // TPC
        self.none = 1 << 21
        self.far = 200000
        assert self.far > n


def waits_apart(engine):
    engine.nop(nofuse=True)


def chunk_loop(engine, chunks, body):
    for c in range(4):
        body(c, c % 2, c // 2)
    with engine.Fori(2, chunks // 2 - 1) as pair:
        for u in (0, 1):
            body(pair * 2 + u, u, pair)
    for c in range(chunks - 2, chunks + 2):
        body(c, c % 2, c // 2)


def split_first(engine, parts, x, done):
    engine.tensor_copy(parts[0], x).then_inc(done, 1)


def split_others(engine, parts, rest, x, done, at):
    engine.wait_ge(done, at + 1)
    engine.tensor_tensor(rest, x, parts[0], ALU.subtract).then_inc(done, 1)
    engine.wait_ge(done, at + 2)
    engine.tensor_copy(parts[1], rest).then_inc(done, 1)
    engine.wait_ge(done, at + 3)
    engine.tensor_tensor(parts[2], rest, parts[1], ALU.subtract).then_inc(done, 1)


def constants_and_indices(nc, sems, sh, b, io):
    def sem(name):
        return sems.enter(name)

    G, N = sh.G, sh.N
    zeroed, made, sel_done = sem("zeroed"), sem("made"), sem("sel_done")
    weights_in, edges_in, idx_in = sem("weights_in"), sem("edges_in"), sem("idx_in")
    rows_done, turned, columns_done = sem("rows_done"), sem("turned"), sem("columns_done")
    weights_split, weights_picked, masks_done, edges_split, edges_doubled = (
        sem("weights_split"), sem("weights_picked"), sem("masks_done"), sem("edges_split"), sem("edges_doubled"))
    thrice_done, spread_done, first_zero = sem("thrice_done"), sem("spread_done"), sem("first_zero")
    with ExitStack() as scratch:
        def sb(name, shape, dt=F32):
            return scratch.enter_context(nc.sbuf_tensor(name, shape, dt))

        dst_rows, src_rows = sb("dst_rows", [G, TPC, P + 2], I32), sb("src_rows", [G, TPC, P], I32)
        dst_f, end_f = sb("dst_f", [G, TPC, P + 2]), sb("end_f", [G, TPC, P])
        rows_f = sb("rows_f", [G, 5, TPC, P])
        ea16, weights = sb("ea16", [P, sh.tiles, D]), sb("weights", [P, 3, CH])
        parts = [sb(f"weights_part{i}", [P, 3, CH], BF16) for i in range(3)]
        picked = [sb(f"weights_picked{i}", [P, 3, CH]) for i in range(2)]
        blocks, mask = sb("blocks", [P, 8]), sb("mask", [P, 3])
        h_rows, thrice = sb("h_rows", [D, CH]), sb("thrice", [D, 3, D])
        turned_ps = [scratch.enter_context(nc.psum_tensor(f"turned_ps{i}", [P, 512], F32)) for i in range(5)]
        spread_ps = scratch.enter_context(nc.psum_tensor("spread_ps", [P, 512], F32))
        START, SCAT, GDST, GSRC, SRC = range(5)
        src, dst = io["src"], io["dst"]
        last = sh.full - 3 * G

        block = scratch.enter_context(nc.Block())

        @block.gpsimd
        def _(pool):
            pool.memset(b.ident[:, :], 0.0).then_inc(zeroed, 1)
            pool.memset(dst_rows[:, :, :], sh.far).then_inc(zeroed, 1)
            pool.memset(src_rows[:, :, :], sh.N).then_inc(zeroed, 1)
            pool.memset(weights[:, :, :], 0.0).then_inc(zeroed, 1)
            pool.memset(ea16[:, sh.full:sh.tiles, :], 0.0).then_inc(zeroed, 1)
            pool.memset(h_rows[:, :], 1.0).then_inc(made, 1)
            pool.memset(b.w_start[:, :], 0.0).then_inc(made, 1)
            pool.memset(b.lower[:, :], 1.0).then_inc(made, 1)
            pool.memset(b.eps_col[:, :], EPS).then_inc(made, 1)
            pool.memset(b.zeros[:, :], 0.0).then_inc(made, 1)
            for a in (b.gsrc, b.gdst, b.scat):
                pool.memset(a[:, :], 0).then_inc(made, 1)
            for a in (b.start, b.srcf):
                pool.memset(a[:, :], 0.0).then_inc(made, 1)
            pool.iota(b.dummy_i[:, :], pattern=[[0, 1]], base=N + 1, channel_multiplier=1).then_inc(made, 1)
            pool.wait_ge(made, 11)
            pool.wait_ge(zeroed, 1)
            pool.affine_select(out=b.ident[:, :], in_=b.ident[:, :], compare_op=ALU.not_equal, fill=1.0,
                               base=0, pattern=[[-1, P]], channel_multiplier=1).then_inc(sel_done, 1)
            pool.affine_select(out=h_rows[:, :], in_=h_rows[:, :], compare_op=ALU.is_ge, fill=0.0,
                               base=0, pattern=[[1, CH]], channel_multiplier=-D).then_inc(sel_done, 1)
            pool.wait_ge(sel_done, 2)
            pool.affine_select(out=h_rows[:, :], in_=h_rows[:, :], compare_op=ALU.is_ge, fill=0.0,
                               base=D - 1, pattern=[[-1, CH]], channel_multiplier=D).then_inc(sel_done, 1)
            pool.affine_select(out=b.w_start[:, :], in_=b.w_start[:, :], compare_op=ALU.not_equal, fill=RESET,
                               base=-START_ROW, pattern=[[0, P]], channel_multiplier=1).then_inc(sel_done, 1)
            pool.affine_select(out=b.lower[:, :], in_=b.lower[:, :], compare_op=ALU.is_gt, fill=0.0,
                               base=0, pattern=[[-1, P]], channel_multiplier=1).then_inc(sel_done, 1)
            pool.memset(b.edges[:, :, BIAS:BIAS + 3], 1.0).then_inc(edges_doubled, 1)
            pool.memset(b.edges[:, :, START_ROW + 1:P], 0.0).then_inc(edges_doubled, 1)

        @block.sync
        def _(sp):
            sp.wait_ge(zeroed, 3)
            for g in range(TPC):
                n = G if g < 3 else last
                r0 = 0 if g else 1
                at = g * G * P
                sp.dma_start(dst_rows[r0:n, g, :], bass.AP(dst.tensor, at + r0 * P - 1, [[P, n - r0], [1, P + 2]])).then_inc(idx_in, 16)
                sp.dma_start(src_rows[0:n, g, :], src[at:at + n * P].rearrange("(r e) -> r e", e=P)).then_inc(idx_in, 16)
            sp.dma_start(dst_rows[0:1, 0, 1:P + 2], dst[0:P + 1].rearrange("(a e) -> a e", a=1)).then_inc(idx_in, 16)
            sp.dma_start(dst_rows[last:last + 1, 3, 0:sh.rest + 1], dst[sh.full * P - 1:sh.E].rearrange("(a e) -> a e", a=1)).then_inc(idx_in, 16)
            sp.dma_start(src_rows[last:last + 1, 3, 0:sh.rest], src[sh.full * P:sh.E].rearrange("(a e) -> a e", a=1)).then_inc(idx_in, 16)
            sp.wait_ge(made, 11)
            sp.wait_ge(edges_in, 32)
            flat = b.t_first.rearrange("(p j) c -> p (j c)", p=sh.NP)
            n = flat.shape[1] // b.zw // 2
            for k in range(n):
                sp.dma_start(flat[:, k * b.zw:(k + 1) * b.zw], b.zeros[0:sh.NP, :]).then_inc(first_zero, 16)
            sp.wait_ge(first_zero, 16 * n)

        @block.scalar
        def _(act):
            act.preload_act_table_set("natural_log_exp_and_others")
            act.wait_ge(zeroed, 5)
            names = ("L0_gnn_W_attn", "L0_gnn_W_msg", "L2_gnn_W_upd_tp")
            for k, name in enumerate(names):
                w = io[name] if k < 2 else io[name].rearrange("i h k -> i (h k)")
                for n in range(len(PARTS)):
                    act.dma_start(weights[n * D:(n + 1) * D, k, :], w).then_inc(weights_in, 16)
            for k, name in enumerate(("L0_gnn_b_attn", "L0_gnn_b_msg")):
                act.dma_start(weights[BIAS:BIAS + 3, k, :], bass.AP(io[name].tensor, 0, [[0, 3], [1, CH]])).then_inc(weights_in, 16)
            act.wait_ge(idx_in, 16 * 11)
            a = io["edge_attr_16"]
            act.dma_start(ea16[:, 0:sh.full, :], a[0:sh.full * P, :].rearrange("(t p) c -> p t c", p=P)).then_inc(edges_in, 16)
            act.dma_start(ea16[0:sh.rest, sh.full, :], a[sh.full * P:sh.E, :]).then_inc(edges_in, 16)
            for to, of, step in ((1, 0, 1), (2, 0, 1), (4, 3, 3)):
                act.wait_ge(edges_split, step)
                act.activation(b.edges[:, :, to * D:(to + 1) * D], b.edges[:, :, of * D:(of + 1) * D], ACT.Copy).then_inc(edges_doubled, 1)

        @block.vector
        def _(dve):
            dve.wait_ge(idx_in, 16 * 11)
            dve.tensor_copy(dst_f[:, :, :], dst_rows[:, :, :]).then_inc(rows_done, 1)
            dve.tensor_copy(rows_f[:, SRC, :, :], src_rows[:, :, :]).then_inc(rows_done, 1)
            dve.wait_ge(rows_done, 2)
            here = dst_f[:, :, 1:P + 1]
            dve.tensor_tensor(rows_f[:, START, :, :], here, dst_f[:, :, 0:P], ALU.not_equal).then_inc(rows_done, 1)
            dve.tensor_tensor(end_f[:, :, :], here, dst_f[:, :, 2:P + 2], ALU.is_equal).then_inc(rows_done, 1)
            dve.tensor_scalar(rows_f[:, GDST, :, :], here, float(N - 1), None, ALU.min).then_inc(rows_done, 1)
            dve.tensor_scalar(rows_f[:, GSRC, :, :], rows_f[:, SRC, :, :], float(N - 1), None, ALU.min).then_inc(rows_done, 1)
            dve.wait_ge(rows_done, 4)
            dve.scalar_tensor_tensor(rows_f[:, SCAT, :, :], end_f[:, :, :], float(sh.none), here, ALU.mult, ALU.add).then_inc(rows_done, 1)
            dve.wait_ge(made, 11)
            dve.wait_ge(turned, 5)
            for k, out in ((START, b.start), (SCAT, b.scat), (GDST, b.gdst), (GSRC, b.gsrc), (SRC, b.srcf)):
                dve.tensor_copy(out[:, 0:sh.tiles], turned_ps[k][:, 0:sh.tiles]).then_inc(columns_done, 1)
            dve.tensor_copy(b.dummy[:, :], b.dummy_i[:, :]).then_inc(columns_done, 1)
            dve.wait_ge(columns_done, 1)
            dve.tensor_copy(b.edges[:, :, START_ROW], b.start[:, 0:sh.tiles]).then_inc(columns_done, 1)
            dve.wait_ge(sel_done, 5)
            dve.tensor_copy(thrice[:, :, :], b.ident[0:D, 0:D].unsqueeze(1).broadcast_to([D, 3, D])).then_inc(thrice_done, 1)
            dve.tensor_copy(b.ident_b[:, :], b.ident[:, :]).then_inc(columns_done, 1)
            dve.tensor_reduce(b.sel[:, :], b.ident[:, :].rearrange("p (i o) -> p o i", o=D), AX.X, ALU.add).then_inc(columns_done, 1)
            dve.tensor_reduce(blocks[:, 0:6], b.ident[:, 0:ROWS].rearrange("p (n i) -> p n i", i=D), AX.X, ALU.add).then_inc(masks_done, 1)
            dve.wait_ge(masks_done, 1)
            dve.tensor_tensor(mask[:, 0:2], blocks[:, 0:2], blocks[:, 3:5], ALU.add).then_inc(masks_done, 1)
            dve.tensor_tensor(mask[:, 2:3], blocks[:, 2:3], b.ident[:, BIAS + 2:BIAS + 3], ALU.add).then_inc(masks_done, 1)
            dve.wait_ge(masks_done, 2)
            dve.tensor_tensor(mask[:, 0:2], mask[:, 0:2], b.ident[:, BIAS:BIAS + 2], ALU.add).then_inc(masks_done, 1)
            dve.wait_ge(masks_done, 4)
            dve.tensor_tensor(mask[:, 0:1], mask[:, 0:1], blocks[:, 5:6], ALU.add).then_inc(masks_done, 1)
            dve.wait_ge(weights_in, 16 * 20)
            split_first(dve, [p[:, :, :] for p in parts], weights[:, :, :], weights_split)
            split_others(dve, [p[:, :, :] for p in parts], weights[:, :, :], weights[:, :, :], weights_split, 0)
            dve.wait_ge(weights_split, 4)
            dve.wait_ge(masks_done, 5)
            dve.tensor_scalar(picked[0][:, :, :], parts[0][:, :, :], mask[:, 0:1], None, ALU.mult).then_inc(weights_picked, 1)
            for k in (1, 2):
                dve.wait_ge(weights_picked, k)
                dve.scalar_tensor_tensor(picked[k][:, :, :] if k == 1 else b.w_split[:, :, :], parts[k][:, :, :], mask[:, k:k + 1],
                                         picked[k - 1][:, :, :], ALU.mult, ALU.add).then_inc(weights_picked, 1)
            dve.tensor_tensor(b.w_attr[:, 0:D], b.ident[:, 0:D], b.ident[:, 3 * D:4 * D], ALU.add).then_inc(masks_done, 1)
            dve.tensor_copy(b.w_attr[:, D:D + 1], b.ident[:, BIAS:BIAS + 1]).then_inc(masks_done, 1)
            dve.wait_ge(masks_done, 6)
            dve.tensor_tensor(b.w_attr[:, 0:D], b.w_attr[:, 0:D], b.ident[:, 5 * D:6 * D], ALU.add).then_inc(masks_done, 1)
            for u in range(2):
                dve.memset(b.e2[u][:, :, 0:1], 0.0).then_inc(columns_done, 1)
            dve.wait_ge(spread_done, 1)
            dve.tensor_copy(b.w_h[:, :], spread_ps[0:3 * D, 0:CH]).then_inc(columns_done, 1)
            dve.wait_ge(edges_in, 32)
            edges = [b.edges[:, :, n * D:(n + 1) * D] for n in (0, 3, 5)]
            split_first(dve, edges, ea16[:, :, :], edges_split)
            split_others(dve, edges, ea16[:, :, :], ea16[:, :, :], edges_split, 0)

        @block.tensor
        def _(pe):
            pe.wait_ge(sel_done, 1)
            pe.wait_ge(rows_done, 7)
            for k in range(5):
                for g in range(TPC):
                    mm = pe.transpose(turned_ps[k][:, g * G:(g + 1) * G], rows_f[:, k, g, :], b.ident[0:G, 0:G])
                mm.then_inc(turned, 1)
            pe.wait_ge(sel_done, 3)
            pe.wait_ge(thrice_done, 1)
            pe.matmul(spread_ps[0:3 * D, 0:CH], thrice[:, :, :].rearrange("i n o -> i (n o)"), h_rows[:, :],
                      start=True, stop=True).then_inc(spread_done, 1)


def attention_layer(nc, sems, sh, b, io):
    def sem(name):
        return sems.enter(name)

    C, S = sh.chunks, 2 * sh.chunks
    with ExitStack() as scratch:
        def sb(name, shape, dt=F32):
            return scratch.enter_context(nc.sbuf_tensor(name, shape, dt))

        def ps(name):
            return scratch.enter_context(nc.psum_tensor(name, [P, 512], F32))

        gather_idx = [sb(f"a_gather_idx{i}", [P, TPC], U32) for i in range(2)]
        scatter_idx = [sb(f"a_scatter_idx{i}", [P, TPC], U32) for i in range(2)]
        x_src = [sb(f"a_x_src{i}", [P, TPC, D]) for i in range(2)]
        x_parts = [sb(f"a_x_parts{i}", [P, TPC, 3, D], BF16) for i in range(2)]
        x_rest = sb("a_x_rest", [P, TPC, D])
        ut = [sb(f"a_ut{i}", [P, CE], BF16) for i in range(2)]
        vt = [sb(f"a_vt{i}", [3 * D, CE], BF16) for i in range(2)]
        inside = sb("a_inside", [D + 1, CE])
        h_rep = [sb(f"a_h_rep{i}", [P, CE]) for i in range(2)]
        mp = [sb(f"a_mp{i}", [P, 2, CE]) for i in range(2)]
        q = [sb(f"a_q{i}", [P, CE]) for i in range(2)]
        relus = sb("a_relus", [P, 2, CE])
        exps = [sb(f"a_exps{i}", [P, 2, CE]) for i in range(2)]
        msg = [sb(f"a_msg{i}", [P, CE]) for i in range(2)]
        den = [sb(f"a_den{i}", [P, 2, CE]) for i in range(2)]
        num = [sb(f"a_num{i}", [P, 2, CE]) for i in range(2)]
        log_den = sb("a_log_den", [P, CE])
        inv_den = [sb(f"a_inv_den{i}", [P, CE]) for i in range(2)]
        ratio = [sb(f"a_ratio{i}", [P, CE]) for i in range(2)]
        attr_sum = [sb(f"a_attr_sum{i}", [D + 1, CE]) for i in range(2)]
        back = [sb(f"a_back{i}", [P, TPC, D + 1]) for i in range(2)]
        inv_count = sb("a_inv_count", [P, TPC, 1])
        rows = [sb(f"a_rows{i}", [P, TPC, 2 * D]) for i in range(2)]

        f_ps, h_ps, o_ps, attr_ps, wm_ps = ps("a_fps"), ps("a_hps"), ps("a_ops"), ps("a_attrps"), ps("a_wmps")
        t_ps = scratch.enter_context(nc.psum_tensor("a_tps", [P, 2, CE], BF16))
        wa_ps = [ps(f"a_waps{i}") for i in range(2)]

        ft_ps = o_ps[:, 0:TPC * D]
        back_ps = o_ps[:, 128:256].rearrange("p (t c) -> p t c", t=TPC)

        idx_staged, gathered = sem("a_idx_staged"), [sem(f"a_gathered{i}") for i in range(2)]
        split_steps, turned, ut_ready = sem("a_split_steps"), sem("a_turned"), sem("a_ut_ready")
        attr_picked = sem("a_attr_picked")
        start_spread, h_spread = sem("a_start_spread"), sem("a_h_spread")
        logits_projected, projected = sem("a_logits_projected"), sem("a_projected")
        inside_ready, h_ready = sem("a_inside_ready"), sem("a_h_ready")
        e2_done, carried, mp_done, q_done, msg_done = (
            sem("a_e2_done"), sem("a_carried"), sem("a_mp_done"), sem("a_q_done"), sem("a_msg_done"))
        relu_done, exp_done = sem("a_relu_done"), sem("a_exp_done")
        den_done, weighted, num_done = sem("a_den_done"), sem("a_weighted"), sem("a_num_done")
        log_done, inv_done, ratio_done = sem("a_log_done"), sem("a_inv_done"), sem("a_ratio_done")
        ft_done, attr_sum_done, turned_back = sem("a_ft_done"), sem("a_attr_sum_done"), sem("a_turned_back")
        inv_count_done, mean_done, ft_copied, back_copied = (
            sem("a_inv_count_done"), sem("a_mean_done"), sem("a_ft_copied"), sem("a_back_copied"))
        scattered = [sem(f"a_scattered{i}") for i in range(2)]
        first_zero, tables_zero, cleared = sem("a_first_zero"), sem("a_tables_zero"), sem("a_cleared")
        weights_in, edges_in = sem("a_weights_in"), sem("a_edges_in")

        block = scratch.enter_context(nc.Block())

        @block.sync
        def _(sp):
            flat = b.t_first.rearrange("(p j) c -> p (j c)", p=sh.NP)
            first = flat.shape[1] // b.zw // 2
            for k in range(first, 2 * first):
                sp.dma_start(flat[:, k * b.zw:(k + 1) * b.zw], b.zeros[0:sh.NP, :]).then_inc(first_zero, 16)
            sp.wait_ge(cleared, 7)
            k8 = P // D
            sp.dma_start(b.w_tp[:, :], io["L2_gnn_W_msg_tp"].rearrange("i j h -> (i j) h")).then_inc(weights_in, 16)
            for w, name in ((b.bd_lin, "L2_gnn_W_msg_lin"), (b.bd_upd, "L2_gnn_W_upd_lin"), (b.bd1a, "L3_gnn_w1a"),
                            (b.bd1b, "L3_gnn_w1b"), (b.bd2a, "L3_gnn_w2a"), (b.bd2b, "L3_gnn_w2b")):
                for k in range(k8):
                    sp.dma_start(w[k * D:(k + 1) * D, k * D:(k + 1) * D], io[name]).then_inc(weights_in, 16)
            for w, name in ((b.b1a, "L3_gnn_b1a"), (b.b2a, "L3_gnn_b2a")):
                for k in range(k8):
                    sp.dma_start(w[k * D:(k + 1) * D, :], io[name].rearrange("(c a) -> c a", a=1)).then_inc(weights_in, 16)
            for w, name, width in ((b.b1b, "L3_gnn_b1b", D), (b.b2b, "L3_gnn_b2b", D), (b.eps1, "L3_gnn_eps1", 1), (b.eps2, "L3_gnn_eps2", 1)):
                sp.dma_start(w[:, :], bass.AP(io[name].tensor, 0, [[0, P], [1, width]])).then_inc(weights_in, 16)
            n = 0
            per = sh.NJ * D
            for t in [*b.t_adds, b.t_seg1, b.t_seg2]:
                flat = t[0:sh.N, :].rearrange("(p j) c -> p (j c)", p=sh.NP)
                for k in range(per // b.zw):
                    sp.wait_ge(projected, min(2 * n + 2, S))
                    sp.dma_start(flat[:, k * b.zw:(k + 1) * b.zw], b.zeros[0:sh.NP, :]).then_inc(tables_zero, 16)
                    n += 1
            for t in b.t_adds:
                sp.dma_start(t[sh.N:sh.N + P, :], b.zeros[:, 0:D]).then_inc(tables_zero, 16)
                sp.dma_start(t[sh.N + P:sh.N + P + 1, :], b.zeros[0:1, 0:D]).then_inc(tables_zero, 16)
                n += 2
            a = io["edge_attr_8"]
            sp.dma_start(b.ea8[:, 0:sh.full, :], a[0:sh.full * P, :].rearrange("(t p) c -> p t c", p=P)).then_inc(edges_in, 16)
            sp.dma_start(b.ea8[0:sh.rest, sh.full, :], a[sh.full * P:sh.E, :]).then_inc(edges_in, 16)
            sp.wait_ge(first_zero, 16 * first)
            sp.wait_ge(tables_zero, 16 * n)
            sp.wait_ge(weights_in, 16 * (1 + 8 * k8 + 4))
            sp.wait_ge(edges_in, 16 * 2)

        @block.gpsimd
        def _(pool):
            def gather(c, u):
                pool.wait_ge(idx_staged, c + 1)
                waits_apart(pool)
                for k in range(TPC):
                    pool.indirect_dma_start(out=x_src[u][:, k, :], out_offset=None, in_=io["x"],
                                            in_offset=bass.IndirectOffsetOnAxis(ap=gather_idx[u][:, k:k + 1], axis=0),
                                            ).then_inc(gathered[u], 16)

            def scatter(c, u):
                pool.wait_ge(ft_copied, 2 * (c + 1))
                pool.wait_ge(mean_done, c + 1)
                waits_apart(pool)
                for k in range(TPC):
                    pool.indirect_dma_start(out=b.t_first, out_offset=bass.IndirectOffsetOnAxis(ap=scatter_idx[u][:, k:k + 1], axis=0),
                                            in_=rows[u][:, k, :], in_offset=None,
                                            bounds_check=sh.N - 1, oob_is_err=False).then_inc(scattered[u], 16)

            for w in (b.bd_lin, b.bd_upd, b.bd1a, b.bd1b, b.bd2a, b.bd2b):
                pool.memset(w[:, :], 0.0).then_inc(cleared, 1)
            pool.memset(b.ea8[:, sh.full:sh.tiles, :], 0.0).then_inc(cleared, 1)
            for c in range(2):
                gather(c, c)
            pool.wait_ge(first_zero, 16 * (sh.NJ * D // b.zw))

            def divide(s, u, h):
                pool.wait_ge(inv_done, s + 1)
                pool.wait_ge(num_done, s + 1)
                need(pool, ft_done, s - 1)
                pool.tensor_tensor(ratio[h][:, :], num[u][:, h, :], inv_den[h][:, :], ALU.mult).then_inc(ratio_done, 1)

            def body(c, u, pair):
                if there(c - 1, C):
                    divide(2 * c - 2, 1 - u, 0)
                if there(c + 2, C):
                    gather(c + 2, u)
                if there(c - 1, C):
                    divide(2 * c - 1, 1 - u, 1)
                if there(c - 2, C):
                    scatter(c - 2, u)

            chunk_loop(pool, C, body)
            for u in range(2):
                pool.wait_ge(scattered[u], 16 * TPC * (C // 2))

        @block.scalar
        def _(act):
            def stage_gather(c, u):
                need(act, split_steps, 4 * (c - 1))
                act.activation(gather_idx[u][:, :], b.gsrc[:, bass.ds(c * TPC, TPC)], ACT.Copy).then_inc(idx_staged, 1)

            def evacuate_turned(c, u):
                act.wait_ge(turned, c + 1)
                need(act, projected, 2 * (c - 1))
                act.activation(ut[u][:, :], t_ps[:, 0, :], ACT.Copy)
                act.activation(vt[u][:, :], t_ps[0:3 * D, 1, :], ACT.Copy).then_inc(ut_ready, 1)

            def copy_h(s, h):
                act.wait_ge(h_spread, s + 1)
                need(act, msg_done, s - 1)
                act.activation(h_rep[h][:, :], h_ps[:, :], ACT.Copy).then_inc(h_ready, 1)

            def copy_inside(c):
                need(act, attr_sum_done, c)
                act.wait_ge(start_spread, c + 1)
                act.activation(inside[:, :], f_ps[0:D + 1, :], ACT.Copy, scale=-1.0 / RESET, bias=1.0).then_inc(inside_ready, 1)

            def softmax_factors(s, h):
                act.wait_ge(q_done, s + 1)
                need(act, exp_done, s)
                act.activation(relus[:, 0, :], q[h][:, :], ACT.Relu).then_inc(relu_done, 1)
                act.activation(relus[:, 1, :], q[h][:, :], ACT.Relu, scale=-1.0).then_inc(relu_done, 1)
                act.wait_ge(relu_done, 2 * (s + 1))
                need(act, num_done, s - 1)
                act.activation(exps[h][:, :, :], relus[:, :, :], ACT.Exp, scale=-1.0).then_inc(exp_done, 1)

            def invert_den(s, u, h):
                act.wait_ge(den_done, s + 1)
                need(act, inv_done, s)
                act.activation(log_den[:, :], den[u][:, h, :], ACT.Ln).then_inc(log_done, 1)
                act.wait_ge(log_done, s + 1)
                need(act, ratio_done, s - 1)
                act.activation(inv_den[h][:, :], log_den[:, :], ACT.Exp, scale=-1.0).then_inc(inv_done, 1)

            def copy_ft(c, u, pair):
                act.wait_ge(ft_done, 2 * (c + 1))
                need(act, scattered[u], pair * (16 * TPC))
                act.activation(rows[u][:, :, 0:D], ft_ps.rearrange("p (t c) -> p t c", t=TPC), ACT.Copy).then_inc(ft_copied, 1)
                act.activation(scatter_idx[u][:, :], b.scat[:, bass.ds(c * TPC, TPC)], ACT.Copy).then_inc(ft_copied, 1)

            def copy_back(c, u):
                act.wait_ge(turned_back, c + 1)
                need(act, ft_done, 2 * c - 1)
                need(act, mean_done, c - 1)
                act.activation(back[u][:, :, :], back_ps[:, :, 0:D + 1], ACT.Copy).then_inc(back_copied, 1)

            act.preload_act_table_set("natural_log_exp_and_others")
            for c in range(3):
                stage_gather(c, c % 2)
            evacuate_turned(0, 0)
            copy_h(0, 0)
            copy_inside(0)

            def body(c, u, pair):
                for h in (0, 1):
                    s = c * 2 + h
                    if h == 0 and there(c - 1, C):
                        copy_back(c - 1, 1 - u)
                    if h == 1 and there(c - 2, C):
                        copy_ft(c - 2, u, pair - 1)
                    if there(s + 1, S):
                        copy_h(s + 1, 1 - h)
                    if there(s, S):
                        softmax_factors(s, h)
                    if h == 1 and there(c + 1, C):
                        copy_inside(c + 1)
                    if there(s - 1, S):
                        invert_den(s - 1, u if h else 1 - u, 1 - h)
                    if h == 0 and there(c + 1, C):
                        evacuate_turned(c + 1, 1 - u)
                if there(c + 3, C):
                    stage_gather(c + 3, 1 - u)

            chunk_loop(act, C, body)

        @block.tensor
        def _(pe):
            def turn(c, u):
                pe.wait_ge(split_steps, 4 * (c + 1))
                need(pe, ut_ready, c)
                waits_apart(pe)
                for k in range(TPC):
                    pe.transpose(t_ps[:, 0, k * P:(k + 1) * P], b.edges[:, bass.ds(c * TPC + k, 1), :].rearrange("p a c -> p (a c)"), b.ident_b[:, :])
                for k in range(TPC):
                    mm = pe.transpose(t_ps[0:3 * D, 1, k * P:(k + 1) * P], x_parts[u][:, k, :, :].rearrange("p a c -> p (a c)"), b.ident_b[:, :])
                mm.then_inc(turned, 1)

            def start_rows(c, u):
                pe.wait_ge(ut_ready, c + 1)
                need(pe, mp_done, 2 * c)
                need(pe, inside_ready, c)
                pe.matmul(f_ps[:, :], b.w_start[:, :], ut[u][:, :], start=True, stop=True).then_inc(start_spread, 1)
                need(pe, attr_sum_done, c)
                pe.matmul(attr_ps[0:D + 1, :], b.w_attr[:, :], ut[u][:, :], start=True, stop=True).then_inc(attr_picked, 1)

            def project_logits(c, u, s, h):
                cols = slice(h * P, (h + 1) * P)
                pe.wait_ge(ut_ready, c + 1)
                need(pe, h_ready, s)
                pe.matmul(h_ps[:, :], b.w_h[:, cols], vt[u][:, :], start=True, stop=True).then_inc(h_spread, 1)
                need(pe, e2_done, s - 1)
                pe.matmul(wa_ps[h][:, :], b.w_split[:, 0, cols], ut[u][:, :], start=True, stop=True).then_inc(logits_projected, 1)

            def project_messages(u, s, h):
                need(pe, msg_done, s)
                pe.matmul(wm_ps[:, :], b.w_split[:, 1, h * P:(h + 1) * P], ut[u][:, :], start=True, stop=True).then_inc(projected, 1)

            def sum_inputs(s, c, u, h):
                pe.wait_ge(ratio_done, s + 1)
                if h == 0:
                    need(pe, ft_copied, 2 * c)
                else:
                    need(pe, back_copied, c + 2 if not isinstance(c, int) or c + 2 <= C else C)
                for k in range(TPC):
                    mm = pe.matmul(ft_ps[:, k * D:(k + 1) * D], ratio[h][:, k * P:(k + 1) * P], b.sel[:, :],
                                   start=(h == 0 and k == 0), stop=(h == 1), skip_group_check=True)
                mm.then_inc(ft_done, 1)

            def turn_sums_back(c, u):
                pe.wait_ge(attr_sum_done, c + 1)
                need(pe, ft_copied, 2 * (c - 1))
                waits_apart(pe)
                for k in range(TPC):
                    mm = pe.transpose(back_ps[:, k, 0:D + 1], attr_sum[u][:, k * P:(k + 1) * P], b.ident[0:D + 1, 0:D + 1])
                mm.then_inc(turned_back, 1)

            turn(0, 0)
            project_logits(0, 0, 0, 0)
            project_messages(0, 0, 0)
            start_rows(0, 0)

            def body(c, u, pair):
                for h in (0, 1):
                    s = c * 2 + h
                    if there(s + 1, S):
                        project_logits(c + h, 1 - u if h else u, s + 1, 1 - h)
                        project_messages(1 - u if h else u, s + 1, 1 - h)
                    if h == 1 and there(c + 1, C):
                        start_rows(c + 1, 1 - u)
                    if h == 0 and there(c + 1, C):
                        turn(c + 1, 1 - u)
                    if h == 1 and there(c, C):
                        turn_sums_back(c, u)
                    if there(s - 3, S):
                        if h == 0:
                            sum_inputs(s - 3, c - 2, u, 1)
                        else:
                            sum_inputs(s - 3, c - 1, 1 - u, 0)

            chunk_loop(pe, C, body)

        @block.vector
        def _(dve):
            def logits_and_maximum(c, u, s, h):
                dve.wait_ge(h_ready, s + 1)
                dve.wait_ge(logits_projected, s + 1)
                dve.tensor_tensor(b.e2[u][:, h, 1:CE + 1], wa_ps[h][:, :], h_rep[h][:, :], ALU.mult).then_inc(e2_done, 1)
                need(dve, num_done, s - 1)
                dve.wait_ge(projected, s + 1)
                dve.tensor_tensor(msg[h][:, :], wm_ps[:, :], h_rep[h][:, :], ALU.mult).then_inc(msg_done, 1)
                dve.wait_ge(e2_done, s + 1)
                dve.wait_ge(inside_ready, c + 1)
                need(dve, carried, s - 1)
                dve.tensor_tensor_scan(mp[u][:, h, :], b.e2[u][:, h, 0:CE], f_ps[:, :],
                                       0.0 if isinstance(c, int) and c == 0 else mp[1 - u][:, h, CE - 1:CE],
                                       ALU.max, ALU.add).then_inc(mp_done, 1)
                need(dve, mp_done, s - 1)
                dve.tensor_copy(b.e2[1 - u][:, h, 0:1], b.e2[u][:, h, CE:CE + 1]).then_inc(carried, 1)
                dve.wait_ge(mp_done, s + 1)
                need(dve, relu_done, 2 * (s - 1))
                dve.tensor_tensor(q[h][:, :], mp[u][:, h, :], b.e2[u][:, h, 1:CE + 1], ALU.subtract).then_inc(q_done, 1)

            def parts_of(u):
                return [x_parts[u][:, :, k, :] for k in range(3)]

            def split_x_first(c, u, pair):
                dve.wait_ge(gathered[u], (pair + 1) * (16 * TPC))
                need(dve, turned, c - 1)
                need(dve, split_steps, 4 * c)
                split_first(dve, parts_of(u), x_src[u][:, :, :], split_steps)

            def split_x_others(c, u):
                split_others(dve, parts_of(u), x_rest[:, :, :], x_src[u][:, :, :], split_steps, c * 4)

            def sums(c, u, s, h):
                first = isinstance(c, int) and c == 0
                dve.wait_ge(exp_done, s + 1)
                dve.wait_ge(msg_done, s + 1)
                dve.tensor_tensor(msg[h][:, :], msg[h][:, :], exps[h][:, 0, :], ALU.mult).then_inc(weighted, 1)
                need(dve, den_done, s - 1)
                dve.tensor_tensor_scan(den[u][:, h, :], exps[h][:, 1, :], exps[h][:, 0, :],
                                       0.0 if first else den[1 - u][:, h, CE - 1:CE],
                                       ALU.mult, ALU.add).then_inc(den_done, 1)
                dve.wait_ge(weighted, s + 1)
                need(dve, num_done, s - 1)
                need(dve, ratio_done, s - 3)
                dve.tensor_tensor_scan(num[u][:, h, :], exps[h][:, 1, :], msg[h][:, :],
                                       0.0 if first else num[1 - u][:, h, CE - 1:CE],
                                       ALU.mult, ALU.add).then_inc(num_done, 1)

            def attribute_sums(c, u):
                dve.wait_ge(inside_ready, c + 1)
                dve.wait_ge(attr_picked, c + 1)
                need(dve, turned_back, c - 1)
                need(dve, attr_sum_done, c)
                dve.tensor_tensor_scan(attr_sum[u][:, :], inside[:, :], attr_ps[0:D + 1, :],
                                       0.0 if isinstance(c, int) and c == 0 else attr_sum[1 - u][:, CE - 1:CE],
                                       ALU.mult, ALU.add).then_inc(attr_sum_done, 1)

            def invert_count(c, u):
                dve.wait_ge(back_copied, c + 1)
                need(dve, mean_done, c)
                dve.reciprocal(inv_count[:, :, :], back[u][:, :, D:D + 1]).then_inc(inv_count_done, 1)

            def attribute_mean(c, u, pair):
                dve.wait_ge(inv_count_done, c + 1)
                need(dve, scattered[u], pair * (16 * TPC))
                dve.tensor_tensor(rows[u][:, :, D:2 * D], back[u][:, :, 0:D],
                                  inv_count[:, :, :].broadcast_to([P, TPC, D]), ALU.mult).then_inc(mean_done, 1)

            def body(c, u, pair):
                for h in (0, 1):
                    s = c * 2 + h
                    if there(s, S):
                        logits_and_maximum(c, u, s, h)
                    if h == 0 and there(c + 1, C):
                        split_x_first(c + 1, 1 - u, pair if u == 0 else pair + 1)
                    if h == 0 and there(c, C):
                        attribute_sums(c, u)
                    if h == 0 and there(c + 1, C):
                        split_x_others(c + 1, 1 - u)
                    if h == 1 and there(c - 1, C):
                        invert_count(c - 1, 1 - u)
                    if there(s - 1, S):
                        if h == 0:
                            sums(c - 1, 1 - u, s - 1, 1)
                        else:
                            sums(c, u, s - 1, 0)
                    if h == 1 and there(c - 1, C):
                        attribute_mean(c - 1, 1 - u, pair if u else pair - 1)

            split_x_first(0, 0, 0)
            split_x_others(0, 0)
            chunk_loop(dve, C, body)


def message_layer(nc, sems, sh, b, io):
    def sem(name):
        return sems.enter(name)

    C = sh.chunks
    W = TPC * D
    with ExitStack() as scratch:
        def sb(name, shape, dt=F32):
            return scratch.enter_context(nc.sbuf_tensor(name, shape, dt))

        def ps(name):
            return scratch.enter_context(nc.psum_tensor(name, [P, 512], F32))

        gather_idx = [sb(f"m_gather_idx{i}", [P, TPC], U32) for i in range(2)]
        add_idx = [sb(f"m_add_idx{i}", [P, TPC], U32) for i in range(2)]
        x_dst = [sb(f"m_x_dst{i}", [P, TPC, D]) for i in range(2)]
        z = [sb(f"m_z{i}", [P, TPC, D, DE]) for i in range(2)]
        zt = [sb(f"m_zt{i}", [P, CE]) for i in range(2)]
        act_m = [sb(f"m_act{i}", [P, W]) for i in range(2)]
        act_mt = [sb(f"m_act_t{i}", [W, P]) for i in range(2)]
        m = [sb(f"m_m{i}", [P, W]) for i in range(2)]
        sums = [sb(f"m_sums{i}", [P, TPC, D]) for i in range(2)]
        src = [sb(f"m_src{i}", [P, TPC]) for i in range(2)]
        equal = [sb(f"m_equal{i}", [P, TPC, P]) for i in range(2)]
        earlier = sb("m_earlier", [P, TPC, P])
        before = sb("m_before", [P, TPC])
        to_dummy = sb("m_to_dummy", [P, TPC])
        shift = sb("m_shift", [P, TPC])
        target = [sb(f"m_target{i}", [P, TPC]) for i in range(2)]

        z_ps = [ps(f"m_zps{i}") for i in range(2)]
        src_ps, pre_ps, t_ps, m_ps, sum_ps = ps("m_srcps"), ps("m_preps"), ps("m_tps"), ps("m_mps"), ps("m_sumps")

        idx_staged, gathered = sem("m_idx_staged"), [sem(f"m_gathered{i}") for i in range(2)]
        z_done, z_turned, zt_ready, pre_done, act_done = (
            sem("m_z_done"), sem("m_z_turned"), sem("m_zt_ready"), sem("m_pre_done"), sem("m_act_done"))
        act_turned, act_t_ready, m_done, m_ready = sem("m_act_turned"), sem("m_act_t_ready"), sem("m_m_done"), sem("m_m_ready")
        src_staged, src_spread, equal_done = sem("m_src_staged"), sem("m_src_spread"), sem("m_equal_done")
        earlier_done, before_done, dummy_done, shift_done, add_idx_ready = (
            sem("m_earlier_done"), sem("m_before_done"), sem("m_dummy_done"), sem("m_shift_done"), sem("m_add_idx_ready"))
        target_done = sem("m_target_done")
        summed, sums_ready = sem("m_summed"), sem("m_sums_ready")
        added = [sem(f"m_added{k}") for k in range(TPC)]

        block = scratch.enter_context(nc.Block())

        @block.gpsimd
        def _(pool):
            def gather(c, u):
                pool.wait_ge(idx_staged, c + 1)
                waits_apart(pool)
                for k in range(TPC):
                    pool.indirect_dma_start(out=x_dst[u][:, k, :], out_offset=None, in_=b.t_x,
                                            in_offset=bass.IndirectOffsetOnAxis(ap=gather_idx[u][:, k:k + 1], axis=0),
                                            ).then_inc(gathered[u], 16)

            def add(c, u):
                pool.wait_ge(sums_ready, c + 1)
                pool.wait_ge(add_idx_ready, c + 1)
                for k in range(TPC):
                    need(pool, added[k], c * 16)
                    waits_apart(pool)
                    pool.indirect_dma_start(out=b.t_adds[k], out_offset=bass.IndirectOffsetOnAxis(ap=add_idx[u][:, k:k + 1], axis=0),
                                            in_=sums[u][:, k, :], in_offset=None, compute_op=ALU.add,
                                            ).then_inc(added[k], 16)

            for c in range(2):
                gather(c, c)

            def body(c, u, pair):
                if there(c - 2, C):
                    add(c - 2, u)
                if there(c + 2, C):
                    gather(c + 2, u)

            chunk_loop(pool, C, body)
            for k in range(TPC):
                pool.wait_ge(added[k], 16 * C)

        @block.scalar
        def _(act):
            def stage_gather(c, u):
                need(act, z_done, c - 1)
                act.activation(gather_idx[u][:, :], b.gdst[:, bass.ds(c * TPC, TPC)], ACT.Copy).then_inc(idx_staged, 1)

            def stage_src(c, u):
                need(act, target_done, c - 1)
                need(act, src_spread, c - 1)
                act.activation(src[u][:, :], b.srcf[:, bass.ds(c * TPC, TPC)], ACT.Copy).then_inc(src_staged, 1)

            def early(c, u):
                act.wait_ge(z_turned, c + 1)
                need(act, pre_done, c - 1)
                act.activation(zt[u][:, :], z_ps[u][:, :], ACT.Copy).then_inc(zt_ready, 1)

            def turn(c, u):
                act.wait_ge(act_turned, c + 1)
                need(act, m_done, c - 1)
                act.activation(act_mt[u][:, :], t_ps[0:W, 0:P], ACT.Copy).then_inc(act_t_ready, 1)

            def silu(c, u):
                act.wait_ge(pre_done, c + 1)
                need(act, act_turned, c - 1)
                act.activation(act_m[u][:, :], pre_ps[:, 0:W], ACT.Silu, scale=float(D * DE) ** -0.5).then_inc(act_done, 1)

            def late(c, u):
                act.wait_ge(m_done, c + 1)
                need(act, summed, c - 1)
                act.activation(m[u][:, :], m_ps[:, 0:W], ACT.Copy, scale=float(D) ** -0.5).then_inc(m_ready, 1)
                act.wait_ge(summed, c + 1)
                for k in range(TPC):
                    need(act, added[k], (c - 1) * 16)
                act.activation(sums[u][:, :, :], sum_ps[:, 0:W].rearrange("p (t c) -> p t c", t=TPC), ACT.Copy).then_inc(sums_ready, 1)
                act.wait_ge(target_done, c + 1)
                act.activation(add_idx[u][:, :], target[u][:, :], ACT.Copy).then_inc(add_idx_ready, 1)

            for c in range(2):
                stage_gather(c, c)
                stage_src(c, c)

            def body(c, u, pair):
                if there(c, C):
                    early(c, u)
                if there(c + 2, C):
                    stage_gather(c + 2, u)
                if there(c - 1, C):
                    turn(c - 1, 1 - u)
                if there(c, C):
                    silu(c, u)
                if there(c - 1, C):
                    late(c - 1, 1 - u)
                if there(c + 2, C):
                    stage_src(c + 2, u)

            chunk_loop(act, C, body)

        @block.tensor
        def _(pe):
            def spread_src(c, u):
                pe.wait_ge(src_staged, c + 1)
                need(pe, equal_done, TPC * c)
                for k in range(TPC):
                    mm = pe.matmul(src_ps[:, k * P:(k + 1) * P], src[u][:, k:k + 1].broadcast_to([P, P]), b.ident[:, :],
                                   start=True, stop=True)
                mm.then_inc(src_spread, 1)

            def turn_z(c, u):
                pe.wait_ge(z_done, c + 1)
                need(pe, zt_ready, c - 1)
                waits_apart(pe)
                for k in range(TPC):
                    mm = pe.transpose(z_ps[u][:, k * P:(k + 1) * P], z[u][:, k, :, :].rearrange("p i j -> p (i j)"), b.ident[:, :])
                mm.then_inc(z_turned, 1)

            def mix(c, u):
                pe.wait_ge(zt_ready, c + 1)
                need(pe, act_done, c)
                for k in range(TPC):
                    mm = pe.matmul(pre_ps[:, k * D:(k + 1) * D], zt[u][:, k * P:(k + 1) * P], b.w_tp[:, :], start=True, stop=True)
                mm.then_inc(pre_done, 1)

            def turn_act(c, u):
                pe.wait_ge(act_done, c + 1)
                need(pe, act_t_ready, c)
                waits_apart(pe)
                pe.transpose(t_ps[0:W, 0:P], act_m[u][:, :], b.ident[:, :]).then_inc(act_turned, 1)

            def linear(c, u):
                pe.wait_ge(act_t_ready, c + 1)
                need(pe, m_ready, c)
                pe.matmul(m_ps[:, 0:W], act_mt[u][:, :], b.bd_lin[0:W, 0:W], start=True, stop=True).then_inc(m_done, 1)

            def sum_equal(c, u):
                pe.wait_ge(m_ready, c + 1)
                pe.wait_ge(equal_done, TPC * (c + 1))
                need(pe, sums_ready, c)
                for k in range(TPC):
                    mm = pe.matmul(sum_ps[:, k * D:(k + 1) * D], equal[u][:, k, :], m[u][:, k * D:(k + 1) * D], start=True, stop=True)
                mm.then_inc(summed, 1)

            def body(c, u, pair):
                if there(c, C):
                    turn_z(c, u)
                    spread_src(c, u)
                if there(c - 1, C):
                    turn_act(c - 1, 1 - u)
                if there(c, C):
                    mix(c, u)
                if there(c - 1, C):
                    linear(c - 1, 1 - u)
                    sum_equal(c - 1, 1 - u)

            chunk_loop(pe, C, body)

        @block.vector
        def _(dve):
            def body(c, u, pair):
                if not there(c, C):
                    return
                dve.wait_ge(gathered[u], (pair + 1) * (16 * TPC))
                need(dve, z_turned, c - 1)
                dve.tensor_tensor(z[u][:, :, :, :], x_dst[u][:, :, :].unsqueeze(3).broadcast_to([P, TPC, D, DE]),
                                  b.ea8[:, bass.ds(c * TPC, TPC), :].unsqueeze(2).broadcast_to([P, TPC, D, DE]),
                                  ALU.mult).then_inc(z_done, 1)
                dve.wait_ge(src_spread, c + 1)
                need(dve, summed, c - 1)
                for k in range(TPC):
                    dve.tensor_scalar(equal[u][:, k, :], src_ps[:, k * P:(k + 1) * P], src[u][:, k:k + 1], None,
                                      ALU.is_equal).then_inc(equal_done, 1)
                dve.tensor_scalar(to_dummy[:, :], src[u][:, :], -1.0, b.dummy[:, 0:1], ALU.mult, ALU.add).then_inc(dummy_done, 1)
                dve.wait_ge(equal_done, TPC * (c + 1))
                dve.tensor_tensor(earlier[:, :, :], equal[u][:, :, :], b.lower[:, :].unsqueeze(1).broadcast_to([P, TPC, P]),
                                  ALU.mult).then_inc(earlier_done, 1)
                dve.wait_ge(earlier_done, c + 1)
                dve.tensor_reduce(before[:, :], earlier[:, :, :], AX.X, ALU.add).then_inc(before_done, 1)
                dve.wait_ge(before_done, c + 1)
                dve.wait_ge(dummy_done, c + 1)
                dve.scalar_tensor_tensor(shift[:, :], before[:, :], 1.0, to_dummy[:, :], ALU.min, ALU.mult).then_inc(shift_done, 1)
                dve.wait_ge(shift_done, c + 1)
                need(dve, add_idx_ready, c - 1)
                dve.tensor_tensor(target[u][:, :], shift[:, :], src[u][:, :], ALU.add).then_inc(target_done, 1)

            chunk_loop(dve, C, body)


def neighbour_sums(nc, sems, sh, b, name, table_in, table_out):
    def sem(what):
        return sems.enter(name + what)

    C = sh.chunks
    with ExitStack() as scratch:
        def sb(what, shape, dt=F32):
            return scratch.enter_context(nc.sbuf_tensor(name + what, shape, dt))

        def ps(what):
            return scratch.enter_context(nc.psum_tensor(name + what, [P, 512], F32))

        gather_idx = [sb(f"gather_idx{i}", [P, TPC], U32) for i in range(2)]
        scatter_idx = [sb(f"scatter_idx{i}", [P, TPC], U32) for i in range(2)]
        x_src = [sb(f"x_src{i}", [P, TPC, D]) for i in range(2)]
        mask = [sb(f"mask{i}", [P, TPC, D]) for i in range(2)]
        inside = [sb(f"inside{i}", [D, CE]) for i in range(2)]
        run = [sb(f"run{i}", [D, CE]) for i in range(2)]
        rows = [sb(f"rows{i}", [P, TPC, D]) for i in range(2)]
        x_ps = [ps(f"x_ps{i}") for i in range(2)]
        mask_ps = [ps(f"mask_ps{i}") for i in range(2)]
        back_ps = [ps(f"back_ps{i}") for i in range(2)]
        idx_staged, gathered = sem("idx_staged"), [sem(f"gathered{i}") for i in range(2)]
        mask_staged, mask_turned, inside_ready = sem("mask_staged"), sem("mask_turned"), sem("inside_ready")
        x_turned, run_done, turned_back, rows_ready = sem("x_turned"), sem("run_done"), sem("turned_back"), sem("rows_ready")
        scattered = [sem(f"scattered{i}") for i in range(2)]

        block = scratch.enter_context(nc.Block())

        @block.gpsimd
        def _(pool):
            def gather(c, u):
                pool.wait_ge(idx_staged, c + 1)
                waits_apart(pool)
                for k in range(TPC):
                    pool.indirect_dma_start(out=x_src[u][:, k, :], out_offset=None, in_=table_in,
                                            in_offset=bass.IndirectOffsetOnAxis(ap=gather_idx[u][:, k:k + 1], axis=0),
                                            ).then_inc(gathered[u], 16)

            for c in range(2):
                gather(c, c)

            def body(c, u, pair):
                if there(c + 2, C):
                    gather(c + 2, u)
                if there(c - 1, C):
                    pool.wait_ge(rows_ready, 2 * c)
                    waits_apart(pool)
                    for k in range(TPC):
                        pool.indirect_dma_start(out=table_out, out_offset=bass.IndirectOffsetOnAxis(ap=scatter_idx[1 - u][:, k:k + 1], axis=0),
                                                in_=rows[1 - u][:, k, :], in_offset=None,
                                                bounds_check=sh.N - 1, oob_is_err=False).then_inc(scattered[1 - u], 16)

            chunk_loop(pool, C, body)
            for u in range(2):
                pool.wait_ge(scattered[u], 16 * TPC * (C // 2))

        @block.scalar
        def _(act):
            def stage(c, u):
                need(act, x_turned, c - 1)
                act.activation(gather_idx[u][:, :], b.gsrc[:, bass.ds(c * TPC, TPC)], ACT.Copy).then_inc(idx_staged, 1)
                need(act, mask_turned, c - 1)
                act.activation(mask[u][:, :, :], b.start[:, bass.ds(c * TPC, TPC)].unsqueeze(2).broadcast_to([P, TPC, D]),
                               ACT.Copy, scale=-1.0, bias=1.0).then_inc(mask_staged, 1)

            def mask_out(c, u):
                act.wait_ge(mask_turned, c + 1)
                need(act, run_done, c - 1)
                act.activation(inside[u][:, :], mask_ps[u][0:D, :], ACT.Copy).then_inc(inside_ready, 1)

            def rows_out(c, u, pair):
                act.wait_ge(turned_back, c + 1)
                need(act, scattered[u], pair * (16 * TPC))
                act.activation(rows[u][:, :, :], back_ps[u][:, 0:TPC * D].rearrange("p (t c) -> p t c", t=TPC), ACT.Copy).then_inc(rows_ready, 1)
                act.activation(scatter_idx[u][:, :], b.scat[:, bass.ds(c * TPC, TPC)], ACT.Copy).then_inc(rows_ready, 1)

            for c in range(2):
                stage(c, c)

            def body(c, u, pair):
                if there(c, C):
                    mask_out(c, u)
                if there(c + 2, C):
                    stage(c + 2, u)
                if there(c, C):
                    rows_out(c, u, pair)

            chunk_loop(act, C, body)

        @block.tensor
        def _(pe):
            def body(c, u, pair):
                if not there(c, C):
                    return
                pe.wait_ge(mask_staged, c + 1)
                need(pe, inside_ready, c - 1)
                waits_apart(pe)
                for k in range(TPC):
                    mm = pe.transpose(mask_ps[u][0:D, k * P:(k + 1) * P], mask[u][:, k, :], b.ident[:, :])
                mm.then_inc(mask_turned, 1)
                pe.wait_ge(gathered[u], (pair + 1) * (16 * TPC))
                need(pe, run_done, c - 1)
                waits_apart(pe)
                for k in range(TPC):
                    mm = pe.transpose(x_ps[u][0:D, k * P:(k + 1) * P], x_src[u][:, k, :], b.ident[:, :])
                mm.then_inc(x_turned, 1)
                pe.wait_ge(run_done, c + 1)
                need(pe, rows_ready, 2 * (c - 1))
                waits_apart(pe)
                for k in range(TPC):
                    mm = pe.transpose(back_ps[u][:, k * D:(k + 1) * D], run[u][:, k * P:(k + 1) * P], b.ident[0:D, 0:D])
                mm.then_inc(turned_back, 1)

            chunk_loop(pe, C, body)

        @block.vector
        def _(dve):
            def body(c, u, pair):
                if not there(c, C):
                    return
                dve.wait_ge(x_turned, c + 1)
                dve.wait_ge(inside_ready, c + 1)
                need(dve, turned_back, c - 1)
                need(dve, run_done, c)
                dve.tensor_tensor_scan(run[u][:, :], inside[u][:, :], x_ps[u][0:D, :],
                                       0.0 if isinstance(c, int) and c == 0 else run[1 - u][:, CE - 1:CE],
                                       ALU.mult, ALU.add).then_inc(run_done, 1)

            chunk_loop(dve, C, body)


INPUTS = ["x", "src", "dst", "edge_attr_16", "edge_attr_8", "node_vec1", "L0_gnn_W_msg", "L0_gnn_b_msg",
          "L0_gnn_W_attn", "L0_gnn_b_attn", "L2_gnn_W_msg_tp", "L2_gnn_W_msg_lin", "L2_gnn_W_upd_tp",
          "L2_gnn_W_upd_lin", "L3_gnn_eps1", "L3_gnn_w1a", "L3_gnn_b1a", "L3_gnn_w1b", "L3_gnn_b1b",
          "L3_gnn_eps2", "L3_gnn_w2a", "L3_gnn_b2a", "L3_gnn_w2b", "L3_gnn_b2b"]
class Norm:

    def __init__(self, nc, sems, scratch, name, np_, nj):
        def sb(what, shape):
            return scratch.enter_context(nc.sbuf_tensor(name + what, shape, F32))

        def sem(what):
            return sems.enter(name + what)

        self.shape = [np_, nj, D]
        self.total, self.var, self.log_var, self.rstd = (sb(w, [np_, nj]) for w in ("total", "var", "log_var", "rstd"))
        self.centred, self.square = sb("centred", self.shape), sb("square", self.shape)
        self.total_done, self.centred_done, self.square_done, self.var_done = (
            sem("total_done"), sem("centred_done"), sem("square_done"), sem("var_done"))
        self.log_done, self.rstd_done, self.done = sem("log_done"), sem("rstd_done"), sem("done")

    def centre(self, dve, n, x):
        dve.tensor_reduce(self.total[:, :], x, AX.X, ALU.add).then_inc(self.total_done, 1)
        dve.wait_ge(self.total_done, n + 1)
        need(dve, self.done, n)
        dve.scalar_tensor_tensor(self.centred[:, :, :], self.total[:, :].unsqueeze(2).broadcast_to(self.shape), -1.0 / D, x,
                                 ALU.mult, ALU.add).then_inc(self.centred_done, 1)

    def square_up(self, act, n):
        act.wait_ge(self.centred_done, n + 1)
        need(act, self.var_done, n)
        act.activation(self.square[:, :, :], self.centred[:, :, :], ACT.Square).then_inc(self.square_done, 1)

    def variance(self, dve, n):
        dve.wait_ge(self.square_done, n + 1)
        dve.tensor_reduce(self.var[:, :], self.square[:, :, :], AX.X, ALU.add).then_inc(self.var_done, 1)

    def scale(self, dve, n, out):
        dve.wait_ge(self.rstd_done, n + 1)
        dve.tensor_tensor(out, self.centred[:, :, :], self.rstd[:, :].unsqueeze(2).broadcast_to(self.shape), ALU.mult).then_inc(self.done, 1)

    def deviation(self, act, n, eps_col):
        act.wait_ge(self.var_done, n + 1)
        act.activation(self.log_var[:, :], self.var[:, :], ACT.Ln, bias=eps_col, scale=1.0 / D).then_inc(self.log_done, 1)
        act.wait_ge(self.log_done, n + 1)
        act.activation(self.rstd[:, :], self.log_var[:, :], ACT.Exp, scale=-0.5).then_inc(self.rstd_done, 1)


def first_norms(nc, sems, sh, b, io):
    def sem(name):
        return sems.enter(name)

    J = 40
    B = 2
    I = sh.NJ // (J * B)
    NP = sh.NP
    with ExitStack() as scratch:
        def sb(name, shape):
            return scratch.enter_context(nc.sbuf_tensor(name, shape, F32))

        agg = [sb(f"n1_agg{i}", [NP, B, J, 2 * D]) for i in range(2)]
        y = [[sb(f"n1_y{i}_{k}", [NP, J, D]) for k in range(B)] for i in range(2)]
        y2 = [sb(f"n1_y2_{k}", [NP, J, D]) for k in range(B)]
        norms = [Norm(nc, sems, scratch, f"n1_{k}_", NP, J) for k in range(B)]
        last = [Norm(nc, sems, scratch, f"n1_last{k}_", NP, J) for k in range(B)]
        agg_in = [sem(f"n1_agg_in{i}") for i in range(2)]
        summed, summed_again, stored, eps_done = sem("n1_summed"), sem("n1_summed_again"), sem("n1_stored"), sem("n1_eps_done")
        table = b.t_first.rearrange("(p j) c -> p j c", p=NP)
        x_in = io["x"].rearrange("(p j) c -> p j c", p=NP)
        out = b.t_x.rearrange("(p j) c -> p j c", p=NP)
        xn = b.xn[0:NP, :].rearrange("p (j c) -> p j c", c=D)
        block = scratch.enter_context(nc.Block())

        @block.sync
        def _(sp):
            def load(i, u):
                need(sp, summed_again, B * (i - 1))
                sp.dma_start(agg[u][:, :, :, :], table[:, bass.ds(i * (B * J), B * J), :].rearrange("p (b j) c -> p b j c", b=B)).then_inc(agg_in[u], 16)
                sp.dma_start(xn[:, bass.ds(i * (B * J), B * J), :], x_in[:, bass.ds(i * (B * J), B * J), :]).then_inc(agg_in[u], 16)

            for i in range(2):
                load(i, i)

            def body(i, u, pair):
                if there(i - 1, I):
                    for norm in last:
                        sp.wait_ge(norm.done, i)
                    sp.dma_start(out[:, bass.ds((i - 1) * (B * J), B * J), :], xn[:, bass.ds((i - 1) * (B * J), B * J), :]).then_inc(stored, 16)
                if there(i + 2, I):
                    load(i + 2, u)

            chunk_loop(sp, I, body)
            sp.wait_ge(stored, 16 * I)

        @block.gpsimd
        def _(pool):
            def first(i, u, pair):
                pool.wait_ge(agg_in[u], (pair + 1) * 32)
                for k in range(B):
                    need(pool, summed_again, B * (i - 2) + k + 1)
                    pool.tensor_tensor(y[u][k][:, :, :], xn[:, bass.ds(i * (B * J) + k * J, J), :], agg[u][:, k, :, 0:D],
                                       ALU.add).then_inc(summed, 1)

            def second(i, u):
                for k in range(B):
                    pool.wait_ge(norms[k].done, i + 1)
                    need(pool, last[k].centred_done, i)
                    pool.tensor_tensor(y2[k][:, :, :], y[u][k][:, :, :], agg[u][:, k, :, D:2 * D], ALU.add).then_inc(summed_again, 1)

            first(0, 0, 0)

            def body(i, u, pair):
                if there(i + 1, I):
                    first(i + 1, 1 - u, pair if u == 0 else pair + 1)
                if there(i, I):
                    second(i, u)

            chunk_loop(pool, I, body)

        @block.vector
        def _(dve):
            for eps in (b.eps1, b.eps2):
                dve.tensor_scalar(eps[:, :], eps[:, :], 1.0, None, ALU.add).then_inc(eps_done, 1)

            def body(i, u, pair):
                for k in range(B):
                    if there(i, I):
                        dve.wait_ge(summed, B * i + k + 1)
                        norms[k].centre(dve, i, y[u][k][:, :, :])
                for k in range(B):
                    if there(i - 1, I):
                        dve.wait_ge(summed_again, B * (i - 1) + k + 1)
                        last[k].centre(dve, i - 1, y2[k][:, :, :])
                for k in range(B):
                    if there(i, I):
                        norms[k].variance(dve, i)
                for k in range(B):
                    if there(i - 1, I):
                        last[k].variance(dve, i - 1)
                for k in range(B):
                    if there(i, I):
                        norms[k].scale(dve, i, y[u][k][:, :, :])
                for k in range(B):
                    if there(i - 1, I):
                        last[k].scale(dve, i - 1, xn[:, bass.ds((i - 1) * (B * J) + k * J, J), :])

            chunk_loop(dve, I, body)

        @block.scalar
        def _(act):
            act.preload_act_table_set("natural_log_exp_and_others")

            def body(i, u, pair):
                for step in ("square_up", "deviation"):
                    for group, n in ((norms, i), (last, i - 1)):
                        for norm in group:
                            if there(n, I):
                                if step == "square_up":
                                    norm.square_up(act, n)
                                else:
                                    norm.deviation(act, n, b.eps_col[0:NP, :])

            chunk_loop(act, I, body)


def update_nodes(nc, sems, sh, b, io):
    def sem(name):
        return sems.enter(name)

    J = 16
    I = sh.NJ // J
    NP = sh.NP
    GROUPS = J // 2
    BANKS = 4
    with ExitStack() as scratch:
        def sb(name, shape, dt=F32):
            return scratch.enter_context(nc.sbuf_tensor(name, shape, dt))

        def ps(name, shape=(P, 512), dt=F32):
            return scratch.enter_context(nc.psum_tensor(name, list(shape), dt))

        parts = [sb(f"n2_parts{i}", [NP, TPC, J * D]) for i in range(2)]
        pairs, agg = sb("n2_pairs", [NP, 2, J * D]), [sb(f"n2_agg{i}", [NP, J, D]) for i in range(2)]
        x_parts = sb("n2_x_parts", [NP, J, len(PARTS), D], BF16)
        x_rest = sb("n2_x_rest", [NP, J, D])
        xt = [sb(f"n2_xt{i}", [ROWS, J * P], BF16) for i in range(2)]
        product = [sb(f"n2_product{i}", [NP, J, D, D]) for i in range(2)]
        early_half, late_half = sb("n2_early_half", [NP, J // 2, D // 2, D]), sb("n2_late_half", [NP, J // 2, D // 2, D])
        quarter = sb("n2_quarter", [NP, J // 2, D // 4, D])
        mixed, act_u = sb("n2_mixed", [NP, J * D]), sb("n2_act", [NP, J * D])
        act_ut = sb("n2_act_t", [P, 2, NP])
        y = sb("n2_y", [NP, J, D])
        norm = Norm(nc, sems, scratch, "n2_", NP, J)
        xt_ps = ps("n2_xtps", (ROWS, J * P), BF16)
        y_ps = [ps(f"n2_yps{i}") for i in range(BANKS)]
        t_ps, v_ps = ps("n2_tps"), ps("n2_vps")
        parts_in = [sem(f"n2_parts_in{i}") for i in range(2)]
        pairs_done, agg_done = sem("n2_pairs_done"), sem("n2_agg_done")
        first_done, rest_done, second_done, third_done = (
            sem("n2_first_done"), sem("n2_rest_done"), sem("n2_second_done"), sem("n2_third_done"))
        x_turned, xt_ready, group_done, product_done = sem("n2_x_turned"), sem("n2_xt_ready"), sem("n2_group_done"), sem("n2_product_done")
        early_half_done, late_half_done = sem("n2_early_half_done"), sem("n2_late_half_done")
        quarter_done, mixed_done = sem("n2_quarter_done"), sem("n2_mixed_done")
        act_done, act_turned, act_t_ready, v_done = sem("n2_act_done"), sem("n2_act_turned"), sem("n2_act_t_ready"), sem("n2_v_done")
        y_done, stored = sem("n2_y_done"), sem("n2_stored")
        tables = [t[0:sh.N, :].rearrange("(p j) c -> p (j c)", p=NP) for t in b.t_adds]
        out = b.t_x.rearrange("(p j) c -> p j c", p=NP)
        xn = b.xn[0:NP, :].rearrange("p (j c) -> p j c", c=D)
        block = scratch.enter_context(nc.Block())

        @block.sync
        def _(sp):
            def load(i, u):
                need(sp, pairs_done, i - 1)
                for k in range(TPC):
                    sp.dma_start(parts[u][:, k, :], tables[k][:, bass.ds(i * (J * D), J * D)]).then_inc(parts_in[u], 16)

            for i in range(2):
                load(i, i)

            def body(i, u, pair):
                if there(i + 2, I):
                    load(i + 2, u)
                if there(i - 2, I):
                    sp.wait_ge(norm.done, i - 1)
                    sp.dma_start(out[:, bass.ds((i - 2) * J, J), :], xn[:, bass.ds((i - 2) * J, J), :]).then_inc(stored, 16)

            chunk_loop(sp, I, body)
            sp.wait_ge(stored, 16 * I)

        @block.gpsimd
        def _(pool):
            def add_pairs(i, u, pair):
                pool.wait_ge(parts_in[u], (pair + 1) * (16 * TPC))
                need(pool, agg_done, i)
                pool.tensor_tensor(pairs[:, :, :], parts[u][:, 0:2, :], parts[u][:, 2:4, :], ALU.add).then_inc(pairs_done, 1)

            def aggregate(i, u):
                pool.wait_ge(pairs_done, i + 1)
                need(pool, product_done, GROUPS * (i - 1))
                pool.tensor_tensor(agg[u][:, :, :].rearrange("p j c -> p (j c)"), pairs[:, 0, :], pairs[:, 1, :], ALU.add).then_inc(agg_done, 1)

            def rest(i):
                x = xn[:, bass.ds(i * J, J), :]
                pool.wait_ge(first_done, i + 1)
                need(pool, second_done, i)
                pool.tensor_tensor(x_rest[:, :, :], x, x_parts[:, :, 0, :], ALU.subtract).then_inc(rest_done, 1)

            def third_part(i):
                pool.wait_ge(second_done, i + 1)
                pool.tensor_tensor(x_parts[:, :, 5, :], x_rest[:, :, :], x_parts[:, :, 3, :], ALU.subtract).then_inc(third_done, 1)

            def fold_early(i, u):
                pool.wait_ge(product_done, GROUPS * i + GROUPS // 2)
                need(pool, quarter_done, i)
                pool.tensor_tensor(early_half[:, :, :, :], product[u][:, 0:J // 2, 0:8, :], product[u][:, 0:J // 2, 8:16, :], ALU.add).then_inc(early_half_done, 1)
                pool.wait_ge(early_half_done, i + 1)
                need(pool, mixed_done, 2 * i)
                pool.tensor_tensor(quarter[:, :, :, :], early_half[:, :, 0:4, :], early_half[:, :, 4:8, :], ALU.add).then_inc(quarter_done, 1)

            def fold_late(i, u):
                pool.wait_ge(product_done, GROUPS * (i + 1))
                need(pool, mixed_done, 2 * i)
                pool.tensor_tensor(late_half[:, :, :, :], product[u][:, J // 2:J, 0:8, :], product[u][:, J // 2:J, 8:16, :], ALU.add).then_inc(late_half_done, 1)

            def prepare(i, u, pair):
                rest(i)
                add_pairs(i, u, pair)
                third_part(i)
                aggregate(i, u)

            prepare(0, 0, 0)

            def body(i, u, pair):
                if there(i - 1, I):
                    fold_late(i - 1, 1 - u)
                if there(i + 1, I):
                    prepare(i + 1, 1 - u, pair if u == 0 else pair + 1)
                if there(i, I):
                    fold_early(i, u)

            chunk_loop(pool, I, body)

        @block.scalar
        def _(act):
            def first_part(i):
                need(act, x_turned, i)
                need(act, third_done, i)
                act.activation(x_parts[:, :, 0:3, :], xn[:, bass.ds(i * J, J), :].unsqueeze(2).broadcast_to([NP, J, 3, D]), ACT.Copy).then_inc(first_done, 1)

            def second_part(i):
                act.wait_ge(rest_done, i + 1)
                act.activation(x_parts[:, :, 3:5, :], x_rest[:, :, :].unsqueeze(2).broadcast_to([NP, J, 2, D]), ACT.Copy).then_inc(second_done, 1)

            def copy_turned(i, u):
                act.wait_ge(x_turned, i + 1)
                need(act, group_done, GROUPS * (i - 1))
                act.activation(xt[u][:, :].rearrange("c (j p) -> c j p", j=J)[:, :, 0:NP],
                               xt_ps[:, :].rearrange("c (j p) -> c j p", j=J)[:, :, 0:NP], ACT.Copy).then_inc(xt_ready, 1)

            first_part(0)
            second_part(0)
            copy_turned(0, 0)

            def body(i, u, pair):
                if there(i + 1, I):
                    first_part(i + 1)
                if there(i - 2, I):
                    act.preload_act_table_set("natural_log_exp_and_others")
                    norm.square_up(act, i - 2)
                    norm.deviation(act, i - 2, b.eps_col[0:NP, :])
                if there(i + 1, I):
                    second_part(i + 1)
                if there(i - 1, I):
                    act.wait_ge(mixed_done, 2 * i)
                    need(act, act_turned, i - 1)
                    act.activation(act_u[:, :], mixed[:, :], ACT.Silu, scale=1.0 / D).then_inc(act_done, 1)
                if there(i - 1, I):
                    act.wait_ge(act_turned, i)
                    need(act, v_done, i - 1)
                    act.activation(act_ut[:, :, :], t_ps[:, 0:2 * NP].rearrange("p (k n) -> p k n", k=2), ACT.Copy,
                                   scale=float(D) ** -0.5).then_inc(act_t_ready, 1)
                if there(i + 1, I):
                    copy_turned(i + 1, 1 - u)

            chunk_loop(act, I, body)

        @block.tensor
        def _(pe):
            def turn(nodes):
                for j in nodes:
                    mm = pe.transpose(xt_ps[:, j * P:j * P + NP], x_parts[:, j, :, :].rearrange("p n c -> p (n c)"), b.ident_b[0:NP, 0:NP])
                return mm

            def turn_first(i):
                pe.wait_ge(third_done, i + 1)
                pe.wait_ge(second_done, i + 1)
                need(pe, xt_ready, i)
                waits_apart(pe)
                turn(range(0, J // 2))

            def turn_others():
                turn(range(J // 2, J)).then_inc(x_turned, 1)

            turn_first(0)
            turn_others()

            def body(i, u, pair):
                if there(i, I):
                    pe.wait_ge(xt_ready, i + 1)
                    for g in range(GROUPS):
                        need(pe, product_done, GROUPS * i + g - BANKS + 1)
                        for j in (2 * g, 2 * g + 1):
                            mm = pe.matmul(y_ps[g % BANKS][0:NP, (j % 2) * CH:(j % 2 + 1) * CH], xt[u][:, j * P:j * P + NP], b.w_split[0:ROWS, 2, :],
                                           start=True, stop=True)
                        mm.then_inc(group_done, 1)
                if there(i + 1, I):
                    turn_first(i + 1)
                if there(i - 1, I):
                    pe.wait_ge(act_done, i)
                    need(pe, act_t_ready, i - 1)
                    waits_apart(pe)
                    for k in range(2):
                        mm = pe.transpose(t_ps[:, k * NP:(k + 1) * NP], act_u[:, k * P:(k + 1) * P], b.ident[0:NP, 0:NP])
                    mm.then_inc(act_turned, 1)
                if there(i + 1, I):
                    turn_others()
                if there(i - 1, I):
                    pe.wait_ge(act_t_ready, i)
                    need(pe, y_done, i - 1)
                    for k in range(2):
                        mm = pe.matmul(v_ps[0:NP, k * P:(k + 1) * P], act_ut[:, k, :], b.bd_upd[:, :], start=True, stop=True)
                    mm.then_inc(v_done, 1)

            chunk_loop(pe, I, body)

        @block.vector
        def _(dve):
            def products(i, u, groups):
                dve.wait_ge(agg_done, i + 1)
                need(dve, early_half_done, i - 1)
                need(dve, late_half_done, i - 1)
                for g in groups:
                    dve.wait_ge(group_done, GROUPS * i + g + 1)
                    dve.tensor_tensor(product[u][:, 2 * g:2 * g + 2, :, :], y_ps[g % BANKS][0:NP, :].rearrange("p (j h k) -> p j h k", j=2, h=D),
                                      agg[u][:, 2 * g:2 * g + 2, :].unsqueeze(3).broadcast_to([NP, 2, D, D]), ALU.mult).then_inc(product_done, 1)

            def mix(i):
                need(dve, act_done, i)
                for done, part, nodes in ((quarter_done, quarter[:, :, :, :], slice(0, J * D // 2)),
                                          (late_half_done, late_half[:, :, :, :], slice(J * D // 2, J * D))):
                    dve.wait_ge(done, i + 1)
                    dve.tensor_reduce(mixed[:, nodes].rearrange("p (j k) -> p j k", k=D), part.rearrange("p j h k -> p j k h"),
                                      AX.X, ALU.add).then_inc(mixed_done, 1)

            def update(i):
                dve.wait_ge(v_done, i + 1)
                need(dve, norm.centred_done, i)
                dve.scalar_tensor_tensor(y[:, :, :], xn[:, bass.ds(i * J, J), :], 2.0, v_ps[0:NP, 0:J * D].rearrange("p (j c) -> p j c", c=D),
                                         ALU.mult, ALU.add).then_inc(y_done, 1)
                dve.wait_ge(y_done, i + 1)
                norm.centre(dve, i, y[:, :, :])

            def body(i, u, pair):
                if there(i - 2, I):
                    update(i - 2)
                if there(i, I):
                    products(i, u, range(0, 2))
                if there(i - 2, I):
                    norm.variance(dve, i - 2)
                if there(i, I):
                    products(i, u, range(2, 4))
                if there(i - 1, I):
                    mix(i - 1)
                if there(i, I):
                    products(i, u, range(4, GROUPS))
                if there(i - 2, I):
                    norm.scale(dve, i - 2, xn[:, bass.ds((i - 2) * J, J), :])

            chunk_loop(dve, I, body)


def graph_mlp(nc, sems, sh, b, name, seg_table, x_in, eps1, wa, ba, wb, bb, final):
    def sem(what):
        return sems.enter(name + what)

    J = 40
    I = sh.NJ // J
    NP = sh.NP
    B = J * D // P
    W0 = 4 * NP
    with ExitStack() as scratch:
        def sb(what, shape):
            return scratch.enter_context(nc.sbuf_tensor(name + what, shape, F32))

        def ps(what):
            return scratch.enter_context(nc.psum_tensor(name + what, [P, 1024], F32))

        seg = [sb(f"seg{i}", [NP, J, D]) for i in range(2)]
        scaled, h_in = sb("scaled", [NP, J, D]), [sb(f"h_in{i}", [NP, J, D]) for i in range(2)]
        ht, hidden_t = [sb(f"ht{i}", [P, B * NP]) for i in range(2)], sb("hidden_t", [P, B * NP])
        y = sb("y", [NP, J, D])
        t_ps, hid_ps, o_ps = ps("t_ps"), ps("hid_ps"), ps("o_ps")
        seg_in = [sem(f"seg_in{i}") for i in range(2)]
        h_done, h_turned, ht_ready, hid_done, hidden_ready, o_done = (
            sem("h_done"), sem("h_turned"), sem("ht_ready"), sem("hid_done"), sem("hidden_ready"), sem("o_done"))
        scaled_done = sem("scaled_done")
        biased, done, stored = sem("biased"), sem("done"), [sem(f"stored{i}") for i in range(2)]
        if final:
            norm = Norm(nc, sems, scratch, name + "norm_", NP, J)
            top, den, log_den, shift = sb("top", [NP, J]), sb("den", [NP, J]), sb("log_den", [NP, J]), sb("shift", [NP, J])
            less, prob, z = sb("less", [NP, J, D]), sb("prob", [NP, J, D]), sb("z", [NP, J, D])
            with_x = [sb(f"with_x{i}", [NP, J, D]) for i in range(2)]
            result = [sb(f"result{i}", [NP, J, D]) for i in range(2)]
            top_done, less_done, prob_done, den_done, log_den_done, shift_done, with_x_done, z_done = (
                sem("top_done"), sem("less_done"), sem("prob_done"), sem("den_done"), sem("log_den_done"),
                sem("shift_done"), sem("with_x_done"), sem("z_done"))
            finished = norm.done
        else:
            finished = done
        table = seg_table.rearrange("(p j) c -> p j c", p=NP)
        out = (b.out if final else b.t_h).rearrange("(p j) c -> p j c", p=NP)
        nodes = x_in[0:NP, :].rearrange("p (j c) -> p j c", c=D)
        xn = b.xn[0:NP, :].rearrange("p (j c) -> p j c", c=D)
        hn = b.hn[0:NP, :].rearrange("p (j c) -> p j c", c=D)
        block = scratch.enter_context(nc.Block())

        def halves(t, rows=P):
            return ((t[0:rows, 0:W0], slice(0, W0)), (t[0:rows, 512:512 + NP], slice(W0, B * NP)))

        def at(k):
            return k * NP if k < 4 else 512

        @block.sync
        def _(sp):
            def load(i, u):
                need(sp, h_done, i - 1)
                sp.dma_start(seg[u][:, :, :], table[:, bass.ds(i * J, J), :]).then_inc(seg_in[u], 16)

            for i in range(2):
                load(i, i)

            def body(i, u, pair):
                if there(i + 2, I):
                    load(i + 2, u)
                if there(i - 2, I):
                    sp.wait_ge(finished, i - 1)
                    sp.dma_start(out[:, bass.ds((i - 2) * J, J), :],
                                 result[u][:, :, :] if final else hn[:, bass.ds((i - 2) * J, J), :]).then_inc(stored[u], 16)

            chunk_loop(sp, I, body)
            for u in range(2):
                sp.wait_ge(stored[u], 16 * (I // 2))

        @block.vector
        def _(dve):
            def add_bias(i):
                dve.wait_ge(o_done, i + 1)
                if final:
                    need(dve, less_done, i)
                    need(dve, with_x_done, i)
                else:
                    need(dve, done, i)
                dve.tensor_tensor(y[:, :, :], o_ps[0:NP, 0:J * D].rearrange("p (j c) -> p j c", c=D),
                                  bb[0:NP, :].unsqueeze(1).broadcast_to([NP, J, D]), ALU.add).then_inc(biased, 1)
                dve.wait_ge(biased, i + 1)

            def relu(i):
                dve.tensor_scalar(hn[:, bass.ds(i * J, J), :], y[:, :, :], 0.0, None, ALU.max).then_inc(done, 1)

            def largest(i):
                dve.tensor_reduce(top[:, :], y[:, :, :], AX.X, ALU.max).then_inc(top_done, 1)

            def subtract_largest(i):
                dve.wait_ge(top_done, i + 1)
                need(dve, prob_done, i)
                dve.tensor_tensor(less[:, :, :], y[:, :, :], top[:, :].unsqueeze(2).broadcast_to([NP, J, D]), ALU.subtract).then_inc(less_done, 1)

            def denominator(i):
                dve.wait_ge(prob_done, i + 1)
                need(dve, log_den_done, i)
                dve.tensor_reduce(den[:, :], prob[:, :, :], AX.X, ALU.add).then_inc(den_done, 1)

            def residual(i, u):
                dve.wait_ge(log_den_done, i + 1)
                need(dve, z_done, i)
                dve.tensor_tensor(shift[:, :], top[:, :], log_den[:, :], ALU.add).then_inc(shift_done, 1)
                dve.wait_ge(shift_done, i + 1)
                dve.wait_ge(with_x_done, i + 1)
                need(dve, norm.centred_done, i)
                dve.tensor_tensor(z[:, :, :], with_x[u][:, :, :], shift[:, :].unsqueeze(2).broadcast_to([NP, J, D]), ALU.subtract).then_inc(z_done, 1)
                dve.wait_ge(z_done, i + 1)
                norm.centre(dve, i, z[:, :, :])

            def body(i, u, pair):
                if not final:
                    if there(i - 1, I):
                        add_bias(i - 1)
                        relu(i - 1)
                    return
                if there(i - 2, I):
                    denominator(i - 2)
                if there(i - 1, I):
                    add_bias(i - 1)
                if there(i - 2, I):
                    residual(i - 2, u)
                if there(i - 1, I):
                    largest(i - 1)
                if there(i - 2, I):
                    norm.variance(dve, i - 2)
                if there(i - 1, I):
                    subtract_largest(i - 1)
                if there(i - 2, I):
                    need(dve, stored[u], (pair - 1) * 16)
                    norm.scale(dve, i - 2, result[u][:, :, :])

            chunk_loop(dve, I, body)

        @block.gpsimd
        def _(pool):
            def start(i, u, pair):
                need(pool, h_done, i)
                pool.tensor_tensor(scaled[:, :, :], nodes[:, bass.ds(i * J, J), :],
                                   eps1[0:NP, 0:1].unsqueeze(2).broadcast_to([NP, J, D]), ALU.mult).then_inc(scaled_done, 1)
                pool.wait_ge(scaled_done, i + 1)
                pool.wait_ge(seg_in[u], (pair + 1) * 16)
                need(pool, h_turned, i - 1)
                pool.tensor_tensor(h_in[u][:, :, :], scaled[:, :, :], seg[u][:, :, :], ALU.add).then_inc(h_done, 1)

            start(0, 0, 0)

            def body(i, u, pair):
                if there(i + 1, I):
                    start(i + 1, 1 - u, pair if u == 0 else pair + 1)
                if final and there(i - 1, I):
                    pool.wait_ge(biased, i)
                    need(pool, z_done, i - 2)
                    pool.tensor_tensor(with_x[1 - u][:, :, :], y[:, :, :], xn[:, bass.ds((i - 1) * J, J), :], ALU.add).then_inc(with_x_done, 1)

            chunk_loop(pool, I, body)

        @block.tensor
        def _(pe):
            def turn(i, u):
                pe.wait_ge(h_done, i + 1)
                need(pe, ht_ready, 2 * i)
                waits_apart(pe)
                for k in range(B):
                    mm = pe.transpose(t_ps[:, at(k):at(k) + NP], h_in[u][:, 8 * k:8 * k + 8, :].rearrange("p j c -> p (j c)"), b.ident[0:NP, 0:NP])
                mm.then_inc(h_turned, 1)

            turn(0, 0)

            def body(i, u, pair):
                if not there(i, I):
                    return
                need(pe, hidden_ready, 2 * i)
                for k, (part, cols) in enumerate(halves(hid_ps)):
                    pe.wait_ge(ht_ready, 2 * i + k + 1)
                    mm = pe.matmul(part, wa[:, :], ht[u][:, cols], start=True, stop=True)
                    mm.then_inc(hid_done, 1)
                if there(i + 1, I):
                    turn(i + 1, 1 - u)
                pe.wait_ge(hidden_ready, 2 * (i + 1))
                need(pe, biased, i)
                for k in range(B):
                    mm = pe.matmul(o_ps[0:NP, k * P:(k + 1) * P], hidden_t[:, k * NP:(k + 1) * NP], wb[:, :], start=True, stop=True)
                mm.then_inc(o_done, 1)

            chunk_loop(pe, I, body)

        @block.scalar
        def _(act):
            def copy_turned(i, u):
                act.wait_ge(h_turned, i + 1)
                need(act, hid_done, 2 * (i - 1))
                for part, cols in halves(t_ps):
                    act.activation(ht[u][:, cols], part, ACT.Copy).then_inc(ht_ready, 1)

            act.preload_act_table_set("natural_log_exp_and_others")
            copy_turned(0, 0)

            def body(i, u, pair):
                if final and there(i - 2, I):
                    act.wait_ge(den_done, i - 1)
                    need(act, shift_done, i - 2)
                    act.activation(log_den[:, :], den[:, :], ACT.Ln).then_inc(log_den_done, 1)
                if final and there(i - 2, I):
                    norm.square_up(act, i - 2)
                if there(i, I):
                    need(act, o_done, i)
                    for k, (part, cols) in enumerate(halves(hid_ps)):
                        act.wait_ge(hid_done, 2 * i + k + 1)
                        act.activation(hidden_t[:, cols], part, ACT.Relu, bias=ba[:, 0:1]).then_inc(hidden_ready, 1)
                if there(i + 1, I):
                    copy_turned(i + 1, 1 - u)
                if final and there(i - 2, I):
                    norm.deviation(act, i - 2, b.eps_col[0:NP, :])
                if final and there(i - 1, I):
                    act.wait_ge(less_done, i)
                    need(act, den_done, i - 1)
                    act.activation(prob[:, :, :], less[:, :, :], ACT.Exp).then_inc(prob_done, 1)

            chunk_loop(act, I, body)


class Buffers:
    pass


def build(nc, io, out):
    N, E = io["x"].shape[0], io["src"].shape[0]
    sh = Shapes(N, E)
    b = Buffers()
    with ExitStack() as ctx:
        def sb(name, shape, dt=F32):
            return ctx.enter_context(nc.sbuf_tensor(name, shape, dt))

        b.out = out
        b.t_first = nc.dram_tensor("t_first", [N, 2 * D], F32, kind="Internal").ap()
        b.t_x = nc.dram_tensor("t_x", [N, D], F32, kind="Internal").ap()
        b.t_h = nc.dram_tensor("t_h", [N, D], F32, kind="Internal").ap()
        b.t_adds = [nc.dram_tensor(f"t_add{k}", [N + 1 + P, D], F32, kind="Internal").ap() for k in range(TPC)]
        b.t_seg1 = nc.dram_tensor("t_seg1", [N, D], F32, kind="Internal").ap()
        b.t_seg2 = nc.dram_tensor("t_seg2", [N, D], F32, kind="Internal").ap()

        b.ident, b.lower, b.sel = sb("ident", [P, P]), sb("lower", [P, P]), sb("sel", [P, D])
        b.ident_b = sb("ident_b", [P, P], BF16)
        b.eps_col, b.dummy, b.dummy_i = sb("eps_col", [P, 1]), sb("dummy_row", [P, 1]), sb("dummy_row_i", [P, 1], I32)
        b.w_split = sb("w_split", [P, 3, CH], BF16)
        b.w_tp = sb("w_tp", [P, D])
        b.bd_lin, b.bd_upd, b.bd1a, b.bd1b, b.bd2a, b.bd2b = (sb(w, [P, P]) for w in ("bd_lin", "bd_upd", "bd1a", "bd1b", "bd2a", "bd2b"))
        b.b1a, b.b2a, b.b1b, b.b2b = sb("b1a", [P, 1]), sb("b2a", [P, 1]), sb("b1b", [P, D]), sb("b2b", [P, D])
        b.eps1, b.eps2 = sb("eps1", [P, 1]), sb("eps2", [P, 1])
        cols = sh.tiles + 2 * TPC
        b.gsrc, b.gdst, b.scat = (sb(w, [P, cols], I32) for w in ("gsrc", "gdst", "scat"))
        b.start, b.srcf = sb("start", [P, cols]), sb("srcf", [P, cols])
        with ExitStack() as outer:
            b.ea8 = outer.enter_context(nc.sbuf_tensor("ea8", [P, sh.tiles, DE], F32))
            with ExitStack() as first:
                def early(name, shape, dt=F32):
                    return first.enter_context(nc.sbuf_tensor(name, shape, dt))

                b.zw = 800
                b.zeros = early("zeros", [P, b.zw])
                b.edges = early("edges", [P, sh.tiles, P], BF16)
                b.w_start, b.w_attr, b.w_h = early("w_start", [P, P], BF16), early("w_attr", [P, D + 1], BF16), early("w_h", [3 * D, CH], BF16)
                b.e2 = [early(f"e2_{i}", [P, 2, CE + 1]) for i in range(2)]
                with Semaphores(nc) as sems:
                    constants_and_indices(nc, sems, sh, b, io)
                with Semaphores(nc) as sems:
                    attention_layer(nc, sems, sh, b, io)
            b.xn = outer.enter_context(nc.sbuf_tensor("xn", [P, sh.NJ * D], F32))
            with Semaphores(nc) as sems:
                first_norms(nc, sems, sh, b, io)
            with Semaphores(nc) as sems:
                message_layer(nc, sems, sh, b, io)
            with Semaphores(nc) as sems:
                update_nodes(nc, sems, sh, b, io)
            b.hn = outer.enter_context(nc.sbuf_tensor("hn", [P, sh.NJ * D], F32))
            with Semaphores(nc) as sems:
                neighbour_sums(nc, sems, sh, b, "s1_", b.t_x, b.t_seg1)
            with Semaphores(nc) as sems:
                graph_mlp(nc, sems, sh, b, "g1_", b.t_seg1, b.xn, b.eps1, b.bd1a, b.b1a, b.bd1b, b.b1b, False)
            with Semaphores(nc) as sems:
                neighbour_sums(nc, sems, sh, b, "s2_", b.t_h, b.t_seg2)
            with Semaphores(nc) as sems:
                graph_mlp(nc, sems, sh, b, "g2_", b.t_seg2, b.hn, b.eps2, b.bd2a, b.b2a, b.bd2b, b.b2b, True)


def kernel(**inputs):
    import numpy as np
    import concourse.bacc as bacc
    from concourse.bass_utils import run_bass_kernel_spmd

    nc = bacc.Bacc("TRN2", target_bir_lowering=False, num_devices=1)
    arrays, io = {}, {}
    for name in INPUTS:
        a = np.ascontiguousarray(inputs[name])
        if a.ndim == 0:
            a = a.reshape(1)
        arrays[f"in_{name}"] = a
        io[name] = nc.dram_tensor(f"in_{name}", a.shape, mybir.dt.from_np(a.dtype), kind="ExternalInput").ap()
    out = nc.dram_tensor("out", list(inputs["x"].shape), F32, kind="ExternalOutput").ap()
    build(nc, io, out)
    r = run_bass_kernel_spmd(nc, [arrays], core_ids=[0])
    return r.results[0]["out"]
```
